# Optimizing a Trainium2 kernel written in Bass

```python
import numpy as np
import jax
import jax.numpy as jnp

def _softmax(x, axis=-1):
    return jax.nn.softmax(x, axis=axis)

def _gelu(x):
    return jax.nn.gelu(x, approximate=True)

def _silu(x):
    return jax.nn.silu(x)

def _sigmoid(x):
    return jax.nn.sigmoid(x)

def _layernorm(x, axis=-1, eps=1e-05):
    m = jnp.mean(x, axis=axis, keepdims=True)
    v = jnp.var(x, axis=axis, keepdims=True)
    return (x - m) / jnp.sqrt(v + eps)

def _scatter_add(tgt, idx, src, axis=0):
    return tgt.at[idx].add(src)

def _segment_sum(src, seg, n):
    return jax.ops.segment_sum(src, seg, n)
kernel_name = 'mk_gnn_preln_d4_gnn_r64_9fd760'

def setup_inputs(seed: int=0):
    np.random.seed(seed)
    _w = jnp.asarray

    def _rec_inputs():
        import jax
        import jax.numpy as jnp
        _gk = jax.random.key(seed)
        x = -6.415e-05 + 1 * jax.random.normal(jax.random.fold_in(_gk, 1), (10000, 512), jnp.float32)
        src = jax.random.randint(jax.random.fold_in(_gk, 2), (5000,), 0, 10000, jnp.int32)
        dst = jax.random.randint(jax.random.fold_in(_gk, 3), (5000,), 0, 10000, jnp.int32)
        _o = jnp.argsort(dst, stable=True)
        src = src[_o]
        dst = dst[_o]
        edge_attr_64 = 0.000279952 + 1.00013 * jax.random.normal(jax.random.fold_in(_gk, 12), (5000, 64), jnp.float32)
        return (x, src, dst, edge_attr_64)
    x, src, dst, edge_attr_64 = _rec_inputs()

    def _L0_gnn_setup():
        import jax, jax.numpy as jnp
        import numpy as np
        N_NODES = 20000
        N_EDGES = 5000
        HIDDEN = 512
        EDGE_DIM = 64
        LN_EPS = 1e-05

        def mish(x):
            return x * jnp.tanh(jax.nn.softplus(x))
        key = jax.random.key(seed)
        ks = jax.random.split(key, 8)
        s = lambda fan_in: 1.0 / np.sqrt(fan_in)
        return {'x': jax.random.normal(ks[0], (N_NODES, HIDDEN), dtype=jnp.float32), 'edge_index': jax.random.randint(ks[1], (2, N_EDGES), 0, N_NODES, dtype=jnp.int64), 'edge_attr': jax.random.normal(ks[2], (N_EDGES, EDGE_DIM), dtype=jnp.float32), 'W1': jax.random.normal(ks[3], (2 * HIDDEN + EDGE_DIM, HIDDEN), dtype=jnp.float32) * s(2 * HIDDEN + EDGE_DIM), 'b1': jnp.zeros((HIDDEN,), dtype=jnp.float32), 'W2': jax.random.normal(ks[4], (HIDDEN, HIDDEN), dtype=jnp.float32) * s(HIDDEN), 'b2': jnp.zeros((HIDDEN,), dtype=jnp.float32), 'W3': jax.random.normal(ks[5], (2 * HIDDEN, HIDDEN), dtype=jnp.float32) * s(2 * HIDDEN), 'b3': jnp.zeros((HIDDEN,), dtype=jnp.float32), 'W4': jax.random.normal(ks[6], (HIDDEN, HIDDEN), dtype=jnp.float32) * s(HIDDEN), 'b4': jnp.zeros((HIDDEN,), dtype=jnp.float32), 'gamma': jnp.ones((HIDDEN,), dtype=jnp.float32), 'beta': jnp.zeros((HIDDEN,), dtype=jnp.float32)}
    _L0_gnn_all = _L0_gnn_setup()
    _L0_gnn_in = {k: v for k, v in _L0_gnn_all.items() if k in ('W1', 'b1', 'W2', 'b2', 'W3', 'b3', 'W4', 'b4', 'gamma', 'beta')}
    del _L0_gnn_all

    def _L1_gnn_setup():
        import jax, jax.numpy as jnp
        import numpy as np
        BN_EPS = 1e-05
        N_NODES, N_EDGES, D, N_LAYERS = (50000, 6250, 512, 3)
        key = jax.random.key(seed)
        k_x, k_e, k_w = jax.random.split(key, 3)
        x = jax.random.normal(k_x, (N_NODES, D), dtype=jnp.float32)
        edge_index = jax.random.randint(k_e, (2, N_EDGES), 0, N_NODES, dtype=jnp.int64)
        W = jax.random.normal(k_w, (N_LAYERS, D, D), dtype=jnp.float32) * (1.0 / np.sqrt(D))
        b = jnp.zeros((N_LAYERS, D), dtype=jnp.float32)
        gamma = jnp.ones((N_LAYERS, D), dtype=jnp.float32)
        beta = jnp.zeros((N_LAYERS, D), dtype=jnp.float32)
        return {'x': x, 'edge_index': edge_index, 'W': W, 'b': b, 'gamma': gamma, 'beta': beta}
    _L1_gnn_all = _L1_gnn_setup()
    _L1_gnn_in = {k: v for k, v in _L1_gnn_all.items() if k in ('W', 'b', 'gamma', 'beta')}
    del _L1_gnn_all

    def _L2_gnn_setup():
        import jax, jax.numpy as jnp
        import numpy as np
        N = 10000
        E = 2500
        IN = 512
        HID = 512
        OUT = 512

        def _gcn_norm(edge_index, n):
            loops = jnp.arange(n, dtype=edge_index.dtype)
            row = jnp.concatenate([edge_index[0], loops])
            col = jnp.concatenate([edge_index[1], loops])
            deg = jax.ops.segment_sum(jnp.ones_like(col, jnp.float32), col, num_segments=n)
            dis = jnp.where(deg > 0, jax.lax.rsqrt(jnp.maximum(deg, 1.0)), 0.0)
            norm = dis[row] * dis[col]
            return (row, col, norm)

        def _gcn_layer(x, row, col, norm, W, b, n):
            h = x @ W
            msg = h[row] * norm[:, None]
            out = jax.ops.segment_sum(msg, col, num_segments=n)
            return out + b
        key = jax.random.key(seed)
        ks = jax.random.split(key, 8)
        x = jax.random.normal(ks[0], (N, IN), dtype=jnp.float32)
        edge_index = jax.random.randint(ks[1], (2, E), 0, N, dtype=jnp.int64)

        def w(k, fi, fo):
            return jax.random.normal(k, (fi, fo), dtype=jnp.float32) * (1.0 / np.sqrt(fi)).astype(np.float32)
        return {'x': x, 'edge_index': edge_index, 'W1': w(ks[2], IN, HID), 'b1': jnp.zeros((HID,), jnp.float32), 'W2': w(ks[3], HID, HID), 'b2': jnp.zeros((HID,), jnp.float32), 'W3': w(ks[4], HID, OUT), 'b3': jnp.zeros((OUT,), jnp.float32)}
    _L2_gnn_all = _L2_gnn_setup()
    _L2_gnn_in = {k: v for k, v in _L2_gnn_all.items() if k in ('W1', 'b1', 'W2', 'b2', 'W3', 'b3')}
    del _L2_gnn_all

    def _L3_gnn_setup():
        import jax, jax.numpy as jnp
        import numpy as np
        N_NODES = 10000
        N_EDGES = 2500
        D_IN = 512
        D_OUT = 512
        key = jax.random.key(seed)
        k1, k2, k3, k4, k5 = jax.random.split(key, 5)
        feature = jax.random.normal(k1, (N_NODES, D_IN), dtype=jnp.float32)
        src = jax.random.randint(k2, (N_EDGES,), 0, N_NODES, dtype=jnp.int64)
        dst = jax.random.randint(k3, (N_EDGES,), 0, N_NODES, dtype=jnp.int64)
        W = jax.random.normal(k4, (2 * D_IN, D_OUT), dtype=jnp.float32) * (1.0 / np.sqrt(2 * D_IN))
        b = jax.random.normal(k5, (D_OUT,), dtype=jnp.float32) * 0.01
        return {'feature': feature, 'src': src, 'dst': dst, 'W': W, 'b': b}
    _L3_gnn_all = _L3_gnn_setup()
    _L3_gnn_in = {k: v for k, v in _L3_gnn_all.items() if k in ('W', 'b')}
    del _L3_gnn_all
    return {'x': x, 'src': src, 'dst': dst, 'edge_attr_64': edge_attr_64, 'L0_gnn_W1': _L0_gnn_in['W1'], 'L0_gnn_b1': _L0_gnn_in['b1'], 'L0_gnn_W2': _L0_gnn_in['W2'], 'L0_gnn_b2': _L0_gnn_in['b2'], 'L0_gnn_W3': _L0_gnn_in['W3'], 'L0_gnn_b3': _L0_gnn_in['b3'], 'L0_gnn_W4': _L0_gnn_in['W4'], 'L0_gnn_b4': _L0_gnn_in['b4'], 'L0_gnn_gamma': _L0_gnn_in['gamma'], 'L0_gnn_beta': _L0_gnn_in['beta'], 'L1_gnn_W': _L1_gnn_in['W'], 'L1_gnn_b': _L1_gnn_in['b'], 'L1_gnn_gamma': _L1_gnn_in['gamma'], 'L1_gnn_beta': _L1_gnn_in['beta'], 'L2_gnn_W1': _L2_gnn_in['W1'], 'L2_gnn_b1': _L2_gnn_in['b1'], 'L2_gnn_W2': _L2_gnn_in['W2'], 'L2_gnn_b2': _L2_gnn_in['b2'], 'L2_gnn_W3': _L2_gnn_in['W3'], 'L2_gnn_b3': _L2_gnn_in['b3'], 'L3_gnn_W': _L3_gnn_in['W'], 'L3_gnn_b': _L3_gnn_in['b']}

def reference(x, src, dst, edge_attr_64, L0_gnn_W1, L0_gnn_b1, L0_gnn_W2, L0_gnn_b2, L0_gnn_W3, L0_gnn_b3, L0_gnn_W4, L0_gnn_b4, L0_gnn_gamma, L0_gnn_beta, L1_gnn_W, L1_gnn_b, L1_gnn_gamma, L1_gnn_beta, L2_gnn_W1, L2_gnn_b1, L2_gnn_W2, L2_gnn_b2, L2_gnn_W3, L2_gnn_b3, L3_gnn_W, L3_gnn_b):
    import jax
    import jax.numpy as jnp

    def _L0_gnn_ref(x, edge_index, edge_attr, W1, b1, W2, b2, W3, b3, W4, b4, gamma, beta):
        import jax, jax.numpy as jnp
        import numpy as np
        N_NODES = 20000
        N_EDGES = 5000
        HIDDEN = 512
        EDGE_DIM = 64
        LN_EPS = 1e-05

        def mish(x):
            return x * jnp.tanh(jax.nn.softplus(x))
        src, dst = (edge_index[0], edge_index[1])
        edge_feat = jnp.concatenate([x[src], x[dst], edge_attr], axis=-1)
        h = mish(edge_feat @ W1 + b1)
        messages = mish(h @ W2 + b2)
        agg = jax.ops.segment_sum(messages, dst, num_segments=x.shape[0])
        u = mish(jnp.concatenate([x, agg], axis=-1) @ W3 + b3)
        out = u @ W4 + b4
        y = x + out
        mu = jnp.mean(y, axis=-1, keepdims=True)
        var = jnp.mean(jnp.square(y - mu), axis=-1, keepdims=True)
        return (y - mu) * jax.lax.rsqrt(var + LN_EPS) * gamma + beta

    def _L1_gnn_ref(x, W, b, gamma, beta, edge_index):
        import jax, jax.numpy as jnp
        import numpy as np
        BN_EPS = 1e-05
        N_NODES, N_EDGES, D, N_LAYERS = (50000, 6250, 512, 3)
        N = x.shape[0]
        loops = jnp.arange(N, dtype=edge_index.dtype)
        src = jnp.concatenate([edge_index[0], loops])
        dst = jnp.concatenate([edge_index[1], loops])
        deg = jax.ops.segment_sum(jnp.ones(src.shape, jnp.float32), dst, num_segments=N)
        dinv = jax.lax.rsqrt(deg)
        norm = dinv[src] * dinv[dst]
        for l in range(W.shape[0]):
            h = x @ W[l].T
            agg = jax.ops.segment_sum(h[src] * norm[:, None], dst, num_segments=N) + b[l]
            mean = jnp.mean(agg, axis=0)
            var = jnp.mean((agg - mean) ** 2, axis=0)
            xn = (agg - mean) * jax.lax.rsqrt(var + BN_EPS)
            x = jax.nn.relu(gamma[l] * xn + beta[l])
        return x

    def _L2_gnn_ref(x, edge_index, W1, b1, W2, b2, W3, b3):
        import jax, jax.numpy as jnp
        import numpy as np
        N = 10000
        E = 2500
        IN = 512
        HID = 512
        OUT = 512

        def _gcn_norm(edge_index, n):
            loops = jnp.arange(n, dtype=edge_index.dtype)
            row = jnp.concatenate([edge_index[0], loops])
            col = jnp.concatenate([edge_index[1], loops])
            deg = jax.ops.segment_sum(jnp.ones_like(col, jnp.float32), col, num_segments=n)
            dis = jnp.where(deg > 0, jax.lax.rsqrt(jnp.maximum(deg, 1.0)), 0.0)
            norm = dis[row] * dis[col]
            return (row, col, norm)

        def _gcn_layer(x, row, col, norm, W, b, n):
            h = x @ W
            msg = h[row] * norm[:, None]
            out = jax.ops.segment_sum(msg, col, num_segments=n)
            return out + b
        n = x.shape[0]
        row, col, norm = _gcn_norm(edge_index, n)
        h = _gcn_layer(x, row, col, norm, W1, b1, n)
        h = jax.nn.relu(h)
        h = _gcn_layer(h, row, col, norm, W2, b2, n)
        h = jax.nn.relu(h)
        h = _gcn_layer(h, row, col, norm, W3, b3, n)
        return h

    def _L3_gnn_ref(feature, src, dst, W, b):
        import jax, jax.numpy as jnp
        import numpy as np
        N_NODES = 10000
        N_EDGES = 2500
        D_IN = 512
        D_OUT = 512
        n = feature.shape[0]
        neigh = jax.ops.segment_sum(feature[src], dst, num_segments=n)
        degs = jax.ops.segment_sum(jnp.ones_like(dst, dtype=feature.dtype), dst, num_segments=n)
        hk_neigh = neigh / jnp.maximum(degs, 1.0)[:, None]
        hk = jnp.concatenate([feature, hk_neigh], axis=-1) @ W + b
        return jax.nn.relu(hk)
    edge_index = jnp.stack([src, dst])
    h = jnp.maximum(_layernorm(x, axis=-1), 0.0)
    x = x + _L0_gnn_ref(h, edge_index, edge_attr_64, L0_gnn_W1, L0_gnn_b1, L0_gnn_W2, L0_gnn_b2, L0_gnn_W3, L0_gnn_b3, L0_gnn_W4, L0_gnn_b4, L0_gnn_gamma, L0_gnn_beta)
    h = jnp.maximum(_layernorm(x, axis=-1), 0.0)
    x = x + _L1_gnn_ref(h, L1_gnn_W, L1_gnn_b, L1_gnn_gamma, L1_gnn_beta, edge_index)
    h = jnp.maximum(_layernorm(x, axis=-1), 0.0)
    x = x + _L2_gnn_ref(h, edge_index, L2_gnn_W1, L2_gnn_b1, L2_gnn_W2, L2_gnn_b2, L2_gnn_W3, L2_gnn_b3)
    h = jnp.maximum(_layernorm(x, axis=-1), 0.0)
    x = x + _L3_gnn_ref(h, src, dst, L3_gnn_W, L3_gnn_b)
    return x

_drawn_inputs = setup_inputs


def setup_inputs(seed=0):
    import zlib

    import numpy as np

    out = dict(_drawn_inputs(seed))
    spreads = {'L0_gnn_b1': (0.0, 0.666),
     'L0_gnn_b2': (0.0, 0.451),
     'L0_gnn_b3': (0.0, 0.1),
     'L0_gnn_b4': (0.0, 0.1),
     'L0_gnn_gamma': (1.0, 0.2),
     'L0_gnn_beta': (0.0, 0.1),
     'L1_gnn_b': (0.0, 0.8),
     'L1_gnn_gamma': (1.0, 0.2),
     'L1_gnn_beta': (0.0, 0.1),
     'L2_gnn_b1': (0.0, 0.323),
     'L2_gnn_b2': (0.0, 0.1),
     'L2_gnn_b3': (0.0, 0.1)}
    factors = {'L3_gnn_b': 8.0}
    for name, (base, spread) in spreads.items():
        noise = np.random.default_rng([zlib.crc32(name.encode()), seed]).standard_normal(out[name].shape)
        drawn = base * np.exp(spread * noise) if base else spread * noise
        out[name] = jnp.asarray(drawn.astype(out[name].dtype))
    for name, factor in factors.items():
        out[name] = (out[name] * factor).astype(out[name].dtype)
    return out
```

```python
from contextlib import ExitStack

import numpy as np
import concourse.bass as bass
from concourse import mybir

ALU = mybir.AluOpType
ACT = mybir.ActivationFunctionType
F32 = mybir.dt.float32
F32R = mybir.dt.float32r
BF16 = mybir.dt.bfloat16
I32 = mybir.dt.int32

P = 128
U = 2
EPS = 1e-5
FAR = 1 << 20
EXP_MAX = 20.0


class Mark:

    def __init__(self, sem, base):
        self.sem, self.base = sem, base

    def at(self, n):
        return self.base + n


class Step:

    def __init__(self, group, lane, n, fixed):
        self.group, self.lane, self.n, self.fixed = group, lane, n, fixed

    def tile(self, ahead):
        return Step(self.group + (self.lane + ahead) // U, (self.lane + ahead) % U, self.n, self.fixed)

    @property
    def index(self):
        return self.group * U + self.lane

    @property
    def slot(self):
        return self.lane

    @property
    def exists(self):
        return not self.fixed or 0 <= self.index < self.n

    def has(self, before):
        return not self.fixed or self.index >= before


def steps(eng, n, body, ahead, behind):
    first = 2 * U
    last = (n - 2 * U) // U * U
    for t in range(-ahead, first):
        body(Step(t // U, t % U, n, True))
    with eng.Fori(first // U, last // U) as group:
        for lane in range(U):
            body(Step(group, lane, n, False))
    for t in range(last, n + behind):
        body(Step(t // U, t % U, n, True))


class Phase:

    def __init__(self, name, kind, n, before, out=None, tile=None, gathers=(), attr=False, agg=None, w=None,
                 wide=False, raw=None, turned=False, epi=None, bias=None, gamma=None, beta=None, side=(),
                 x_in=None, x_out=None, last=False):
        self.name, self.kind, self.n, self.before = name, kind, n, before
        self.m = {}
        self.out, self.x_in, self.x_out = out, x_in, x_out
        self.tile, self.gathers, self.attr, self.side = tile, gathers, attr, side
        self.agg = agg
        self.w, self.wide, self.raw, self.turned = w, wide, raw, turned
        self.epi, self.bias, self.gamma, self.beta, self.last = epi, bias, gamma, beta, last


def build(nc, a, out):
    x = a["x"]
    n_nodes, D = x.shape
    n_edges = a["src"].shape[0]
    DE = a["edge_attr_64"].shape[1]
    KC = D // P
    NT = -(-n_nodes // P)
    NT += NT % U
    ET = -(-n_edges // P)
    ET += ET % U
    NR, ER = NT * P, ET * P
    full_nt, rest_n = n_nodes // P, n_nodes % P
    EP = n_edges // ET
    assert EP * ET == n_edges and EP <= P

    def scratch(name, shape, dt=F32):
        return nc.dram_tensor(name, shape, dt, kind="Internal").ap()

    h0 = scratch("h0", [NR, D])
    ga = scratch("ga", [NR, D])
    gb = scratch("gb", [NR, D])
    msg = scratch("msg", [ER, D])
    e1 = scratch("e1", [ER, D])
    e2 = scratch("e2", [ER, D])
    u0 = scratch("u0", [NR, D])
    x1 = scratch("x1", [NR, D])
    x2 = scratch("x2", [NR, D])
    x3 = scratch("x3", [NR, D])
    spill = scratch("spill", [NR, D])
    slots_dram = scratch("slot_table", [NR, 4], I32)

    with ExitStack() as ctx:
        def sb(name, shape, dt=F32):
            return ctx.enter_context(nc.sbuf_tensor(name, shape, dt))

        def psum(name, shape, dt=F32):
            return ctx.enter_context(nc.psum_tensor(name, shape, dt))

        sems, stood = {}, {}

        def sem(name):
            if name not in sems:
                sems[name] = ctx.enter_context(nc.semaphore(name))
                stood[name] = 0
            return sems[name]

        w_hi = sb("w_hi", [P, KC, D], F32R)
        w_lo = sb("w_lo", [P, KC, D], F32R)
        zt_hi = sb("zt_hi", [P, U, KC * P], F32R)
        zt_lo = sb("zt_lo", [P, U, KC * P], F32R)
        share = ExitStack()
        w_raw_bn = share.enter_context(nc.sbuf_tensor("w_raw_bn", [P, KC, D], F32))
        share.close()
        tile_in = sb("tile_in", [P, U, D])
        gathered = sb("gathered", [P, U, D])
        select = sb("select", [P, U, P])
        ident = sb("ident", [P, P])
        ones = sb("ones", [P, P])
        iota_row = sb("iota_row", [P, P])
        src_col = sb("src_col", [P, ET], I32)
        dst_col = sb("dst_col", [P, ET], I32)
        dst_f = sb("dst_f", [P, ET])
        edge_id = sb("edge_id", [P, ET], I32)
        slot_src = sb("slot_src", [P, NT], I32)
        slot_edge = sb("slot_edge", [P, NT], I32)
        slot_node = sb("slot_node", [P, NT])
        spill_row = sb("spill_row", [P, NT], I32)
        dinv = sb("dinv", [P, NT])
        rdeg = sb("rdeg", [P, NT])
        minus_half = sb("minus_half", [P, NT])
        idx = sb("idx", [P, 2, U], I32)
        idx_spill = sb("idx_spill", [P, 2], I32)
        crowded = sb("crowded", [P, 1], I32)
        ln_st = sb("ln_st", [P, 2, U, 6])
        ln_mv = sb("ln_mv", [P, 2, U, 2])
        ln_sc = sb("ln_sc", [P, 2, U, 4])
        own = ExitStack()
        bn_sum = own.enter_context(nc.sbuf_tensor("bn_sum", [P, D], F32))
        bn_sq = own.enter_context(nc.sbuf_tensor("bn_sq", [P, D], F32))
        square = own.enter_context(nc.sbuf_tensor("square", [P, U, D], F32))
        kept = own.enter_context(nc.sbuf_tensor("kept", [P, NT, D], F32))
        own.close()

        w_raw = sb("w_raw", [P, 2 * KC + 1, D])
        w1_hi = sb("w1_hi", [P, 2 * KC + 1, D], F32R)
        w1_lo = sb("w1_lo", [P, 2 * KC + 1, D], F32R)
        e_hi = sb("e_hi", [P, U, (2 * KC + 1) * P], F32R)
        e_lo = sb("e_lo", [P, U, (2 * KC + 1) * P], F32R)
        attr = sb("attr", [P, U, P])
        v_buf = sb("v_buf", [P, U, D])
        c_buf = sb("c_buf", [P, U, D])
        e_buf = sb("e_buf", [P, U, D])
        res = sb("res", [P, U, D])
        x_out = sb("x_out", [P, U, D])
        side_a = sb("side_a", [P, U, D])
        side_b = sb("side_b", [P, U, D])
        bias = sb("bias", [P, D])
        gamma_row = sb("gamma_row", [P, D])
        beta_row = sb("beta_row", [P, D])
        half = sb("half", [P, 1])

        zt_ps = [psum(f"zt_ps{i}", [P, D]) for i in range(U)]
        y_ps = [psum(f"y_ps{i}", [P, D]) for i in range(U)]
        agg_ps = [psum(f"agg_ps{i}", [P, D]) for i in range(U)]
        at_ps = [psum(f"at_ps{i}", [P, D]) for i in range(U)]

        phases = []

        def phase(name, kind, n, **kw):
            ph = Phase(name, kind, n, phases[-1] if phases else None, **kw)
            phases.append(ph)
            return ph

        def count(ph, name, total):
            s_ = sem(name)
            ph.m[name] = Mark(s_, stood[name])
            stood[name] += total

        def node_rows(t_):
            return t_[0:NR, :]

        L0, L1, L2, L3 = "L0_gnn_", "L1_gnn_", "L2_gnn_", "L3_gnn_"
        w1 = a[L0 + "W1"]
        one = [("tile", KC, 0)]
        phase("norm_in", "norm", NT, out=h0)
        phase("edge_1", "dense", ET, tile=None, gathers=[(h0, src_col), (h0, dst_col)], attr=True, agg=None,
              w=w1, wide=True, raw=w_raw, epi="mish", bias=a[L0 + "b1"], out=e1)
        phase("edge_2", "dense", ET, tile=e1, gathers=[], attr=False, agg=None,
              w=a[L0 + "W2"], wide=False, raw=w_raw, epi="mish", bias=a[L0 + "b2"], out=e2)
        phase("edge_3", "dense", ET, tile=e2, gathers=[], attr=False, agg=None,
              w=a[L0 + "W3"][D:2 * D, :], wide=False, raw=w_raw, epi="copy", bias=None, out=msg)
        phase("node_1", "dense", NT, tile=h0, gathers=[(msg, slot_edge)], attr=False, agg="post",
              w=a[L0 + "W3"][0:D, :], wide=False, raw=w_raw, epi="mish", bias=a[L0 + "b3"], out=u0)
        phase("node_2", "dense", NT, tile=u0, gathers=[], attr=False, agg=None,
              w=a[L0 + "W4"], wide=False, raw=w_raw, epi="norm2", bias=a[L0 + "b4"], side=[h0, None],
              gamma=a[L0 + "gamma"], beta=a[L0 + "beta"], out=ga, x_out=x1)
        g_now, g_next = ga, gb
        n_bn = a[L1 + "W"].shape[0]
        for l in range(n_bn):
            phase(f"bn_{l}", "dense", NT, tile=ga, gathers=[(ga, slot_src)], attr=False, agg="pre",
                  w=a[L1 + "W"][l], wide=False, raw=w_raw_bn, turned=True, epi="bn", bias=None, out=None)
            phase(f"bn_apply_{l}", "apply", NT, bias=a[L1 + "b"][l], gamma=a[L1 + "gamma"][l],
                  beta=a[L1 + "beta"][l], last=l == n_bn - 1, out=ga, x_in=x1, x_out=x2)
        for l in (1, 2):
            phase(f"gcn_{l}", "dense", NT, tile=g_now, gathers=[(g_now, slot_src)], attr=False, agg="pre",
                  w=a[L2 + f"W{l}"], wide=False, raw=w_raw, epi="gcn", bias=a[L2 + f"b{l}"], out=g_next)
            g_now, g_next = g_next, g_now
        phase("gcn_3", "dense", NT, tile=g_now, gathers=[(g_now, slot_src)], attr=False, agg="pre",
              w=a[L2 + "W3"], wide=False, raw=w_raw, epi="gcn_last", bias=a[L2 + "b3"], side=[x2],
              out=h0, x_out=x3)
        phase("sage_edge", "dense", ET, tile=None, gathers=[(h0, src_col)], attr=False, agg=None,
              w=a[L3 + "W"][D:2 * D, :], wide=False, raw=w_raw, epi="copy", bias=None, out=msg)
        phase("sage_node", "dense", NT, tile=h0, gathers=[(msg, slot_edge)], attr=False, agg="sep",
              w=a[L3 + "W"][0:D, :], wide=False, raw=w_raw, epi="sage", bias=a[L3 + "b"], side=[x3], out=out)

        for ph in phases:
            n = ph.n
            per_slot = 16 * (n // U)
            ph.spills = sum(p_.kind == "dense" and p_.agg is not None for p_ in phases[:phases.index(ph)])
            ph.groups = 1
            if ph.kind == "dense":
                if ph.tile is not None:
                    ph.parts = [(tile_in, KC, zt_ps)]
                else:
                    ph.parts = [(gathered, KC, zt_ps)]
                if ph.attr:
                    ph.parts = [(gathered, KC, zt_ps), (tile_in, KC, agg_ps), (attr, 1, at_ps)]
                ph.groups = len(ph.parts)
                ph.hi, ph.lo = (e_hi, e_lo) if ph.wide else (zt_hi, zt_lo)
                ph.wh, ph.wl = (w1_hi, w1_lo) if ph.wide else (w_hi, w_lo)
                ph.chunks = sum(c for _, c, _ in ph.parts)
                count(ph, "w_loaded", 16 * (1 if not ph.wide else 2))
                count(ph, "rows_loaded", 16 * sum(r is not None for r in (ph.bias, ph.gamma,
                                                                        ph.beta)))
                count(ph, "w_turned", KC if ph.turned else 0)
                count(ph, "w_hi_done", ph.chunks)
                count(ph, "w_lo_done", ph.chunks)
                if ph.agg:
                    count(ph, "selected", n)
                count(ph, "turned", n * ph.groups)
                count(ph, "hi_done", n * ph.groups)
                count(ph, "lo_done", n * ph.groups)
                count(ph, "mm_done", n)
                for i in range(len(ph.gathers)):
                    count(ph, f"idx_done{i}", n)
                    for s_ in range(U):
                        count(ph, f"gathered{i}_{s_}", per_slot)
                if ph.attr:
                    for s_ in range(U):
                        count(ph, f"attr{s_}", per_slot)
                e = ph.epi
                if e == "mish":
                    count(ph, "v_done", n)
                    count(ph, "clipped", n)
                    count(ph, "mish_act", 4 * n)
                    count(ph, "res_dve", n)
                elif e == "copy":
                    count(ph, "res_act", n)
                elif e == "bn":
                    count(ph, "kept_done", n)
                    count(ph, "square_done", n)
                    count(ph, "sum_done", n + 1)
                    count(ph, "sq_done", n + 1)
                elif e == "gcn":
                    count(ph, "v_done", n)
                    count(ph, "res_act", n)
                elif e == "gcn_last":
                    count(ph, "side_done", n)
                    count(ph, "x_done", n)
                    count(ph, "res_act", n)
                elif e == "norm2":
                    count(ph, "side_done", 2 * n)
                    count(ph, "v_done", n)
                    count(ph, "normed", n)
                    count(ph, "scaled", n)
                    count(ph, "x_done", n)
                    count(ph, "res_act", n)
                elif e == "sage":
                    count(ph, "v_done", 2 * n)
                    count(ph, "res_dve", n)
                if e in ("gcn_last", "norm2"):
                    for k in ((0, 1) if e == "norm2" else (1,)):
                        count(ph, f"stats{k}", n)
                        count(ph, f"moments{k}", n)
                        count(ph, f"ln_ready{k}", (4 if k == 1 and e == "norm2" else 3) * n)
            if ph.kind == "norm":
                count(ph, "stats1", n)
                count(ph, "moments1", n)
                count(ph, "ln_ready1", 3 * n)
                count(ph, "res_act", n)
            if ph.kind == "apply":
                count(ph, "rows_loaded", 48)
                count(ph, "totals_done", 2)
                count(ph, "bn_dve", 7)
                count(ph, "bn_pool", 2)
                count(ph, "mul_done", n)
                count(ph, "add_done", n)
                count(ph, "res_act", n)
                if ph.last:
                    count(ph, "x_done", n)
                    count(ph, "stats1", n)
                    count(ph, "moments1", n)
                    count(ph, "ln_ready1", 4 * n)
            def loads(what, on):
                for s_ in range(U):
                    if on:
                        count(ph, f"{what}{s_}", per_slot)
            ph.loads_x = ph.kind == "norm" or (ph.kind == "dense" and ph.epi == "norm2")
            loads("loaded", ph.kind == "dense" and ph.tile is not None)
            loads("side_a", (ph.kind == "dense" and len(ph.side) > 0) or (ph.kind == "apply" and ph.last))
            if ph.loads_x:
                for s_ in range(U):
                    count(ph, f"x_loaded{s_}",
                          sum(16 for t in range(s_, n, U) if t < full_nt or (t == full_nt and rest_n)))
            loads("x_stored", ph.x_out is not None and (ph.kind == "dense" or ph.last))
            if ph.kind == "dense" and ph.epi == "sage":
                for s_ in range(U):
                    count(ph, f"stored{s_}",
                          sum(16 for t in range(s_, n, U) if t < full_nt or (t == full_nt and rest_n)))
            else:
                loads("stored", ph.out is not None)

        def hold(eng, step):
            if not step.fixed:
                eng.sem_inc(held[id(eng)], 1)

        def slot_wait(eng, ph, name, step, ahead_of=0):
            m = ph.m[f"{name}{step.slot}"]
            eng.wait_ge(m.sem, m.at(16 * (step.group + 1 - ahead_of // U)))
            if eng is nc.gpsimd:
                hold(eng, step)

        def all_stored(eng, ph):
            for name in ("stored", "x_stored"):
                for s_ in range(U):
                    if f"{name}{s_}" in ph.m:
                        m = ph.m[f"{name}{s_}"]
                        total = m.base + 16 * (ph.n // U)
                        if ph.kind == "dense" and ph.epi == "sage":
                            total = m.base + sum(16 for t in range(s_, ph.n, U)
                                                 if t < full_nt or (t == full_nt and rest_n))
                        eng.wait_ge(m.sem, total)

        def wait(eng, ph, name, n):
            m = ph.m[name]
            eng.wait_ge(m.sem, m.at(n))

        def rows(t_, step):
            return t_[bass.ds(step.index * P, P), :]

        def bcast(row):
            return row.rearrange("(o d) -> o d", o=1).to_broadcast([P, row.shape[0]])

        n_grp = 5
        assert ET % (n_grp * U) == 0 and n_grp * NT <= 512 and NT % U == 0
        of_tile = sb("of_tile", [P, ET, NT], BF16)
        earlier = sb("earlier", [P, ET, NT], BF16)
        of_node = sb("of_node", [P, ET, P], BF16)
        before_me = sb("before_me", [P, P], BF16)
        ones_bf = sb("ones_bf", [P, P], BF16)
        ranked = sb("ranked", [P, U, n_grp, NT])
        lane = sb("lane", [P, 1], I32)
        lane_f = sb("lane_f", [P, 1])
        row_i = sb("row_i", [P, P], I32)
        tile_i = sb("tile_i", [P, ET], I32)
        tile_f = sb("tile_f", [P, ET])
        node_i = sb("node_i", [P, ET], I32)
        node_f = sb("node_f", [P, ET])
        rank = sb("rank", [P, ET])
        over = sb("over", [P, ET])
        position = sb("position", [P, ET], I32)
        payload = sb("payload", [P, ET, 4], I32)
        pay_now = sb("pay_now", [P, U, 4], I32)
        at_now = sb("at_now", [P, U], I32)
        degree = sb("degree", [P, NT])
        deg1 = sb("deg1", [P, NT])
        empty = sb("empty", [P, NT, 4], I32)
        slots = sb("slots", [P, NT, 4], I32)
        node_id = sb("node_id", [P, NT], I32)
        node_id_f = sb("node_id_f", [P, NT])
        real_f = sb("real_f", [P, NT])
        crowded_f = sb("crowded_f", [P, 1])
        many = sb("many", [P, NT])
        slot_f = sb("slot_f", [P, 2, NT])
        spill_f = sb("spill_f", [P, 2, NT])
        last_sum = sb("last_sum", [P, NT], BF16)
        counted = sb("counted", [P, NT])
        s_memset, s_const, s_cols, s_consts = sem("s_memset"), sem("s_const"), sem("s_cols"), sem("s_consts")
        s_prep, s_ranks, s_rank, s_pos = sem("s_prep"), sem("s_ranks"), sem("s_rank"), sem("s_pos")
        s_count, s_pay, s_put = sem("s_count"), sem("s_pay"), [sem("s_put0"), sem("s_put1")]
        s_empty, s_slots, s_table, s_dinv, s_inv = (sem("s_empty"), sem("s_slots"), sem("s_table"), sem("s_dinv"),
                                                    sem("s_inv"))

        def setup_sync(sp):
            sp.wait_ge(s_memset, 2)
            for col, name in ((src_col, "src"), (dst_col, "dst")):
                sp.dma_start(col[0:EP, :], a[name].rearrange("(p k) -> p k", k=ET)).then_inc(s_cols, 16)
            sp.wait_ge(s_memset, 5)
            sp.wait_ge(s_const, 14)
            sp.dma_start(slots_dram.rearrange("(a p) c -> p a c", p=P), empty[:, :, :]).then_inc(s_empty, 16)

        def table_sync(sp):
            for s_ in range(U):
                sp.wait_ge(s_put[s_], 16 * (ET // U))
            sp.dma_start(slots[:, :, :], slots_dram.rearrange("(a p) c -> p a c", p=P)).then_inc(s_slots, 16)

        def setup_pool(pool):
            pool.memset(src_col[:, :], FAR).then_inc(s_memset, 1)
            pool.memset(dst_col[:, :], FAR).then_inc(s_memset, 1)
            pool.memset(empty[:, :, 0:2], FAR).then_inc(s_memset, 1)
            pool.memset(empty[:, :, 2:3], 2 * P).then_inc(s_memset, 1)
            pool.memset(empty[:, :, 3:4], 0).then_inc(s_memset, 1)
            pool.iota(lane[:, :], pattern=[[0, 1]], base=0, channel_multiplier=1).then_inc(s_const, 1)
            pool.iota(row_i[:, :], pattern=[[1, P]], base=0, channel_multiplier=0).then_inc(s_const, 1)
            pool.iota(edge_id[:, :], pattern=[[P, ET]], base=0, channel_multiplier=1).then_inc(s_const, 1)
            pool.iota(node_id[:, :], pattern=[[P, NT]], base=0, channel_multiplier=1).then_inc(s_const, 1)
            pool.memset(minus_half[:, :], -0.5).then_inc(s_const, 1)
            pool.memset(ones_bf[:, :], 1.0).then_inc(s_const, 1)
            pool.memset(ones[:, :], 1.0).then_inc(s_const, 1)
            pool.memset(gathered[:, :, :], 0.0).then_inc(s_const, 1)
            pool.memset(tile_in[:, :, :], 0.0).then_inc(s_const, 1)
            pool.memset(attr[:, :, :], 0.0).then_inc(s_const, 1)
            pool.memset(w_raw[:, 2 * KC, :], 0.0).then_inc(s_const, 1)
            pool.memset(side_b[:, :, :], 0.0).then_inc(s_const, 1)
            pool.memset(side_a[:, :, :], 0.0).then_inc(s_const, 1)
            pool.memset(half[:, :], 0.5).then_inc(s_const, 1)

        def scatter_pool(pool):
            pool.wait_ge(s_empty, 16)
            pool.wait_ge(s_pos, 9)

            def body(step):
                k = step.index
                if step.has(U):
                    pool.wait_ge(s_put[step.slot], 16 * step.group)
                    hold(pool, step)
                pool.tensor_copy(pay_now[:, step.slot, :], payload[:, bass.ds(k, 1), :]
                                 .rearrange("p o c -> p (o c)")).then_inc(s_pay, 1)
                pool.tensor_copy(at_now[:, step.slot:step.slot + 1], position[:, bass.ds(k, 1)]).then_inc(s_pay, 1)
                pool.wait_ge(s_pay, 2 * k + 2)
                hold(pool, step)
                pool.indirect_dma_start(slots_dram[:, :],
                                        bass.IndirectOffsetOnAxis(ap=at_now[:, step.slot:step.slot + 1], axis=0),
                                        pay_now[:, step.slot, :], None, bounds_check=NR - 1,
                                        oob_is_err=False).then_inc(s_put[step.slot], 16)
            steps(pool, ET, body, 0, 0)

        def dinv_pool(pool):
            pool.wait_ge(s_dinv, 1)
            pool.tensor_tensor(deg1[:, :], deg1[:, :], minus_half[:, :], ALU.pow).then_inc(s_inv, 1)

        def setup_vector(dve):
            dve.wait_ge(s_const, 14)
            dve.tensor_copy(lane_f[:, :], lane[:, :]).then_inc(s_consts, 1)
            dve.tensor_copy(iota_row[:, :], row_i[:, :]).then_inc(s_consts, 1)
            dve.tensor_copy(node_id_f[:, :], node_id[:, :]).then_inc(s_consts, 1)
            dve.memset(earlier[:, 0, :], 0.0).then_inc(s_consts, 1)
            dve.wait_ge(s_consts, 4)
            dve.tensor_scalar(ident[:, :], iota_row[:, :], lane_f[:, 0:1], None, ALU.is_equal).then_inc(s_consts, 1)
            dve.tensor_scalar(before_me[:, :], iota_row[:, :], lane_f[:, 0:1], None, ALU.is_gt).then_inc(s_consts, 1)
            dve.tensor_scalar(real_f[:, :], node_id_f[:, :], float(n_nodes), None, ALU.is_lt).then_inc(s_consts, 1)
            dve.memset(degree[:, :], 0.0).then_inc(s_consts, 1)
            dve.wait_ge(s_cols, 32)
            dve.tensor_scalar(tile_i[:, :], dst_col[:, :], 7, None, ALU.logical_shift_right).then_inc(s_pos, 1)
            dve.tensor_scalar(node_i[:, :], dst_col[:, :], P - 1, None, ALU.bitwise_and).then_inc(s_pos, 1)
            dve.wait_ge(s_pos, 2)
            dve.tensor_copy(tile_f[:, :], tile_i[:, :]).then_inc(s_pos, 1)
            dve.tensor_copy(node_f[:, :], node_i[:, :]).then_inc(s_pos, 1)
            dve.wait_ge(s_pos, 4)
            with dve.Fori(0, ET) as k:
                dve.tensor_scalar(of_tile[:, bass.ds(k, 1), :].rearrange("p o a -> p (o a)"), iota_row[:, 0:NT],
                                  tile_f[:, bass.ds(k, 1)], None, ALU.is_equal).then_inc(s_prep, 1)
                dve.tensor_scalar(of_node[:, bass.ds(k, 1), :].rearrange("p o a -> p (o a)"), iota_row[:, :],
                                  node_f[:, bass.ds(k, 1)], None, ALU.is_equal).then_inc(s_prep, 1)
            dve.wait_ge(s_prep, 2 * ET)
            with dve.Fori(1, ET) as k:
                dve.tensor_tensor(earlier[:, bass.ds(k, 1), :], earlier[:, bass.ds(k - 1, 1), :],
                                  of_tile[:, bass.ds(k - 1, 1), :], ALU.add).then_inc(s_prep, 1)
                dve.wait_ge(s_prep, k + 2 * ET)
            dve.tensor_tensor(last_sum[:, :], earlier[:, ET - 1, :], of_tile[:, ET - 1, :],
                              ALU.add).then_inc(s_prep, 1)

            def body(step):
                g, s_ = step.index, step.slot
                dve.wait_ge(s_ranks, g + 1)
                if step.has(U):
                    dve.wait_ge(s_rank, 3 * (g - U) + 3)
                dve.tensor_tensor(ranked[:, s_, :, :].rearrange("p k a -> p (k a)"), y_ps[s_][:, 0:n_grp * NT],
                                  of_tile[:, bass.ds(g * n_grp, n_grp), :].rearrange("p k a -> p (k a)"),
                                  ALU.mult).then_inc(s_rank, 1)
                dve.tensor_tensor(degree[:, :], degree[:, :], agg_ps[s_][:, 0:NT], ALU.add).then_inc(s_rank, 1)
                dve.wait_ge(s_rank, 3 * g + 2)
                dve.tensor_reduce(rank[:, bass.ds(g * n_grp, n_grp)], ranked[:, s_, :, :],
                                  mybir.AxisListType.X, ALU.add).then_inc(s_rank, 1)
            dve.wait_ge(s_consts, 8)
            for g in range(ET // n_grp):
                body(Step(g // U, g % U, ET // n_grp, True))
            dve.wait_ge(s_rank, 3 * ET // n_grp)
            dve.tensor_scalar(over[:, :], rank[:, :], float(P), float(FAR), ALU.is_ge, ALU.mult).then_inc(s_pos, 1)
            dve.scalar_tensor_tensor(out=rank[:, :], in0=tile_f[:, :], scalar=float(P), in1=rank[:, :],
                                     op0=ALU.mult, op1=ALU.add).then_inc(s_pos, 1)
            dve.wait_ge(s_pos, 6)
            dve.tensor_tensor(position[:, :], rank[:, :], over[:, :], ALU.add).then_inc(s_pos, 1)
            dve.tensor_copy(payload[:, :, 0], src_col[:, :]).then_inc(s_pos, 1)
            dve.tensor_copy(payload[:, :, 1], edge_id[:, :])
            dve.tensor_copy(payload[:, :, 2], node_i[:, :])
            dve.tensor_copy(payload[:, :, 3], node_i[:, :]).then_inc(s_pos, 1)
            dve.tensor_scalar(deg1[:, :], degree[:, :], 1.0, None, ALU.add).then_inc(s_dinv, 1)
            dve.tensor_scalar(rdeg[:, :], degree[:, :], 1.0, None, ALU.max).then_inc(s_dinv, 1)
            dve.wait_ge(s_dinv, 2)
            dve.reciprocal(rdeg[:, :], rdeg[:, :]).then_inc(s_dinv, 1)
            dve.wait_ge(s_inv, 1)
            dve.tensor_tensor(dinv[:, :], deg1[:, :], real_f[:, :], ALU.mult).then_inc(s_dinv, 1)
            dve.wait_ge(s_count, 1)
            dve.tensor_scalar(many[:, :], zt_ps[0][:, 0:NT], float(P), None, ALU.is_gt).then_inc(s_dinv, 1)

        def table_vector(dve):
            dve.wait_ge(s_slots, 16)
            dve.wait_ge(s_dinv, 5)
            dve.tensor_copy(slot_f[:, 0, :], slots[:, :, 0]).then_inc(s_table, 1)
            dve.tensor_copy(slot_f[:, 1, :], slots[:, :, 1]).then_inc(s_table, 1)
            dve.tensor_copy(slot_node[:, :], slots[:, :, 2]).then_inc(s_table, 1)
            dve.tensor_scalar(counted[:, :], node_id_f[:, :], -float(FAR), None, ALU.add).then_inc(s_table, 1)
            dve.wait_ge(s_table, 4)
            for i in range(2):
                dve.tensor_scalar(spill_f[:, i, :], slot_f[:, i, :], -1.0, float(FAR), ALU.mult, ALU.add)\
                    .then_inc(s_table, 1)
            dve.tensor_tensor(counted[:, :], counted[:, :], many[:, :], ALU.mult).then_inc(s_table, 1)
            dve.wait_ge(s_table, 7)
            dve.tensor_scalar(spill_row[:, :], counted[:, :], float(FAR), None, ALU.add).then_inc(s_table, 1)
            for i in range(2):
                dve.tensor_tensor(spill_f[:, i, :], spill_f[:, i, :], many[:, :], ALU.mult).then_inc(s_table, 1)
            dve.wait_ge(s_table, 10)
            dve.tensor_tensor(slot_src[:, :], slot_f[:, 0, :], spill_f[:, 0, :], ALU.add).then_inc(s_table, 1)
            dve.tensor_tensor(slot_edge[:, :], slot_f[:, 1, :], spill_f[:, 1, :], ALU.add).then_inc(s_table, 1)
            dve.tensor_scalar(counted[:, :], slot_node[:, :], lane_f[:, 0:1], -1.0, ALU.subtract,
                              ALU.mult).then_inc(s_table, 1)
            dve.wait_ge(s_table, 13)
            dve.tensor_tensor(counted[:, :], counted[:, :], many[:, :], ALU.mult).then_inc(s_table, 1)
            dve.wait_ge(s_table, 14)
            dve.tensor_tensor(slot_node[:, :], slot_node[:, :], counted[:, :], ALU.add).then_inc(s_table, 1)
            dve.tensor_reduce(crowded_f[:, :], many[:, :], mybir.AxisListType.X, ALU.max).then_inc(s_table, 1)
            dve.tensor_copy(dst_f[:, :], dst_col[:, :]).then_inc(s_table, 1)
            dve.wait_ge(s_table, 17)
            dve.tensor_copy(crowded[:, :], crowded_f[:, :]).then_inc(s_table, 1)

        def setup_tensor(pe):
            pe.wait_ge(s_consts, 6)
            pe.wait_ge(s_prep, 3 * ET)
            for g in range(ET // n_grp):
                if g >= U:
                    pe.wait_ge(s_rank, 3 * (g - U) + 3)
                for i in range(n_grp):
                    k = g * n_grp + i
                    o = y_ps[g % U][:, i * NT:(i + 1) * NT]
                    pe.matmul(o, before_me[:, :], of_tile[:, k, :], start=True, stop=False)
                    pe.matmul(o, ones_bf[:, :], earlier[:, k, :], start=False, stop=True)
                for i in range(n_grp):
                    k = g * n_grp + i
                    last = pe.matmul(agg_ps[g % U][:, 0:NT], of_node[:, k, :], of_tile[:, k, :],
                                     start=(i == 0), stop=(i == n_grp - 1))
                last.then_inc(s_ranks, 1)
            pe.matmul(zt_ps[0][:, 0:NT], ones_bf[:, :], last_sum[:, :], start=True, stop=True).then_inc(s_count, 1)

        s_zeroed, s_sp_rows, s_sp_put, s_sp_add = sem("spill_zeroed"), sem("spill_rows"), sem("spill_put"), \
            sem("spill_slots")
        s_sp_pool, s_sp_dve, s_sp_pe, s_sp_idx = sem("spill_pool"), sem("spill_dve"), sem("spill_pe"), \
            sem("spill_idx")

        def load_crowded(eng):
            reg = eng.alloc_register("crowded")
            eng.wait_ge(s_table, 18)
            eng.reg_load(reg, crowded[0:1, 0:1])
            return reg

        def spill_pool(pool, ph, is_crowded):
            table, column = ph.gathers[0][0], (src_col if ph.agg == "pre" else edge_id)
            sp = ph.spills
            with pool.If_ne(is_crowded, 0):
                pool.memset(gathered[:, :, :], 0.0).then_inc(s_sp_pool, 1)
                done = sp * (1 + 2 * ET) + 1
                pool.wait_ge(s_sp_pool, done)
                with pool.Fori(0, NT) as t:
                    pool.dma_start(spill[bass.ds(t * P, P), :], gathered[:, 0, :]).then_inc(s_zeroed, 16)
                pool.wait_ge(s_zeroed, 16 * NT * (sp + 1))
                with pool.Fori(0, ET) as k:
                    pool.tensor_copy(idx_spill[:, 0:1], column[:, bass.ds(k, 1)]).then_inc(s_sp_pool, 1)
                    pool.tensor_copy(idx_spill[:, 1:2], dst_col[:, bass.ds(k, 1)]).then_inc(s_sp_pool, 1)
                    pool.wait_ge(s_sp_pool, 2 * k + (done + 2))
                    pool.sem_inc(held[id(pool)], 1)
                    pool.indirect_dma_start(gathered[:, 0, :], None, table[:, :],
                                            bass.IndirectOffsetOnAxis(ap=idx_spill[:, 0:1], axis=0),
                                            bounds_check=table.shape[0] - 1, oob_is_err=False)\
                        .then_inc(s_sp_rows, 16)
                    pool.indirect_dma_start(gathered[:, 1, :], None, spill[:, :],
                                            bass.IndirectOffsetOnAxis(ap=idx_spill[:, 1:2], axis=0),
                                            bounds_check=NR - 1, oob_is_err=False).then_inc(s_sp_rows, 16)
                    pool.wait_ge(s_sp_dve, 3 * ET * sp + 3 * k + 3)
                    pool.sem_inc(held[id(pool)], 1)
                    pool.indirect_dma_start(spill[:, :], bass.IndirectOffsetOnAxis(ap=idx_spill[:, 1:2], axis=0),
                                            gathered[:, 1, :], None, bounds_check=NR - 1,
                                            oob_is_err=False).then_inc(s_sp_put, 16)
                    pool.wait_ge(s_sp_put, 16 * ET * sp + 16 * k + 16)
                    pool.sem_inc(held[id(pool)], 1)

        def spill_vector(dve, ph, is_crowded):
            sp = ph.spills
            with dve.If_ne(is_crowded, 0):
                with dve.Fori(0, ET) as k:
                    target, done = dst_f[:, bass.ds(k, 1)], 3 * ET * sp
                    dve.wait_ge(s_sp_rows, 32 * ET * sp + 32 * k + 32)
                    dve.tensor_scalar(select[:, 1, :], ones[:, :], target, None, ALU.mult).then_inc(s_sp_dve, 1)
                    dve.wait_ge(s_sp_pe, 2 * ET * sp + 2 * k + 1)
                    dve.tensor_scalar(select[:, 0, :], at_ps[0][:, 0:P], target, None, ALU.is_equal)\
                        .then_inc(s_sp_dve, 1)
                    dve.wait_ge(s_sp_pe, 2 * ET * sp + 2 * k + 2)
                    dve.tensor_tensor(gathered[:, 1, :], gathered[:, 1, :], at_ps[1][:, :], ALU.add)\
                        .then_inc(s_sp_dve, 1)

        def spill_tensor(pe, ph, is_crowded):
            sp = ph.spills
            with pe.If_ne(is_crowded, 0):
                with pe.Fori(0, ET) as k:
                    pe.wait_ge(s_sp_dve, 3 * ET * sp + 3 * k + 1)
                    pe.matmul(at_ps[0][:, 0:P], select[:, 1, :], ident[:, :], start=True, stop=True)\
                        .then_inc(s_sp_pe, 1)
                    pe.wait_ge(s_sp_dve, 3 * ET * sp + 3 * k + 2)
                    pe.matmul(at_ps[1][:, :], select[:, 0, :], gathered[:, 0, :], start=True, stop=True)\
                        .then_inc(s_sp_pe, 1)

        def spill_slots(pool, ph, step, is_crowded):
            at = ph.spills * NT + step.index + 1
            with pool.If_ne(is_crowded, 0):
                pool.tensor_copy(idx_spill[:, 0:1], spill_row[:, bass.ds(step.index, 1)]).then_inc(s_sp_idx, 1)
                pool.wait_ge(s_sp_idx, at)
                hold(pool, step)
                pool.indirect_dma_start(gathered[:, step.slot, :], None, spill[:, :],
                                        bass.IndirectOffsetOnAxis(ap=idx_spill[:, 0:1], axis=0),
                                        bounds_check=NR - 1, oob_is_err=False).then_inc(s_sp_add, 16)
                pool.wait_ge(s_sp_add, 16 * at)
                hold(pool, step)

        def part_rows(t):
            return P if t < full_nt else (rest_n if t == full_nt else 0)

        def phase_sync(sp, ph):
            prev = ph.before
            if ph.kind == "dense":
                if ph.raw is w_raw_bn or prev.kind != "dense":
                    all_stored(sp, prev)
                else:
                    wait(sp, prev, "w_hi_done", prev.chunks)
                    wait(sp, prev, "w_lo_done", prev.chunks)
                if ph.wide:
                    sp.wait_ge(s_const, 14)
                    sp.dma_start(w_raw[:, 0:2 * KC, :], ph.w[0:2 * D, :].rearrange("(c p) d -> p c d", p=P))\
                        .then_inc(ph.m["w_loaded"].sem, 16)
                    sp.dma_start(w_raw[0:DE, 2 * KC, :], ph.w[2 * D:2 * D + DE, :])\
                        .then_inc(ph.m["w_loaded"].sem, 16)
                else:
                    sp.dma_start(ph.raw[:, 0:KC, :], ph.w.rearrange("(c p) d -> p c d", p=P))\
                        .then_inc(ph.m["w_loaded"].sem, 16)
            if prev is not None:
                all_stored(sp, prev)
                if prev.kind == "dense" and prev.epi == "bn":
                    wait(sp, prev, "mm_done", prev.n)
                    wait(sp, prev, "sum_done", prev.n + 1)
                    wait(sp, prev, "sq_done", prev.n + 1)
            if ph.kind != "norm":
                for row, buf in ((ph.bias, bias), (ph.gamma, gamma_row),
                                 (ph.beta, beta_row)):
                    if ph.kind == "apply":
                        buf = {id(bias): gathered[:, 0, :], id(gamma_row): gathered[:, 1, :],
                               id(beta_row): square[:, 0, :]}[id(buf)]
                    else:
                        buf = buf[:, :]
                    if row is not None:
                        sp.dma_start(buf, bcast(row)).then_inc(ph.m["rows_loaded"].sem, 16)
            if ph.kind == "dense" and ph.raw is w_raw_bn:
                wait(sp, ph, "w_turned", KC)

            def inc(name, step):
                return ph.m[f"{name}{step.slot}"].sem

            def load_x(step, buf):
                r = part_rows(step.index) if step.fixed else P
                if r == P:
                    sp.dma_start(buf[:, step.slot, :], rows(x, step)).then_inc(inc("x_loaded", step), 16)
                elif r:
                    sp.dma_start(buf[0:r, step.slot, :], x[full_nt * P:n_nodes, :])\
                        .then_inc(inc("x_loaded", step), 16)

            def body(step):
                far, near, done = step.tile(2), step.tile(1), step.tile(-1)
                if ph.kind == "dense" and ph.tile is not None and far.exists:
                    if far.has(U):
                        wait(sp, ph, "turned", ph.groups * (far.index - U + 1))
                    sp.dma_start(tile_in[:, far.slot, :], rows(ph.tile, far)).then_inc(inc("loaded", far), 16)
                if ph.kind == "dense" and ph.attr and far.exists:
                    if far.has(U):
                        wait(sp, ph, "turned", ph.groups * (far.index - U + 1))
                    sp.dma_start(attr[0:EP, far.slot, 0:DE],
                                 a["edge_attr_64"].rearrange("(p k) d -> p k d", k=ET)[:, bass.ds(far.index, 1), :]
                                 .rearrange("p o d -> p (o d)")).then_inc(inc("attr", far), 16)
                if ph.kind == "norm" and near.exists:
                    if near.has(U):
                        wait(sp, ph, "res_act", near.index - U + 1)
                    load_x(near, tile_in)
                if ph.kind == "dense" and ph.side and near.exists:
                    name = {"norm2": "v_done", "gcn_last": "x_done", "sage": "res_dve"}[ph.epi]
                    if near.has(U):
                        wait(sp, ph, name, near.index - U + 1)
                    sp.dma_start(side_a[:, near.slot, :], rows(ph.side[0], near)).then_inc(inc("side_a", near), 16)
                    if ph.epi == "norm2":
                        if near.has(U):
                            wait(sp, ph, "x_done", near.index - U + 1)
                        load_x(near, side_b)
                if ph.kind == "apply" and ph.last and near.exists:
                    if near.has(U):
                        wait(sp, ph, "x_done", near.index - U + 1)
                    elif near.fixed and near.index == 0:
                        wait(sp, ph, "bn_dve", 7)
                    sp.dma_start(tile_in[:, near.slot, :], rows(ph.x_in, near)).then_inc(inc("side_a", near), 16)
                if ph.x_out is not None and (ph.kind == "dense" or ph.last) and done.exists:
                    wait(sp, ph, "x_done", done.index + 1)
                    buf = x_out[:, done.slot, :] if ph.kind == "dense" else \
                        kept[:, bass.ds(done.index, 1), :].rearrange("p o d -> p (o d)")
                    sp.dma_start(rows(ph.x_out, done), buf).then_inc(inc("x_stored", done), 16)
                if ph.out is not None:
                    late = step.tile(-2) if (ph.kind == "dense" and ph.epi == "norm2") or ph.kind == "apply" else done
                    if late.exists:
                        which = "res_dve" if ph.kind == "dense" and ph.epi in ("mish", "sage") else "res_act"
                        r = part_rows(late.index) if late.fixed and ph.out is out else P
                        if r:
                            wait(sp, ph, which, late.index + 1)
                        if ph.kind == "apply":
                            buf = (gathered[:, late.slot, :] if ph.last else
                                   kept[:, bass.ds(late.index, 1), :].rearrange("p o d -> p (o d)"))
                        else:
                            buf = res[:, late.slot, :]
                        if r == P:
                            sp.dma_start(rows(ph.out, late), buf).then_inc(inc("stored", late), 16)
                        elif r:
                            sp.dma_start(out[full_nt * P:n_nodes, :], buf[0:r, :]).then_inc(inc("stored", late), 16)
            steps(sp, ph.n, body, 2, 2)

        def gather(pool, ph, i, step, is_crowded):
            table, column = ph.gathers[i]
            dest = (gathered, tile_in)[i]
            m = ph.m[f"idx_done{i}"]
            if ph.agg:
                spill_slots(pool, ph, step, is_crowded)
            pool.tensor_copy(idx[:, i, step.slot:step.slot + 1], column[:, bass.ds(step.index, 1)]).then_inc(m.sem, 1)
            pool.wait_ge(m.sem, m.at(step.index + 1))
            hold(pool, step)
            pool.indirect_dma_start(dest[:, step.slot, :], None, table[:, :],
                                    bass.IndirectOffsetOnAxis(ap=idx[:, i, step.slot:step.slot + 1], axis=0),
                                    bounds_check=table.shape[0] - 1, oob_is_err=False)\
                .then_inc(ph.m[f"gathered{i}_{step.slot}"].sem, 16)

        def ln_pool(pool, ph, k, step, scaled):
            m, s_, mv = ph.m[f"ln_ready{k}"], ln_sc[:, k, step.slot, :], ln_mv[:, k, step.slot, :]
            per = 4 if scaled else 3
            done = step.index * per
            wait(pool, ph, f"moments{k}", step.index + 1)
            hold(pool, step)
            pool.tensor_scalar(s_[:, 0:1], mv[:, 1:2], 1.0, EPS, ALU.mult, ALU.add).then_inc(m.sem, 1)
            pool.wait_ge(m.sem, m.at(done + 1))
            if scaled:
                pool.tensor_tensor(s_[:, 1:2], s_[:, 0:1], minus_half[:, 0:1], ALU.pow).then_inc(m.sem, 1)
                pool.wait_ge(m.sem, m.at(done + 2))
                pool.tensor_tensor(s_[:, 2:3], s_[:, 1:2], dinv[:, bass.ds(step.index, 1)], ALU.mult)\
                    .then_inc(m.sem, 1)
            else:
                pool.tensor_tensor(s_[:, 2:3], s_[:, 0:1], minus_half[:, 0:1], ALU.pow).then_inc(m.sem, 1)
            pool.wait_ge(m.sem, m.at(done + per - 1))
            hold(pool, step)
            pool.tensor_scalar(s_[:, 3:4], mv[:, 0:1], s_[:, 2:3], -1.0, ALU.mult, ALU.mult).then_inc(m.sem, 1)

        def ln_scaled(ph, k):
            return ph.kind == "apply" or (ph.kind == "dense" and ph.epi == "norm2" and k == 1)

        def phase_pool(pool, ph, is_crowded):
            if ph.kind == "dense":
                if ph.epi == "bn":
                    pool.memset(bn_sum[:, :], 0.0).then_inc(ph.m["sum_done"].sem, 1)
                if ph.gathers:
                    all_stored(pool, ph.before)
                if ph.turned:
                    wait(pool, ph, "w_turned", KC)
                if ph.agg:
                    spill_pool(pool, ph, is_crowded)
                if ph.epi in ("norm2", "gcn_last"):
                    wait(pool, ph, "rows_loaded", 48 if ph.epi == "norm2" else 16)
            if ph.kind == "apply":
                wait(pool, ph, "bn_dve", 4)
                pool.memset(square[:, 1, :], -0.5).then_inc(ph.m["bn_pool"].sem, 1)
                wait(pool, ph, "bn_pool", 1)
                pool.tensor_tensor(bn_sum[:, :], bn_sum[:, :], square[:, 1, :], ALU.pow)\
                    .then_inc(ph.m["bn_pool"].sem, 1)
                wait(pool, ph, "bn_dve", 7)

            def body(step):
                if ph.kind == "dense":
                    ahead = step.tile(1 if ph.agg in ("post", "sep") else 2)
                    if ahead.exists:
                        for i in range(len(ph.gathers)):
                            if ahead.has(U):
                                if ph.agg in ("post", "sep"):
                                    wait(pool, ph, "mm_done", ahead.index - U + 1)
                                else:
                                    wait(pool, ph, "turned", ph.groups * (ahead.index - U + 1))
                                hold(pool, ahead)
                            gather(pool, ph, i, ahead, is_crowded)
                    if not step.exists and not (step.tile(-1).exists):
                        return
                    if ph.epi == "mish" and step.exists:
                        wait(pool, ph, "v_done", step.index + 1)
                        if step.has(U):
                            wait(pool, ph, "mish_act", 4 * (step.index - U) + 1)
                        hold(pool, step)
                        pool.tensor_scalar(c_buf[:, step.slot, :], v_buf[:, step.slot, :], EXP_MAX, -80.0,
                                           ALU.min, ALU.max).then_inc(ph.m["clipped"].sem, 1)
                    if ph.epi == "bn" and step.exists:
                        wait(pool, ph, "kept_done", step.index + 1)
                        wait(pool, ph, "sum_done", step.index + 1)
                        pool.tensor_tensor(bn_sum[:, :], bn_sum[:, :],
                                           kept[:, bass.ds(step.index, 1), :].rearrange("p o d -> p (o d)"),
                                           ALU.add).then_inc(ph.m["sum_done"].sem, 1)
                    if ph.epi == "norm2" and step.exists:
                        slot_wait(pool, ph, "side_a", step)
                        pool.tensor_tensor(side_a[:, step.slot, :], side_a[:, step.slot, :], bias[:, :], ALU.add)\
                            .then_inc(ph.m["side_done"].sem, 1)
                        if not step.fixed or part_rows(step.index):
                            slot_wait(pool, ph, "x_loaded", step)
                        pool.tensor_tensor(side_b[:, step.slot, :], side_b[:, step.slot, :], beta_row[:, :], ALU.add)\
                            .then_inc(ph.m["side_done"].sem, 1)
                        ln_pool(pool, ph, 0, step, False)
                    if ph.epi == "norm2" and step.tile(-1).exists:
                        before = step.tile(-1)
                        if before.has(U):
                            wait(pool, ph, "res_act", before.index - U + 1)
                        ln_pool(pool, ph, 1, before, True)
                    if ph.epi == "gcn_last" and step.exists:
                        slot_wait(pool, ph, "side_a", step)
                        pool.tensor_tensor(side_a[:, step.slot, :], side_a[:, step.slot, :], bias[:, :], ALU.add)\
                            .then_inc(ph.m["side_done"].sem, 1)
                        if step.has(U):
                            wait(pool, ph, "res_act", step.index - U + 1)
                        ln_pool(pool, ph, 1, step, False)
                elif ph.kind == "norm":
                    if step.exists:
                        if step.has(U):
                            wait(pool, ph, "res_act", step.index - U + 1)
                        ln_pool(pool, ph, 1, step, False)
                elif ph.kind == "apply":
                    if step.exists:
                        wait(pool, ph, "mul_done", step.index + 1)
                        k_ = kept[:, bass.ds(step.index, 1), :].rearrange("p o d -> p (o d)")
                        pool.tensor_tensor(k_, k_, bn_sq[:, :], ALU.add).then_inc(ph.m["add_done"].sem, 1)
                    if ph.last and step.tile(-1).exists:
                        before = step.tile(-1)
                        if before.has(U):
                            wait(pool, ph, "res_act", before.index - U + 1)
                        ln_pool(pool, ph, 1, before, True)
            steps(pool, ph.n, body, 2, 2)

        def phase_tensor(pe, ph, is_crowded):
            if ph.kind == "norm":
                return
            if ph.kind == "apply":
                bn = ph.before
                wait(pe, bn, "sum_done", ph.n + 1)
                pe.matmul(y_ps[0][:, :], ones[:, :], bn_sum[:, :], start=True, stop=True)\
                    .then_inc(ph.m["totals_done"].sem, 1)
                wait(pe, bn, "sq_done", ph.n + 1)
                pe.matmul(y_ps[1][:, :], ones[:, :], bn_sq[:, :], start=True, stop=True)\
                    .then_inc(ph.m["totals_done"].sem, 1)
                return
            G = ph.groups
            if ph.turned:
                wait(pe, ph, "w_loaded", 16)
                for c in range(KC):
                    if c >= U:
                        wait(pe, ph, "w_lo_done", c - U + 1)
                    for o in range(KC):
                        last = pe.transpose(zt_ps[c % U][:, o * P:(o + 1) * P],
                                            ph.raw[:, o, c * P:(c + 1) * P], ident[:, :])
                    last.then_inc(ph.m["w_turned"].sem, 1)
            wait(pe, ph, "w_lo_done", ph.chunks)
            if ph.agg:
                spill_tensor(pe, ph, is_crowded)

            def turn(step):
                for g, (buf, chunks, ps) in enumerate(ph.parts):
                    if step.has(U):
                        wait(pe, ph, "lo_done", G * (step.index - U) + g + 1)
                    if buf is attr:
                        slot_wait(pe, ph, "attr", step)
                    elif ph.tile is not None:
                        slot_wait(pe, ph, "loaded", step)
                    else:
                        slot_wait(pe, ph, f"gathered{g}_", step)
                    if ph.agg == "pre":
                        slot_wait(pe, ph, "gathered0_", step)
                        wait(pe, ph, "selected", step.index + 1)
                    for c in range(chunks):
                        o = ps[step.slot][:, c * P:(c + 1) * P]
                        piece = buf[:, step.slot, c * P:(c + 1) * P]
                        if ph.agg == "pre":
                            pe.matmul(o, piece, ident[:, :], is_transpose=True, start=True, stop=False)
                            last = pe.matmul(o, gathered[:, step.slot, c * P:(c + 1) * P], select[:, step.slot, :],
                                             start=False, stop=True)
                        else:
                            last = pe.transpose(o, piece, ident[:, :])
                    last.then_inc(ph.m["turned"].sem, 1)

            free = {"mish": ("v_done", 1), "copy": ("res_act", 1), "bn": ("square_done", 1), "gcn": ("v_done", 1),
                    "gcn_last": ("x_done", 1), "norm2": ("v_done", 1), "sage": ("v_done", 2)}[ph.epi]

            def body(step):
                near = step.tile(1)
                if near.exists:
                    turn(near)
                if not step.exists:
                    return
                wait(pe, ph, "lo_done", G * (step.index + 1))
                if step.has(U):
                    wait(pe, ph, free[0], free[1] * (step.index - U + 1))
                y = y_ps[step.slot][:, :]
                if ph.agg in ("post", "sep"):
                    slot_wait(pe, ph, "gathered0_", step)
                    wait(pe, ph, "selected", step.index + 1)
                    pe.matmul(y if ph.agg == "post" else agg_ps[step.slot][:, :], select[:, step.slot, :],
                              gathered[:, step.slot, :], start=True, stop=ph.agg == "sep")
                for c in range(ph.chunks):
                    hi = ph.hi[:, step.slot, c * P:(c + 1) * P]
                    lo = ph.lo[:, step.slot, c * P:(c + 1) * P]
                    pe.matmul(y, lo, ph.wh[:, c, :], start=c == 0 and ph.agg != "post", stop=False)
                    pe.matmul(y, hi, ph.wl[:, c, :], start=False, stop=False)
                    last = pe.matmul(y, hi, ph.wh[:, c, :], start=False, stop=c == ph.chunks - 1)
                last.then_inc(ph.m["mm_done"].sem, 1)
            steps(pe, ph.n, body, 1, 0)

        def phase_scalar(act, ph):
            if ph.kind == "dense":
                if ph.before.kind == "dense":
                    wait(act, ph.before, "mm_done", ph.before.n)
                if not ph.turned:
                    wait(act, ph, "w_loaded", 16 * (2 if ph.wide else 1))
                for c in range(ph.chunks):
                    if ph.turned:
                        wait(act, ph, "w_turned", c + 1)
                    src = zt_ps[c % U][:, :] if ph.turned else ph.raw[:, c, :]
                    nc.scalar.activation(ph.wh[:, c, :], src, ACT.Copy).then_inc(ph.m["w_hi_done"].sem, 1)

            def body(step):
                near, before, older = step.tile(1), step.tile(-1), step.tile(-2)
                s_ = step.slot
                if ph.kind == "dense" and near.exists:
                    for g, (buf, chunks, ps) in enumerate(ph.parts):
                        wait(act, ph, "turned", ph.groups * near.index + g + 1)
                        if near.has(U):
                            wait(act, ph, "mm_done", near.index - U + 1)
                        at = g * KC * P
                        nc.scalar.activation(ph.hi[:, near.slot, at:at + chunks * P],
                                             ps[near.slot][:, 0:chunks * P], ACT.Copy)\
                            .then_inc(ph.m["hi_done"].sem, 1)
                if ph.kind == "dense" and step.exists:
                    if ph.epi == "mish":
                        m, e = ph.m["mish_act"], e_buf[:, s_, :]
                        wait(act, ph, "clipped", step.index + 1)
                        if step.has(U):
                            wait(act, ph, "res_dve", step.index - U + 1)
                        nc.scalar.activation(e, c_buf[:, s_, :], ACT.Exp).then_inc(m.sem, 1)
                        act.wait_ge(m.sem, m.at(4 * step.index + 1))
                        nc.scalar.activation(e, e, ACT.Square, bias=1.0).then_inc(m.sem, 1)
                        act.wait_ge(m.sem, m.at(4 * step.index + 2))
                        nc.scalar.activation(e, e, ACT.Ln, bias=half[:, 0:1], scale=0.5).then_inc(m.sem, 1)
                        act.wait_ge(m.sem, m.at(4 * step.index + 3))
                        nc.scalar.activation(e, e, ACT.Exp, scale=-1.0).then_inc(m.sem, 1)
                    if ph.epi == "copy":
                        wait(act, ph, "mm_done", step.index + 1)
                        if step.has(U):
                            slot_wait(act, ph, "stored", step, U)
                        nc.scalar.activation(res[:, s_, :], y_ps[s_][:, :], ACT.Copy)\
                            .then_inc(ph.m["res_act"].sem, 1)
                    if ph.epi == "bn":
                        wait(act, ph, "mm_done", step.index + 1)
                        hold(act, step)
                        d = dinv[:, bass.ds(step.index, 1)]
                        nc.scalar.activation(kept[:, bass.ds(step.index, 1), :].rearrange("p o d -> p (o d)"),
                                             y_ps[s_][:, :], ACT.Identity, scale=d)\
                            .then_inc(ph.m["kept_done"].sem, 1)
                        if step.has(U):
                            wait(act, ph, "sq_done", step.index - U + 2)
                        hold(act, step)
                        nc.scalar.activation(square[:, s_, :], y_ps[s_][:, :], ACT.Square, scale=d)\
                            .then_inc(ph.m["square_done"].sem, 1)
                    if ph.epi == "gcn":
                        wait(act, ph, "v_done", step.index + 1)
                        if step.has(U):
                            slot_wait(act, ph, "stored", step, U)
                        hold(act, step)
                        nc.scalar.activation(res[:, s_, :], v_buf[:, s_, :], ACT.Relu,
                                             scale=dinv[:, bass.ds(step.index, 1)])\
                            .then_inc(ph.m["res_act"].sem, 1)
                    if ph.epi == "norm2":
                        wait(act, ph, "ln_ready0", 3 * (step.index + 1))
                        sc = ln_sc[:, 0, s_, :]
                        nc.scalar.activation(v_buf[:, s_, :], v_buf[:, s_, :], ACT.Identity,
                                             scale=sc[:, 2:3], bias=sc[:, 3:4]).then_inc(ph.m["normed"].sem, 1)

                def normed_relu(of, source, target):
                    wait(act, ph, "ln_ready1", (4 if ln_scaled(ph, 1) else 3) * (of.index + 1))
                    if of.has(U):
                        slot_wait(act, ph, "stored", of, U)
                    hold(act, of)
                    sc = ln_sc[:, 1, of.slot, :]
                    nc.scalar.activation(target, source, ACT.Relu, scale=sc[:, 2:3], bias=sc[:, 3:4])\
                        .then_inc(ph.m["res_act"].sem, 1)

                if ph.kind == "dense" and ph.epi == "norm2" and older.exists:
                    normed_relu(older, x_out[:, older.slot, :], res[:, older.slot, :])
                if ph.kind == "dense" and ph.epi == "gcn_last" and before.exists:
                    normed_relu(before, x_out[:, before.slot, :], res[:, before.slot, :])
                if ph.kind == "norm" and before.exists:
                    normed_relu(before, tile_in[:, before.slot, :], res[:, before.slot, :])
                if ph.kind == "apply":
                    if not ph.last and step.exists:
                        k_ = kept[:, bass.ds(step.index, 1), :].rearrange("p o d -> p (o d)")
                        wait(act, ph, "add_done", step.index + 1)
                        hold(act, step)
                        nc.scalar.activation(k_, k_, ACT.Relu, scale=dinv[:, bass.ds(step.index, 1)])\
                            .then_inc(ph.m["res_act"].sem, 1)
                    if ph.last and older.exists:
                        k_ = kept[:, bass.ds(older.index, 1), :].rearrange("p o d -> p (o d)")
                        normed_relu(older, k_, gathered[:, older.slot, :])
            steps(act, ph.n, body, 1, 2)

        def phase_vector(dve, ph, is_crowded):
            def moments(k, of, source):
                st, mv, own = ln_st[:, k, of.slot, :], ln_mv[:, k, of.slot, :], ph.m[f"stats{k}"]
                if of.has(U):
                    wait(dve, ph, f"moments{k}", of.index - U + 1)
                hold(dve, of)
                dve.bn_stats(st, source).then_inc(own.sem, 1)
                dve.wait_ge(own.sem, own.at(of.index + 1))
                if of.has(U):
                    wait(dve, ph, f"ln_ready{k}", (4 if ln_scaled(ph, k) else 3) * (of.index - U + 1))
                hold(dve, of)
                dve.bn_aggr(mv, st).then_inc(ph.m[f"moments{k}"].sem, 1)

            if ph.kind == "dense":
                if ph.before.kind == "dense":
                    wait(dve, ph.before, "mm_done", ph.before.n)
                for c in range(ph.chunks):
                    wait(dve, ph, "w_hi_done", c + 1)
                    src = zt_ps[c % U][:, :] if ph.turned else ph.raw[:, c, :]
                    dve.tensor_tensor(ph.wl[:, c, :], src, ph.wh[:, c, :].bitcast(F32), ALU.subtract)\
                        .then_inc(ph.m["w_lo_done"].sem, 1)
                if ph.epi == "bn":
                    dve.memset(bn_sq[:, :], 0.0).then_inc(ph.m["sq_done"].sem, 1)
                if ph.epi in ("mish", "gcn", "sage", "norm2"):
                    wait(dve, ph, "rows_loaded", 48 if ph.epi == "norm2" else 16)
            if ph.kind == "apply":
                b_row, g_row, beta_r = gathered[:, 0, :], gathered[:, 1, :], square[:, 0, :]
                mean, t1 = tile_in[:, 0, :], tile_in[:, 1, :]
                own = ph.m["bn_dve"]
                wait(dve, ph, "totals_done", 1)
                dve.tensor_scalar(mean, y_ps[0][:, :], 1.0 / n_nodes, None, ALU.mult).then_inc(own.sem, 1)
                wait(dve, ph, "bn_dve", 1)
                dve.tensor_tensor(t1, mean, mean, ALU.mult).then_inc(own.sem, 1)
                wait(dve, ph, "totals_done", 2)
                wait(dve, ph, "bn_dve", 2)
                dve.scalar_tensor_tensor(out=bn_sum[:, :], in0=y_ps[1][:, :], scalar=1.0 / n_nodes, in1=t1,
                                         op0=ALU.mult, op1=ALU.subtract).then_inc(own.sem, 1)
                wait(dve, ph, "bn_dve", 3)
                dve.tensor_scalar(bn_sum[:, :], bn_sum[:, :], 0.0, EPS, ALU.max, ALU.add).then_inc(own.sem, 1)
                wait(dve, ph, "rows_loaded", 48)
                wait(dve, ph, "bn_pool", 2)
                dve.tensor_tensor(bn_sum[:, :], bn_sum[:, :], g_row, ALU.mult).then_inc(own.sem, 1)
                dve.tensor_tensor(mean, mean, b_row, ALU.add).then_inc(own.sem, 1)
                wait(dve, ph, "bn_dve", 6)
                dve.tensor_tensor(t1, b_row, mean, ALU.subtract).then_inc(s_bn_tail, 1)
                bn_tail[0] += 1
                dve.wait_ge(s_bn_tail, bn_tail[0])
                dve.tensor_tensor(t1, t1, bn_sum[:, :], ALU.mult).then_inc(s_bn_tail, 1)
                bn_tail[0] += 1
                dve.wait_ge(s_bn_tail, bn_tail[0])
                dve.tensor_tensor(bn_sq[:, :], t1, beta_r, ALU.add).then_inc(own.sem, 1)

            if ph.kind == "dense" and ph.agg:
                spill_vector(dve, ph, is_crowded)

            def choose(step):
                if ph.agg == "pre":
                    if step.has(U):
                        wait(dve, ph, "turned", step.index - U + 1)
                elif step.has(U):
                    wait(dve, ph, "mm_done", step.index - U + 1)
                dve.tensor_scalar(select[:, step.slot, :], iota_row[:, :], slot_node[:, bass.ds(step.index, 1)],
                                  None, ALU.is_equal).then_inc(ph.m["selected"].sem, 1)

            def body(step):
                near, before, s_ = step.tile(1), step.tile(-1), step.slot
                if ph.kind == "dense" and near.exists:
                    for g, (buf, chunks, ps) in enumerate(ph.parts):
                        wait(dve, ph, "hi_done", ph.groups * near.index + g + 1)
                        if near.has(U):
                            wait(dve, ph, "mm_done", near.index - U + 1)
                        at = g * KC * P
                        dve.tensor_tensor(ph.lo[:, near.slot, at:at + chunks * P], ps[near.slot][:, 0:chunks * P],
                                          ph.hi[:, near.slot, at:at + chunks * P].bitcast(F32), ALU.subtract)\
                            .then_inc(ph.m["lo_done"].sem, 1)
                if ph.kind == "dense" and ph.agg:
                    ahead = step.tile(2 if ph.agg == "pre" else 1)
                    if ahead.exists:
                        choose(ahead)
                if ph.kind == "dense" and step.exists:
                    wait_mm = ph.epi in ("mish", "gcn", "gcn_last", "norm2", "sage")
                    if wait_mm:
                        wait(dve, ph, "mm_done", step.index + 1)
                    if ph.epi == "mish":
                        if step.has(U):
                            wait(dve, ph, "res_dve", step.index - U + 1)
                        dve.tensor_tensor(v_buf[:, s_, :], y_ps[s_][:, :], bias[:, :], ALU.add)\
                            .then_inc(ph.m["v_done"].sem, 1)
                    if ph.epi == "bn":
                        wait(dve, ph, "square_done", step.index + 1)
                        wait(dve, ph, "sq_done", step.index + 1)
                        dve.tensor_tensor(bn_sq[:, :], bn_sq[:, :], square[:, s_, :], ALU.add)\
                            .then_inc(ph.m["sq_done"].sem, 1)
                    if ph.epi == "gcn":
                        if step.has(U):
                            wait(dve, ph, "res_act", step.index - U + 1)
                        dve.scalar_tensor_tensor(out=v_buf[:, s_, :], in0=y_ps[s_][:, :],
                                                 scalar=dinv[:, bass.ds(step.index, 1)], in1=bias[:, :],
                                                 op0=ALU.mult, op1=ALU.add).then_inc(ph.m["v_done"].sem, 1)
                    if ph.epi == "gcn_last":
                        wait(dve, ph, "side_done", step.index + 1)
                        if step.has(U):
                            wait(dve, ph, "res_act", step.index - U + 1)
                            slot_wait(dve, ph, "x_stored", step, U)
                        dve.scalar_tensor_tensor(out=x_out[:, s_, :], in0=y_ps[s_][:, :],
                                                 scalar=dinv[:, bass.ds(step.index, 1)], in1=side_a[:, s_, :],
                                                 op0=ALU.mult, op1=ALU.add).then_inc(ph.m["x_done"].sem, 1)
                        wait(dve, ph, "x_done", step.index + 1)
                        moments(1, step, x_out[:, s_, :])
                    if ph.epi == "norm2":
                        wait(dve, ph, "side_done", 2 * step.index + 2)
                        if step.has(U):
                            wait(dve, ph, "x_done", step.index - U + 1)
                        dve.tensor_tensor(v_buf[:, s_, :], y_ps[s_][:, :], side_a[:, s_, :], ALU.add)\
                            .then_inc(ph.m["v_done"].sem, 1)
                        wait(dve, ph, "v_done", step.index + 1)
                        moments(0, step, v_buf[:, s_, :])
                    if ph.epi == "sage":
                        m = ph.m["v_done"]
                        if step.has(U):
                            wait(dve, ph, "res_dve", step.index - U + 1)
                        dve.scalar_tensor_tensor(out=v_buf[:, s_, :], in0=agg_ps[s_][:, :],
                                                 scalar=rdeg[:, bass.ds(step.index, 1)], in1=bias[:, :],
                                                 op0=ALU.mult, op1=ALU.add).then_inc(m.sem, 1)
                        dve.wait_ge(m.sem, m.at(2 * step.index + 1))
                        dve.tensor_tensor(v_buf[:, s_, :], v_buf[:, s_, :], y_ps[s_][:, :], ALU.add)\
                            .then_inc(m.sem, 1)
                        dve.wait_ge(m.sem, m.at(2 * step.index + 2))
                        slot_wait(dve, ph, "side_a", step)
                        if step.has(U):
                            slot_wait(dve, ph, "stored", step, U)
                        dve.scalar_tensor_tensor(out=res[:, s_, :], in0=v_buf[:, s_, :], scalar=0.0,
                                                 in1=side_a[:, s_, :], op0=ALU.max, op1=ALU.add)\
                            .then_inc(ph.m["res_dve"].sem, 1)
                if ph.kind == "dense" and before.exists:
                    b_ = before.slot
                    if ph.epi == "mish":
                        wait(dve, ph, "mish_act", 4 * before.index + 4)
                        if before.has(U):
                            slot_wait(dve, ph, "stored", before, U)
                        dve.scalar_tensor_tensor(out=res[:, b_, :], in0=e_buf[:, b_, :], scalar=1.0,
                                                 in1=v_buf[:, b_, :], op0=ALU.subtract, op1=ALU.mult,
                                                 reverse0=True).then_inc(ph.m["res_dve"].sem, 1)
                    if ph.epi == "norm2":
                        wait(dve, ph, "normed", before.index + 1)
                        dve.tensor_tensor(v_buf[:, b_, :], v_buf[:, b_, :], gamma_row[:, :], ALU.mult)\
                            .then_inc(ph.m["scaled"].sem, 1)
                        wait(dve, ph, "scaled", before.index + 1)
                        if before.has(U):
                            wait(dve, ph, "res_act", before.index - U + 1)
                            slot_wait(dve, ph, "x_stored", before, U)
                        dve.tensor_tensor(x_out[:, b_, :], v_buf[:, b_, :], side_b[:, b_, :], ALU.add)\
                            .then_inc(ph.m["x_done"].sem, 1)
                        wait(dve, ph, "x_done", before.index + 1)
                        moments(1, before, x_out[:, b_, :])
                if ph.kind == "norm" and step.exists:
                    if not step.fixed or part_rows(step.index):
                        slot_wait(dve, ph, "x_loaded", step)
                    moments(1, step, tile_in[:, s_, :])
                if ph.kind == "apply":
                    if step.exists:
                        if step.fixed and step.index == 0:
                            wait(dve, ph, "bn_dve", 7)
                        k_ = kept[:, bass.ds(step.index, 1), :].rearrange("p o d -> p (o d)")
                        dve.tensor_tensor(k_, k_, bn_sum[:, :], ALU.mult).then_inc(ph.m["mul_done"].sem, 1)
                    if ph.last and before.exists:
                        k_ = kept[:, bass.ds(before.index, 1), :].rearrange("p o d -> p (o d)")
                        wait(dve, ph, "add_done", before.index + 1)
                        slot_wait(dve, ph, "side_a", before)
                        dve.scalar_tensor_tensor(out=k_, in0=k_, scalar=0.0, in1=tile_in[:, before.slot, :],
                                                 op0=ALU.max, op1=ALU.add).then_inc(ph.m["x_done"].sem, 1)
                        wait(dve, ph, "x_done", before.index + 1)
                        moments(1, before, k_)
            steps(dve, ph.n, body, 2, 2)

        held = {id(nc.gpsimd): sem("held_pool"), id(nc.scalar): sem("held_act"), id(nc.vector): sem("held_dve")}
        s_bn_tail = sem("s_bn_tail")
        bn_tail = [0]

        block = ctx.enter_context(nc.Block())

        @block.sync
        def _(sp):
            setup_sync(sp)
            for ph in phases:
                phase_sync(sp, ph)
                if ph.kind == "norm":
                    table_sync(sp)
            all_stored(sp, phases[-1])

        @block.gpsimd
        def _(pool):
            setup_pool(pool)
            dinv_pool(pool)
            scatter_pool(pool)
            is_crowded = None
            for ph in phases:
                if ph.kind != "norm" and is_crowded is None and ph.agg:
                    is_crowded = load_crowded(pool)
                phase_pool(pool, ph, is_crowded)

        @block.scalar
        def _(act):
            act.wait_ge(s_const, 14)
            nc.scalar.preload_act_table_set("natural_log_exp_and_others")
            for ph in phases:
                phase_scalar(act, ph)

        @block.vector
        def _(dve):
            setup_vector(dve)
            is_crowded = None
            for ph in phases:
                phase_vector(dve, ph, is_crowded)
                if ph.kind == "norm":
                    table_vector(dve)
                    is_crowded = load_crowded(dve)

        @block.tensor
        def _(pe):
            setup_tensor(pe)
            is_crowded = None
            for ph in phases:
                if ph.kind != "norm" and is_crowded is None and ph.agg:
                    is_crowded = load_crowded(pe)
                phase_tensor(pe, ph, is_crowded)


def kernel(**inputs):
    import numpy as _np
    import concourse.bacc as _bacc
    from concourse import mybir as _mybir
    from concourse.bass_utils import run_bass_kernel_spmd as _run

    nc = _bacc.Bacc("TRN2", target_bir_lowering=False, num_devices=1)
    arrays, handles = {}, {}
    for name, value in inputs.items():
        v = _np.ascontiguousarray(value)
        arrays[f"in_{name}"] = v
        handles[name] = nc.dram_tensor(f"in_{name}", v.shape, _mybir.dt.from_np(v.dtype), kind="ExternalInput").ap()
    out = nc.dram_tensor("out_x", inputs["x"].shape, _mybir.dt.float32, kind="ExternalOutput").ap()
    build(nc, handles, out)
    r = _run(nc, [arrays], core_ids=[0])
    return r.results[0]["out_x"]
```

```python
from contextlib import ExitStack

import numpy as np
import concourse.bass as bass
from concourse import mybir

ALU = mybir.AluOpType
ACT = mybir.ActivationFunctionType
F32 = mybir.dt.float32
F32R = mybir.dt.float32r
BF16 = mybir.dt.bfloat16
I32 = mybir.dt.int32

P = 128
U = 4
T = 2
EPS = 1e-5
FAR = 1 << 20
EXP_MAX = 20.0


class Mark:

    def __init__(self, sem, base):
        self.sem, self.base = sem, base

    def at(self, n):
        return self.base + n


class Step:

    def __init__(self, group, lane, n, fixed):
        self.group, self.lane, self.n, self.fixed = group, lane, n, fixed

    def tile(self, ahead):
        return Step(self.group + (self.lane + ahead) // U, (self.lane + ahead) % U, self.n, self.fixed)

    @property
    def index(self):
        return self.group * U + self.lane

    @property
    def slot(self):
        return self.lane

    @property
    def pair(self):
        return self.lane % T

    @property
    def exists(self):
        return not self.fixed or 0 <= self.index < self.n

    def has(self, before):
        return not self.fixed or self.index >= before


def steps(eng, n, body, ahead, behind):
    first = 2 * U
    last = (n - 2 * U) // U * U
    for t in range(-ahead, first):
        body(Step(t // U, t % U, n, True))
    with eng.Fori(first // U, last // U) as group:
        for lane in range(U):
            body(Step(group, lane, n, False))
    for t in range(last, n + behind):
        body(Step(t // U, t % U, n, True))


class Phase:

    def __init__(self, name, kind, n, before, out=None, tile=None, gathers=(), attr=False, agg=None, w=None,
                 wide=False, raw=None, turned=False, epi=None, bias=None, gamma=None, beta=None, side=(),
                 x_in=None, x_out=None, last=False):
        self.name, self.kind, self.n, self.before = name, kind, n, before
        self.m = {}
        self.out, self.x_in, self.x_out = out, x_in, x_out
        self.tile, self.gathers, self.attr, self.side = tile, gathers, attr, side
        self.agg = agg
        self.w, self.wide, self.raw, self.turned = w, wide, raw, turned
        self.epi, self.bias, self.gamma, self.beta, self.last = epi, bias, gamma, beta, last


def build(nc, a, out):
    x = a["x"]
    n_nodes, D = x.shape
    n_edges = a["src"].shape[0]
    DE = a["edge_attr_64"].shape[1]
    KC = D // P
    NT = -(-n_nodes // P)
    NT += -NT % U
    ET = -(-n_edges // P)
    ET += -ET % U
    NR, ER = NT * P, ET * P
    full_nt, rest_n = n_nodes // P, n_nodes % P
    EP = n_edges // ET
    assert EP * ET == n_edges and EP <= P

    def scratch(name, shape, dt=F32):
        return nc.dram_tensor(name, shape, dt, kind="Internal").ap()

    h0 = scratch("h0", [NR, D])
    ga = scratch("ga", [NR, D])
    gb = scratch("gb", [NR, D])
    msg = scratch("msg", [ER, D])
    e1 = scratch("e1", [ER, D])
    e2 = scratch("e2", [ER, D])
    u0 = scratch("u0", [NR, D])
    x1 = scratch("x1", [NR, D])
    x2 = scratch("x2", [NR, D])
    x3 = scratch("x3", [NR, D])
    spill = scratch("spill", [NR, D])
    slots_dram = scratch("slot_table", [NR, 4], I32)

    with ExitStack() as ctx:
        def sb(name, shape, dt=F32):
            return ctx.enter_context(nc.sbuf_tensor(name, shape, dt))

        def psum(name, shape, dt=F32):
            return ctx.enter_context(nc.psum_tensor(name, shape, dt))

        sems, stood = {}, {}

        def sem(name):
            if name not in sems:
                sems[name] = ctx.enter_context(nc.semaphore(name))
                stood[name] = 0
            return sems[name]

        w_hi = sb("w_hi", [P, KC, D], F32R)
        w_lo = sb("w_lo", [P, KC, D], F32R)
        rest = ExitStack()
        normed_out = rest.enter_context(nc.sbuf_tensor("normed_out", [P, U, D], F32))
        rest.close()
        zt_hi = sb("zt_hi", [P, T, KC * P], F32R)
        zt_lo = sb("zt_lo", [P, T, KC * P], F32R)
        share = ExitStack()
        w_raw_bn = share.enter_context(nc.sbuf_tensor("w_raw_bn", [P, KC, D], F32))
        share.close()
        tile_in = sb("tile_in", [P, T, D])
        gathered = sb("gathered", [P, T, D])
        select = sb("select", [P, T, P])
        ident = sb("ident", [P, P])
        ones = sb("ones", [P, P])
        iota_row = sb("iota_row", [P, P])
        src_col = sb("src_col", [P, ET], I32)
        dst_col = sb("dst_col", [P, ET], I32)
        dst_f = sb("dst_f", [P, ET])
        edge_id = sb("edge_id", [P, ET], I32)
        slot_src = sb("slot_src", [P, NT], I32)
        slot_edge = sb("slot_edge", [P, NT], I32)
        slot_node = sb("slot_node", [P, NT])
        spill_row = sb("spill_row", [P, NT], I32)
        dinv = sb("dinv", [P, NT])
        rdeg = sb("rdeg", [P, NT])
        minus_half = sb("minus_half", [P, NT])
        idx = sb("idx", [P, 2, T], I32)
        idx_spill = sb("idx_spill", [P, 2], I32)
        crowded = sb("crowded", [P, 1], I32)
        ln_st = sb("ln_st", [P, 2, U, 6])
        ln_mv = sb("ln_mv", [P, 2, U, 2])
        ln_sc = sb("ln_sc", [P, 2, U, 4])
        own = ExitStack()
        bn_sum = own.enter_context(nc.sbuf_tensor("bn_sum", [P, D], F32))
        bn_sq = own.enter_context(nc.sbuf_tensor("bn_sq", [P, D], F32))
        square = own.enter_context(nc.sbuf_tensor("square", [P, T, D], F32))
        kept = own.enter_context(nc.sbuf_tensor("kept", [P, NT, D], F32))
        own.close()

        w_raw = sb("w_raw", [P, 2 * KC + 1, D])
        w1_hi = sb("w1_hi", [P, 2 * KC + 1, D], F32R)
        w1_lo = sb("w1_lo", [P, 2 * KC + 1, D], F32R)
        e_hi = sb("e_hi", [P, T, (2 * KC + 1) * P], F32R)
        e_lo = sb("e_lo", [P, T, (2 * KC + 1) * P], F32R)
        attr = sb("attr", [P, T, P])
        v_buf = sb("v_buf", [P, U, D])
        c_buf = sb("c_buf", [P, U, D])
        e_buf = sb("e_buf", [P, U, D])
        res = sb("res", [P, U, D])
        x_out = sb("x_out", [P, U, D])
        side_a = sb("side_a", [P, U, D])
        side_b = sb("side_b", [P, U, D])
        bias = sb("bias", [P, D])
        gamma_row = sb("gamma_row", [P, D])
        beta_row = sb("beta_row", [P, D])
        half = sb("half", [P, 1])

        x_slots = [tile_in[:, 0, :], tile_in[:, 1, :], gathered[:, 0, :], gathered[:, 1, :]]
        zt_ps = [psum(f"zt_ps{i}", [P, D]) for i in range(T)]
        y_ps = [psum(f"y_ps{i}", [P, D]) for i in range(T)]
        agg_ps = [psum(f"agg_ps{i}", [P, D]) for i in range(T)]
        at_ps = [psum(f"at_ps{i}", [P, D]) for i in range(T)]

        phases = []

        def phase(name, kind, n, **kw):
            ph = Phase(name, kind, n, phases[-1] if phases else None, **kw)
            phases.append(ph)
            return ph

        def count(ph, name, total):
            s_ = sem(name)
            ph.m[name] = Mark(s_, stood[name])
            stood[name] += total

        def node_rows(t_):
            return t_[0:NR, :]

        L0, L1, L2, L3 = "L0_gnn_", "L1_gnn_", "L2_gnn_", "L3_gnn_"
        w1 = a[L0 + "W1"]
        one = [("tile", KC, 0)]
        phase("norm_in", "norm", NT, out=h0)
        phase("edge_1", "dense", ET, tile=None, gathers=[(h0, src_col), (h0, dst_col)], attr=True, agg=None,
              w=w1, wide=True, raw=w_raw, epi="mish", bias=a[L0 + "b1"], out=e1)
        phase("edge_2", "dense", ET, tile=e1, gathers=[], attr=False, agg=None,
              w=a[L0 + "W2"], wide=False, raw=w_raw, epi="mish", bias=a[L0 + "b2"], out=e2)
        phase("edge_3", "dense", ET, tile=e2, gathers=[], attr=False, agg=None,
              w=a[L0 + "W3"][D:2 * D, :], wide=False, raw=w_raw, epi="copy", bias=None, out=msg)
        phase("node_1", "dense", NT, tile=h0, gathers=[(msg, slot_edge)], attr=False, agg="post",
              w=a[L0 + "W3"][0:D, :], wide=False, raw=w_raw, epi="mish", bias=a[L0 + "b3"], out=u0)
        phase("node_2", "dense", NT, tile=u0, gathers=[], attr=False, agg=None,
              w=a[L0 + "W4"], wide=False, raw=w_raw, epi="norm2", bias=a[L0 + "b4"], side=[h0, None],
              gamma=a[L0 + "gamma"], beta=a[L0 + "beta"], out=ga, x_out=x1)
        g_now, g_next = ga, gb
        n_bn = a[L1 + "W"].shape[0]
        for l in range(n_bn):
            phase(f"bn_{l}", "dense", NT, tile=ga, gathers=[(ga, slot_src)], attr=False, agg="pre",
                  w=a[L1 + "W"][l], wide=False, raw=w_raw_bn, turned=True, epi="bn", bias=None, out=None)
            phase(f"bn_apply_{l}", "apply", NT, bias=a[L1 + "b"][l], gamma=a[L1 + "gamma"][l],
                  beta=a[L1 + "beta"][l], last=l == n_bn - 1, out=ga, x_in=x1, x_out=x2)
        for l in (1, 2):
            phase(f"gcn_{l}", "dense", NT, tile=g_now, gathers=[(g_now, slot_src)], attr=False, agg="pre",
                  w=a[L2 + f"W{l}"], wide=False, raw=w_raw, epi="gcn", bias=a[L2 + f"b{l}"], out=g_next)
            g_now, g_next = g_next, g_now
        phase("gcn_3", "dense", NT, tile=g_now, gathers=[(g_now, slot_src)], attr=False, agg="pre",
              w=a[L2 + "W3"], wide=False, raw=w_raw, epi="gcn_last", bias=a[L2 + "b3"], side=[x2],
              out=h0, x_out=x3)
        phase("sage_edge", "dense", ET, tile=None, gathers=[(h0, src_col)], attr=False, agg=None,
              w=a[L3 + "W"][D:2 * D, :], wide=False, raw=w_raw, epi="copy", bias=None, out=msg)
        phase("sage_node", "dense", NT, tile=h0, gathers=[(msg, slot_edge)], attr=False, agg="sep",
              w=a[L3 + "W"][0:D, :], wide=False, raw=w_raw, epi="sage", bias=a[L3 + "b"], side=[x3], out=out)

        BN_STEPS = 13

        def ring(what):
            return T if what.startswith(("loaded", "gathered", "attr")) else U

        for ph in phases:
            n = ph.n
            ph.spills = sum(p_.kind == "dense" and p_.agg is not None for p_ in phases[:phases.index(ph)])
            ph.groups = 1
            if ph.kind == "dense":
                if ph.tile is not None:
                    ph.parts = [(tile_in, KC, zt_ps)]
                else:
                    ph.parts = [(gathered, KC, zt_ps)]
                if ph.attr:
                    ph.parts = [(gathered, KC, zt_ps), (tile_in, KC, agg_ps), (attr, 1, at_ps)]
                ph.groups = len(ph.parts)
                ph.hi, ph.lo = (e_hi, e_lo) if ph.wide else (zt_hi, zt_lo)
                ph.wh, ph.wl = (w1_hi, w1_lo) if ph.wide else (w_hi, w_lo)
                ph.chunks = sum(c for _, c, _ in ph.parts)
                count(ph, "w_loaded", 16 * (1 if not ph.wide else 2))
                count(ph, "rows_loaded", 16 * sum(r is not None for r in (ph.bias, ph.gamma,
                                                                        ph.beta)))
                count(ph, "w_turned", KC if ph.turned else 0)
                count(ph, "w_hi_done", ph.chunks)
                count(ph, "w_lo_done", ph.chunks)
                if ph.agg:
                    count(ph, "selected", n)
                count(ph, "turned", n * ph.groups)
                count(ph, "hi_done", n * ph.groups)
                count(ph, "lo_done", n * ph.groups)
                count(ph, "mm_done", n)
                for i in range(len(ph.gathers)):
                    count(ph, f"idx_done{i}", n)
                    for s_ in range(T):
                        count(ph, f"gathered{i}_{s_}", 16 * (n // T))
                if ph.attr:
                    for s_ in range(T):
                        count(ph, f"attr{s_}", 16 * (n // T))
                e = ph.epi
                if e == "mish":
                    count(ph, "v_done", n)
                    count(ph, "clipped", n)
                    count(ph, "mish_act", 4 * n)
                    count(ph, "res_dve", n)
                elif e == "copy":
                    count(ph, "res_act", n)
                elif e == "bn":
                    count(ph, "kept_done", n)
                    count(ph, "square_done", n)
                    count(ph, "sum_done", n + 1)
                    count(ph, "sq_done", n + 1)
                elif e == "gcn":
                    count(ph, "v_done", n)
                    count(ph, "res_act", n)
                elif e == "gcn_last":
                    count(ph, "side_done", n)
                    count(ph, "x_done", n)
                    count(ph, "res_act", n)
                elif e == "norm2":
                    count(ph, "side_done", 2 * n)
                    count(ph, "v_done", n)
                    count(ph, "normed", n)
                    count(ph, "scaled", n)
                    count(ph, "x_done", n)
                    count(ph, "res_act", n)
                elif e == "sage":
                    count(ph, "v_done", 2 * n)
                    count(ph, "res_dve", n)
                if e in ("gcn_last", "norm2"):
                    for k in ((0, 1) if e == "norm2" else (1,)):
                        count(ph, f"stats{k}", n)
                        count(ph, f"moments{k}", n)
                        count(ph, f"ln_ready{k}", (4 if k == 1 and e == "norm2" else 3) * n)
            if ph.kind == "norm":
                count(ph, "stats1", n)
                count(ph, "moments1", n)
                count(ph, "ln_ready1", 3 * n)
                count(ph, "res_act", n)
            if ph.kind == "apply":
                count(ph, "rows_loaded", 48)
                count(ph, "totals_done", 2)
                count(ph, "bn_dve", BN_STEPS)
                count(ph, "bn_act", 2)
                count(ph, "mul_done", n)
                count(ph, "add_done", n)
                count(ph, "res_act", n)
                if ph.last:
                    count(ph, "x_done", n)
                    count(ph, "stats1", n)
                    count(ph, "moments1", n)
                    count(ph, "ln_ready1", 4 * n)
            def loads(what, on):
                for s_ in range(ring(what)):
                    if on:
                        count(ph, f"{what}{s_}", 16 * (n // ring(what)))
            ph.loads_x = ph.kind == "norm" or (ph.kind == "dense" and ph.epi == "norm2")
            loads("loaded", ph.kind == "dense" and ph.tile is not None)
            loads("side_a", (ph.kind == "dense" and len(ph.side) > 0) or (ph.kind == "apply" and ph.last))
            if ph.loads_x:
                for s_ in range(U):
                    count(ph, f"x_loaded{s_}",
                          sum(16 for t in range(s_, n, U) if t < full_nt or (t == full_nt and rest_n)))
            loads("x_stored", ph.x_out is not None and (ph.kind == "dense" or ph.last))
            if ph.kind == "dense" and ph.epi == "sage":
                for s_ in range(U):
                    count(ph, f"stored{s_}",
                          sum(16 for t in range(s_, n, U) if t < full_nt or (t == full_nt and rest_n)))
            else:
                loads("stored", ph.out is not None)

        def hold(eng, step):
            if not step.fixed:
                eng.sem_inc(held[id(eng)], 1)

        def slot_wait(eng, ph, name, step, ahead_of=0):
            r = ring(name)
            m = ph.m[f"{name}{step.lane % r}"]
            eng.wait_ge(m.sem, m.at(16 * (step.group * (U // r) + step.lane // r + 1 - ahead_of // r)))
            if eng is nc.gpsimd:
                hold(eng, step)

        def all_stored(eng, ph):
            for name in ("stored", "x_stored"):
                for s_ in range(U):
                    if f"{name}{s_}" in ph.m:
                        m = ph.m[f"{name}{s_}"]
                        total = m.base + 16 * (ph.n // U)
                        if ph.kind == "dense" and ph.epi == "sage":
                            total = m.base + sum(16 for t in range(s_, ph.n, U)
                                                 if t < full_nt or (t == full_nt and rest_n))
                        eng.wait_ge(m.sem, total)

        def wait(eng, ph, name, n):
            m = ph.m[name]
            eng.wait_ge(m.sem, m.at(n))

        def rows(t_, step):
            return t_[bass.ds(step.index * P, P), :]

        def bcast(row):
            return row.rearrange("(o d) -> o d", o=1).to_broadcast([P, row.shape[0]])

        n_grp = 5
        assert ET % (n_grp * U) == 0 and n_grp * NT <= 512 and NT % U == 0
        of_tile = sb("of_tile", [P, ET, NT], BF16)
        earlier = sb("earlier", [P, ET, NT], BF16)
        of_node = sb("of_node", [P, ET, P], BF16)
        before_me = sb("before_me", [P, P], BF16)
        ones_bf = sb("ones_bf", [P, P], BF16)
        ranked = sb("ranked", [P, T, n_grp, NT])
        lane = sb("lane", [P, 1], I32)
        lane_f = sb("lane_f", [P, 1])
        row_i = sb("row_i", [P, P], I32)
        tile_i = sb("tile_i", [P, ET], I32)
        tile_f = sb("tile_f", [P, ET])
        node_i = sb("node_i", [P, ET], I32)
        node_f = sb("node_f", [P, ET])
        rank = sb("rank", [P, ET])
        over = sb("over", [P, ET])
        position = sb("position", [P, ET], I32)
        payload = sb("payload", [P, ET, 4], I32)
        pay_now = sb("pay_now", [P, U, 4], I32)
        at_now = sb("at_now", [P, U], I32)
        degree = sb("degree", [P, NT])
        deg1 = sb("deg1", [P, NT])
        empty = sb("empty", [P, NT, 4], I32)
        slots = sb("slots", [P, NT, 4], I32)
        node_id = sb("node_id", [P, NT], I32)
        node_id_f = sb("node_id_f", [P, NT])
        real_f = sb("real_f", [P, NT])
        crowded_f = sb("crowded_f", [P, 1])
        many = sb("many", [P, NT])
        slot_f = sb("slot_f", [P, 2, NT])
        spill_f = sb("spill_f", [P, 2, NT])
        last_sum = sb("last_sum", [P, NT], BF16)
        counted = sb("counted", [P, NT])
        s_memset, s_const, s_cols, s_consts = sem("s_memset"), sem("s_const"), sem("s_cols"), sem("s_consts")
        s_prep, s_ranks, s_rank, s_pos = sem("s_prep"), sem("s_ranks"), sem("s_rank"), sem("s_pos")
        s_count, s_pay, s_put = sem("s_count"), sem("s_pay"), [sem(f"s_put{i}") for i in range(U)]
        s_empty, s_slots, s_table, s_dinv, s_inv = (sem("s_empty"), sem("s_slots"), sem("s_table"), sem("s_dinv"),
                                                    sem("s_inv"))

        def setup_sync(sp):
            sp.wait_ge(s_memset, 2)
            for col, name in ((src_col, "src"), (dst_col, "dst")):
                sp.dma_start(col[0:EP, :], a[name].rearrange("(p k) -> p k", k=ET)).then_inc(s_cols, 16)
            sp.wait_ge(s_memset, 5)
            sp.wait_ge(s_const, 14)
            sp.dma_start(slots_dram.rearrange("(a p) c -> p a c", p=P), empty[:, :, :]).then_inc(s_empty, 16)

        def table_sync(sp):
            for s_ in range(U):
                sp.wait_ge(s_put[s_], 16 * (ET // U))
            sp.dma_start(slots[:, :, :], slots_dram.rearrange("(a p) c -> p a c", p=P)).then_inc(s_slots, 16)

        def setup_pool(pool):
            pool.memset(src_col[:, :], FAR).then_inc(s_memset, 1)
            pool.memset(dst_col[:, :], FAR).then_inc(s_memset, 1)
            pool.memset(empty[:, :, 0:2], FAR).then_inc(s_memset, 1)
            pool.memset(empty[:, :, 2:3], 2 * P).then_inc(s_memset, 1)
            pool.memset(empty[:, :, 3:4], 0).then_inc(s_memset, 1)
            pool.iota(lane[:, :], pattern=[[0, 1]], base=0, channel_multiplier=1).then_inc(s_const, 1)
            pool.iota(row_i[:, :], pattern=[[1, P]], base=0, channel_multiplier=0).then_inc(s_const, 1)
            pool.iota(edge_id[:, :], pattern=[[P, ET]], base=0, channel_multiplier=1).then_inc(s_const, 1)
            pool.iota(node_id[:, :], pattern=[[P, NT]], base=0, channel_multiplier=1).then_inc(s_const, 1)
            pool.memset(minus_half[:, :], -0.5).then_inc(s_const, 1)
            pool.memset(ones_bf[:, :], 1.0).then_inc(s_const, 1)
            pool.memset(ones[:, :], 1.0).then_inc(s_const, 1)
            pool.memset(gathered[:, :, :], 0.0).then_inc(s_const, 1)
            pool.memset(tile_in[:, :, :], 0.0).then_inc(s_const, 1)
            pool.memset(attr[:, :, :], 0.0).then_inc(s_const, 1)
            pool.memset(w_raw[:, 2 * KC, :], 0.0).then_inc(s_const, 1)
            pool.memset(side_b[:, :, :], 0.0).then_inc(s_const, 1)
            pool.memset(side_a[:, :, :], 0.0).then_inc(s_const, 1)
            pool.memset(half[:, :], 0.5).then_inc(s_const, 1)

        def scatter_pool(pool):
            pool.wait_ge(s_empty, 16)
            pool.wait_ge(s_pos, 9)

            def body(step):
                k = step.index
                if step.has(U):
                    pool.wait_ge(s_put[step.slot], 16 * step.group)
                    hold(pool, step)
                pool.tensor_copy(pay_now[:, step.slot, :], payload[:, bass.ds(k, 1), :]
                                 .rearrange("p o c -> p (o c)")).then_inc(s_pay, 1)
                pool.tensor_copy(at_now[:, step.slot:step.slot + 1], position[:, bass.ds(k, 1)]).then_inc(s_pay, 1)
                pool.wait_ge(s_pay, 2 * k + 2)
                hold(pool, step)
                pool.indirect_dma_start(slots_dram[:, :],
                                        bass.IndirectOffsetOnAxis(ap=at_now[:, step.slot:step.slot + 1], axis=0),
                                        pay_now[:, step.slot, :], None, bounds_check=NR - 1,
                                        oob_is_err=False).then_inc(s_put[step.slot], 16)
            steps(pool, ET, body, 0, 0)

        def dinv_pool(pool):
            pool.wait_ge(s_dinv, 1)
            pool.tensor_tensor(deg1[:, :], deg1[:, :], minus_half[:, :], ALU.pow).then_inc(s_inv, 1)

        def setup_vector(dve):
            dve.wait_ge(s_const, 14)
            dve.tensor_copy(lane_f[:, :], lane[:, :]).then_inc(s_consts, 1)
            dve.tensor_copy(iota_row[:, :], row_i[:, :]).then_inc(s_consts, 1)
            dve.tensor_copy(node_id_f[:, :], node_id[:, :]).then_inc(s_consts, 1)
            dve.memset(earlier[:, 0, :], 0.0).then_inc(s_consts, 1)
            dve.wait_ge(s_consts, 4)
            dve.tensor_scalar(ident[:, :], iota_row[:, :], lane_f[:, 0:1], None, ALU.is_equal).then_inc(s_consts, 1)
            dve.tensor_scalar(before_me[:, :], iota_row[:, :], lane_f[:, 0:1], None, ALU.is_gt).then_inc(s_consts, 1)
            dve.tensor_scalar(real_f[:, :], node_id_f[:, :], float(n_nodes), None, ALU.is_lt).then_inc(s_consts, 1)
            dve.memset(degree[:, :], 0.0).then_inc(s_consts, 1)
            dve.wait_ge(s_cols, 32)
            dve.tensor_scalar(tile_i[:, :], dst_col[:, :], 7, None, ALU.logical_shift_right).then_inc(s_pos, 1)
            dve.tensor_scalar(node_i[:, :], dst_col[:, :], P - 1, None, ALU.bitwise_and).then_inc(s_pos, 1)
            dve.wait_ge(s_pos, 2)
            dve.tensor_copy(tile_f[:, :], tile_i[:, :]).then_inc(s_pos, 1)
            dve.tensor_copy(node_f[:, :], node_i[:, :]).then_inc(s_pos, 1)
            dve.wait_ge(s_pos, 4)
            with dve.Fori(0, ET) as k:
                dve.tensor_scalar(of_tile[:, bass.ds(k, 1), :].rearrange("p o a -> p (o a)"), iota_row[:, 0:NT],
                                  tile_f[:, bass.ds(k, 1)], None, ALU.is_equal).then_inc(s_prep, 1)
                dve.tensor_scalar(of_node[:, bass.ds(k, 1), :].rearrange("p o a -> p (o a)"), iota_row[:, :],
                                  node_f[:, bass.ds(k, 1)], None, ALU.is_equal).then_inc(s_prep, 1)
            dve.wait_ge(s_prep, 2 * ET)
            with dve.Fori(1, ET) as k:
                dve.tensor_tensor(earlier[:, bass.ds(k, 1), :], earlier[:, bass.ds(k - 1, 1), :],
                                  of_tile[:, bass.ds(k - 1, 1), :], ALU.add).then_inc(s_prep, 1)
                dve.wait_ge(s_prep, k + 2 * ET)
            dve.tensor_tensor(last_sum[:, :], earlier[:, ET - 1, :], of_tile[:, ET - 1, :],
                              ALU.add).then_inc(s_prep, 1)

            dve.wait_ge(s_consts, 8)
            for g in range(ET // n_grp):
                s_ = g % T
                dve.wait_ge(s_ranks, g + 1)
                if g >= T:
                    dve.wait_ge(s_rank, 3 * (g - T) + 3)
                dve.tensor_tensor(ranked[:, s_, :, :].rearrange("p k a -> p (k a)"), y_ps[s_][:, 0:n_grp * NT],
                                  of_tile[:, bass.ds(g * n_grp, n_grp), :].rearrange("p k a -> p (k a)"),
                                  ALU.mult).then_inc(s_rank, 1)
                dve.tensor_tensor(degree[:, :], degree[:, :], agg_ps[s_][:, 0:NT], ALU.add).then_inc(s_rank, 1)
                dve.wait_ge(s_rank, 3 * g + 2)
                dve.tensor_reduce(rank[:, bass.ds(g * n_grp, n_grp)], ranked[:, s_, :, :],
                                  mybir.AxisListType.X, ALU.add).then_inc(s_rank, 1)
            dve.wait_ge(s_rank, 3 * ET // n_grp)
            dve.tensor_scalar(over[:, :], rank[:, :], float(P), float(FAR), ALU.is_ge, ALU.mult).then_inc(s_pos, 1)
            dve.scalar_tensor_tensor(out=rank[:, :], in0=tile_f[:, :], scalar=float(P), in1=rank[:, :],
                                     op0=ALU.mult, op1=ALU.add).then_inc(s_pos, 1)
            dve.wait_ge(s_pos, 6)
            dve.tensor_tensor(position[:, :], rank[:, :], over[:, :], ALU.add).then_inc(s_pos, 1)
            dve.tensor_copy(payload[:, :, 0], src_col[:, :]).then_inc(s_pos, 1)
            dve.tensor_copy(payload[:, :, 1], edge_id[:, :])
            dve.tensor_copy(payload[:, :, 2], node_i[:, :])
            dve.tensor_copy(payload[:, :, 3], node_i[:, :]).then_inc(s_pos, 1)
            dve.tensor_scalar(deg1[:, :], degree[:, :], 1.0, None, ALU.add).then_inc(s_dinv, 1)
            dve.tensor_scalar(rdeg[:, :], degree[:, :], 1.0, None, ALU.max).then_inc(s_dinv, 1)
            dve.wait_ge(s_dinv, 2)
            dve.reciprocal(rdeg[:, :], rdeg[:, :]).then_inc(s_dinv, 1)
            dve.wait_ge(s_inv, 1)
            dve.tensor_tensor(dinv[:, :], deg1[:, :], real_f[:, :], ALU.mult).then_inc(s_dinv, 1)
            dve.wait_ge(s_count, 1)
            dve.tensor_scalar(many[:, :], zt_ps[0][:, 0:NT], float(P), None, ALU.is_gt).then_inc(s_dinv, 1)

        def table_vector(dve):
            dve.wait_ge(s_slots, 16)
            dve.wait_ge(s_dinv, 5)
            dve.tensor_copy(slot_f[:, 0, :], slots[:, :, 0]).then_inc(s_table, 1)
            dve.tensor_copy(slot_f[:, 1, :], slots[:, :, 1]).then_inc(s_table, 1)
            dve.tensor_copy(slot_node[:, :], slots[:, :, 2]).then_inc(s_table, 1)
            dve.tensor_scalar(counted[:, :], node_id_f[:, :], -float(FAR), None, ALU.add).then_inc(s_table, 1)
            dve.wait_ge(s_table, 4)
            for i in range(2):
                dve.tensor_scalar(spill_f[:, i, :], slot_f[:, i, :], -1.0, float(FAR), ALU.mult, ALU.add)\
                    .then_inc(s_table, 1)
            dve.tensor_tensor(counted[:, :], counted[:, :], many[:, :], ALU.mult).then_inc(s_table, 1)
            dve.wait_ge(s_table, 7)
            dve.tensor_scalar(spill_row[:, :], counted[:, :], float(FAR), None, ALU.add).then_inc(s_table, 1)
            for i in range(2):
                dve.tensor_tensor(spill_f[:, i, :], spill_f[:, i, :], many[:, :], ALU.mult).then_inc(s_table, 1)
            dve.wait_ge(s_table, 10)
            dve.tensor_tensor(slot_src[:, :], slot_f[:, 0, :], spill_f[:, 0, :], ALU.add).then_inc(s_table, 1)
            dve.tensor_tensor(slot_edge[:, :], slot_f[:, 1, :], spill_f[:, 1, :], ALU.add).then_inc(s_table, 1)
            dve.tensor_scalar(counted[:, :], slot_node[:, :], lane_f[:, 0:1], -1.0, ALU.subtract,
                              ALU.mult).then_inc(s_table, 1)
            dve.wait_ge(s_table, 13)
            dve.tensor_tensor(counted[:, :], counted[:, :], many[:, :], ALU.mult).then_inc(s_table, 1)
            dve.wait_ge(s_table, 14)
            dve.tensor_tensor(slot_node[:, :], slot_node[:, :], counted[:, :], ALU.add).then_inc(s_table, 1)
            dve.tensor_reduce(crowded_f[:, :], many[:, :], mybir.AxisListType.X, ALU.max).then_inc(s_table, 1)
            dve.tensor_copy(dst_f[:, :], dst_col[:, :]).then_inc(s_table, 1)
            dve.wait_ge(s_table, 17)
            dve.tensor_copy(crowded[:, :], crowded_f[:, :]).then_inc(s_table, 1)

        def setup_tensor(pe):
            pe.wait_ge(s_consts, 6)
            pe.wait_ge(s_prep, 3 * ET)
            for g in range(ET // n_grp):
                if g >= T:
                    pe.wait_ge(s_rank, 3 * (g - T) + 3)
                for i in range(n_grp):
                    k = g * n_grp + i
                    o = y_ps[g % T][:, i * NT:(i + 1) * NT]
                    pe.matmul(o, before_me[:, :], of_tile[:, k, :], start=True, stop=False)
                    pe.matmul(o, ones_bf[:, :], earlier[:, k, :], start=False, stop=True)
                for i in range(n_grp):
                    k = g * n_grp + i
                    last = pe.matmul(agg_ps[g % T][:, 0:NT], of_node[:, k, :], of_tile[:, k, :],
                                     start=(i == 0), stop=(i == n_grp - 1))
                last.then_inc(s_ranks, 1)
            pe.matmul(zt_ps[0][:, 0:NT], ones_bf[:, :], last_sum[:, :], start=True, stop=True).then_inc(s_count, 1)

        s_zeroed, s_sp_rows, s_sp_put, s_sp_add = sem("spill_zeroed"), sem("spill_rows"), sem("spill_put"), \
            sem("spill_slots")
        s_sp_pool, s_sp_dve, s_sp_pe, s_sp_idx = sem("spill_pool"), sem("spill_dve"), sem("spill_pe"), \
            sem("spill_idx")

        def load_crowded(eng):
            reg = eng.alloc_register("crowded")
            eng.wait_ge(s_table, 18)
            eng.reg_load(reg, crowded[0:1, 0:1])
            return reg

        def spill_pool(pool, ph, is_crowded):
            table, column = ph.gathers[0][0], (src_col if ph.agg == "pre" else edge_id)
            sp = ph.spills
            with pool.If_ne(is_crowded, 0):
                pool.memset(gathered[:, :, :], 0.0).then_inc(s_sp_pool, 1)
                done = sp * (1 + 2 * ET) + 1
                pool.wait_ge(s_sp_pool, done)
                with pool.Fori(0, NT) as t:
                    pool.dma_start(spill[bass.ds(t * P, P), :], gathered[:, 0, :]).then_inc(s_zeroed, 16)
                pool.wait_ge(s_zeroed, 16 * NT * (sp + 1))
                with pool.Fori(0, ET) as k:
                    pool.tensor_copy(idx_spill[:, 0:1], column[:, bass.ds(k, 1)]).then_inc(s_sp_pool, 1)
                    pool.tensor_copy(idx_spill[:, 1:2], dst_col[:, bass.ds(k, 1)]).then_inc(s_sp_pool, 1)
                    pool.wait_ge(s_sp_pool, 2 * k + (done + 2))
                    pool.sem_inc(held[id(pool)], 1)
                    pool.indirect_dma_start(gathered[:, 0, :], None, table[:, :],
                                            bass.IndirectOffsetOnAxis(ap=idx_spill[:, 0:1], axis=0),
                                            bounds_check=table.shape[0] - 1, oob_is_err=False)\
                        .then_inc(s_sp_rows, 16)
                    pool.indirect_dma_start(gathered[:, 1, :], None, spill[:, :],
                                            bass.IndirectOffsetOnAxis(ap=idx_spill[:, 1:2], axis=0),
                                            bounds_check=NR - 1, oob_is_err=False).then_inc(s_sp_rows, 16)
                    pool.wait_ge(s_sp_dve, 3 * ET * sp + 3 * k + 3)
                    pool.sem_inc(held[id(pool)], 1)
                    pool.indirect_dma_start(spill[:, :], bass.IndirectOffsetOnAxis(ap=idx_spill[:, 1:2], axis=0),
                                            gathered[:, 1, :], None, bounds_check=NR - 1,
                                            oob_is_err=False).then_inc(s_sp_put, 16)
                    pool.wait_ge(s_sp_put, 16 * ET * sp + 16 * k + 16)
                    pool.sem_inc(held[id(pool)], 1)

        def spill_vector(dve, ph, is_crowded):
            sp = ph.spills
            with dve.If_ne(is_crowded, 0):
                with dve.Fori(0, ET) as k:
                    target, done = dst_f[:, bass.ds(k, 1)], 3 * ET * sp
                    dve.wait_ge(s_sp_rows, 32 * ET * sp + 32 * k + 32)
                    dve.tensor_scalar(select[:, 1, :], ones[:, :], target, None, ALU.mult).then_inc(s_sp_dve, 1)
                    dve.wait_ge(s_sp_pe, 2 * ET * sp + 2 * k + 1)
                    dve.tensor_scalar(select[:, 0, :], at_ps[0][:, 0:P], target, None, ALU.is_equal)\
                        .then_inc(s_sp_dve, 1)
                    dve.wait_ge(s_sp_pe, 2 * ET * sp + 2 * k + 2)
                    dve.tensor_tensor(gathered[:, 1, :], gathered[:, 1, :], at_ps[1][:, :], ALU.add)\
                        .then_inc(s_sp_dve, 1)

        def spill_tensor(pe, ph, is_crowded):
            sp = ph.spills
            with pe.If_ne(is_crowded, 0):
                with pe.Fori(0, ET) as k:
                    pe.wait_ge(s_sp_dve, 3 * ET * sp + 3 * k + 1)
                    pe.matmul(at_ps[0][:, 0:P], select[:, 1, :], ident[:, :], start=True, stop=True)\
                        .then_inc(s_sp_pe, 1)
                    pe.wait_ge(s_sp_dve, 3 * ET * sp + 3 * k + 2)
                    pe.matmul(at_ps[1][:, :], select[:, 0, :], gathered[:, 0, :], start=True, stop=True)\
                        .then_inc(s_sp_pe, 1)

        def spill_slots(pool, ph, step, is_crowded):
            at = ph.spills * NT + step.index + 1
            with pool.If_ne(is_crowded, 0):
                pool.tensor_copy(idx_spill[:, 0:1], spill_row[:, bass.ds(step.index, 1)]).then_inc(s_sp_idx, 1)
                pool.wait_ge(s_sp_idx, at)
                hold(pool, step)
                pool.indirect_dma_start(gathered[:, step.pair, :], None, spill[:, :],
                                        bass.IndirectOffsetOnAxis(ap=idx_spill[:, 0:1], axis=0),
                                        bounds_check=NR - 1, oob_is_err=False).then_inc(s_sp_add, 16)
                pool.wait_ge(s_sp_add, 16 * at)
                hold(pool, step)

        def part_rows(t):
            return P if t < full_nt else (rest_n if t == full_nt else 0)

        def lag(ph, what):
            kind = ph.epi if ph.kind == "dense" else ph.kind
            return {("mish", "res"): 2, ("norm2", "x_out"): 2, ("norm2", "res"): 3, ("gcn_last", "res"): 2,
                    ("norm", "res"): 1, ("apply", "x_out"): 1, ("apply", "res"): 3 if ph.last else 0}\
                .get((kind, what), 0)

        def phase_sync(sp, ph):
            prev = ph.before
            if ph.kind == "dense":
                if ph.raw is w_raw_bn or prev.kind != "dense":
                    all_stored(sp, prev)
                else:
                    wait(sp, prev, "w_hi_done", prev.chunks)
                    wait(sp, prev, "w_lo_done", prev.chunks)
                if ph.wide:
                    sp.wait_ge(s_const, 14)
                    sp.dma_start(w_raw[:, 0:2 * KC, :], ph.w[0:2 * D, :].rearrange("(c p) d -> p c d", p=P))\
                        .then_inc(ph.m["w_loaded"].sem, 16)
                    sp.dma_start(w_raw[0:DE, 2 * KC, :], ph.w[2 * D:2 * D + DE, :])\
                        .then_inc(ph.m["w_loaded"].sem, 16)
                else:
                    sp.dma_start(ph.raw[:, 0:KC, :], ph.w.rearrange("(c p) d -> p c d", p=P))\
                        .then_inc(ph.m["w_loaded"].sem, 16)
            if prev is not None:
                all_stored(sp, prev)
                if prev.kind == "dense" and prev.epi == "bn":
                    wait(sp, prev, "mm_done", prev.n)
                    wait(sp, prev, "sum_done", prev.n + 1)
                    wait(sp, prev, "sq_done", prev.n + 1)
            if ph.kind != "norm":
                for row, buf in ((ph.bias, bias), (ph.gamma, gamma_row),
                                 (ph.beta, beta_row)):
                    if ph.kind == "apply":
                        buf = {id(bias): gathered[:, 0, :], id(gamma_row): gathered[:, 1, :],
                               id(beta_row): square[:, 0, :]}[id(buf)]
                    else:
                        buf = buf[:, :]
                    if row is not None:
                        sp.dma_start(buf, bcast(row)).then_inc(ph.m["rows_loaded"].sem, 16)
            if ph.kind == "dense" and ph.raw is w_raw_bn:
                wait(sp, ph, "w_turned", KC)

            def inc(name, step):
                return ph.m[f"{name}{step.lane % ring(name)}"].sem

            def load_x(step, buf):
                r = part_rows(step.index) if step.fixed else P
                if r == P:
                    sp.dma_start(buf[:, step.slot, :], rows(x, step)).then_inc(inc("x_loaded", step), 16)
                elif r:
                    sp.dma_start(buf[0:r, step.slot, :], x[full_nt * P:n_nodes, :])\
                        .then_inc(inc("x_loaded", step), 16)

            def body(step):
                far, near = step.tile(2), step.tile(1)
                if ph.kind == "dense" and ph.tile is not None and far.exists:
                    if far.has(T):
                        wait(sp, ph, "turned", ph.groups * (far.index - T + 1))
                    sp.dma_start(tile_in[:, far.pair, :], rows(ph.tile, far)).then_inc(inc("loaded", far), 16)
                if ph.kind == "dense" and ph.attr and far.exists:
                    if far.has(T):
                        wait(sp, ph, "turned", ph.groups * (far.index - T + 1))
                    sp.dma_start(attr[0:EP, far.pair, 0:DE],
                                 a["edge_attr_64"].rearrange("(p k) d -> p k d", k=ET)[:, bass.ds(far.index, 1), :]
                                 .rearrange("p o d -> p (o d)")).then_inc(inc("attr", far), 16)
                if ph.kind == "norm" and far.exists:
                    if far.has(U):
                        wait(sp, ph, "res_act", far.index - U + 1)
                    load_x(far, side_a)
                if ph.kind == "dense" and ph.side and near.exists:
                    name = {"norm2": "v_done", "gcn_last": "x_done", "sage": "res_dve"}[ph.epi]
                    if near.has(U):
                        wait(sp, ph, name, near.index - U + 1)
                    sp.dma_start(side_a[:, near.slot, :], rows(ph.side[0], near)).then_inc(inc("side_a", near), 16)
                    if ph.epi == "norm2":
                        if near.has(U):
                            wait(sp, ph, "x_done", near.index - U + 1)
                        load_x(near, side_b)
                if ph.kind == "apply" and ph.last and far.exists:
                    if far.has(U):
                        wait(sp, ph, "x_done", far.index - U + 1)
                    elif far.fixed and far.index == 0:
                        wait(sp, ph, "bn_dve", BN_STEPS)
                    sp.dma_start(x_slots[far.slot], rows(ph.x_in, far)).then_inc(inc("side_a", far), 16)
                x_late, late = step.tile(-lag(ph, "x_out") - 1), step.tile(-lag(ph, "res") - 1)
                if ph.x_out is not None and (ph.kind == "dense" or ph.last) and x_late.exists:
                    wait(sp, ph, "x_done", x_late.index + 1)
                    buf = x_out[:, x_late.slot, :] if ph.kind == "dense" else \
                        kept[:, bass.ds(x_late.index, 1), :].rearrange("p o d -> p (o d)")
                    sp.dma_start(rows(ph.x_out, x_late), buf).then_inc(inc("x_stored", x_late), 16)
                if ph.out is not None:
                    if late.exists:
                        which = "res_dve" if ph.kind == "dense" and ph.epi in ("mish", "sage") else "res_act"
                        r = part_rows(late.index) if late.fixed and ph.out is out else P
                        if r:
                            wait(sp, ph, which, late.index + 1)
                        if ph.kind == "apply":
                            buf = (normed_out[:, late.slot, :] if ph.last else
                                   kept[:, bass.ds(late.index, 1), :].rearrange("p o d -> p (o d)"))
                        else:
                            buf = res[:, late.slot, :]
                        if r == P:
                            sp.dma_start(rows(ph.out, late), buf).then_inc(inc("stored", late), 16)
                        elif r:
                            sp.dma_start(out[full_nt * P:n_nodes, :], buf[0:r, :]).then_inc(inc("stored", late), 16)
            steps(sp, ph.n, body, 2, 4)

        def gather(pool, ph, i, step, is_crowded):
            table, column = ph.gathers[i]
            dest = (gathered, tile_in)[i]
            m = ph.m[f"idx_done{i}"]
            if ph.agg:
                spill_slots(pool, ph, step, is_crowded)
            pool.tensor_copy(idx[:, i, step.pair:step.pair + 1], column[:, bass.ds(step.index, 1)]).then_inc(m.sem, 1)
            pool.wait_ge(m.sem, m.at(step.index + 1))
            hold(pool, step)
            pool.indirect_dma_start(dest[:, step.pair, :], None, table[:, :],
                                    bass.IndirectOffsetOnAxis(ap=idx[:, i, step.pair:step.pair + 1], axis=0),
                                    bounds_check=table.shape[0] - 1, oob_is_err=False)\
                .then_inc(ph.m[f"gathered{i}_{step.pair}"].sem, 16)

        def ln_pool(pool, ph, k, step, scaled):
            m, s_, mv = ph.m[f"ln_ready{k}"], ln_sc[:, k, step.slot, :], ln_mv[:, k, step.slot, :]
            per = 4 if scaled else 3
            done = step.index * per
            wait(pool, ph, f"moments{k}", step.index + 1)
            hold(pool, step)
            pool.tensor_scalar(s_[:, 0:1], mv[:, 1:2], 1.0, EPS, ALU.mult, ALU.add).then_inc(m.sem, 1)
            pool.wait_ge(m.sem, m.at(done + 1))
            if scaled:
                pool.tensor_tensor(s_[:, 1:2], s_[:, 0:1], minus_half[:, 0:1], ALU.pow).then_inc(m.sem, 1)
                pool.wait_ge(m.sem, m.at(done + 2))
                pool.tensor_tensor(s_[:, 2:3], s_[:, 1:2], dinv[:, bass.ds(step.index, 1)], ALU.mult)\
                    .then_inc(m.sem, 1)
            else:
                pool.tensor_tensor(s_[:, 2:3], s_[:, 0:1], minus_half[:, 0:1], ALU.pow).then_inc(m.sem, 1)
            pool.wait_ge(m.sem, m.at(done + per - 1))
            hold(pool, step)
            pool.tensor_scalar(s_[:, 3:4], mv[:, 0:1], s_[:, 2:3], -1.0, ALU.mult, ALU.mult).then_inc(m.sem, 1)

        def ln_scaled(ph, k):
            return ph.kind == "apply" or (ph.kind == "dense" and ph.epi == "norm2" and k == 1)

        def phase_pool(pool, ph, is_crowded):
            if ph.kind == "dense":
                if ph.epi == "bn":
                    pool.memset(bn_sum[:, :], 0.0).then_inc(ph.m["sum_done"].sem, 1)
                if ph.gathers:
                    all_stored(pool, ph.before)
                if ph.turned:
                    wait(pool, ph, "w_turned", KC)
                if ph.agg:
                    spill_pool(pool, ph, is_crowded)
                if ph.epi in ("norm2", "gcn_last"):
                    wait(pool, ph, "rows_loaded", 48 if ph.epi == "norm2" else 16)
            if ph.kind == "apply":
                wait(pool, ph, "bn_dve", BN_STEPS)

            def body(step):
                if ph.kind == "dense":
                    ahead, before = step.tile(2), step.tile(-1)
                    if ahead.exists:
                        for i in range(len(ph.gathers)):
                            if ahead.has(T):
                                if ph.agg in ("post", "sep"):
                                    wait(pool, ph, "mm_done", ahead.index - T + 1)
                                else:
                                    wait(pool, ph, "turned", ph.groups * (ahead.index - T + 1))
                                hold(pool, ahead)
                            gather(pool, ph, i, ahead, is_crowded)
                    if ph.epi == "mish" and step.exists:
                        wait(pool, ph, "v_done", step.index + 1)
                        if step.has(U):
                            wait(pool, ph, "mish_act", 4 * (step.index - U) + 1)
                        hold(pool, step)
                        pool.tensor_scalar(c_buf[:, step.slot, :], v_buf[:, step.slot, :], EXP_MAX, -80.0,
                                           ALU.min, ALU.max).then_inc(ph.m["clipped"].sem, 1)
                    if ph.epi == "bn" and before.exists:
                        wait(pool, ph, "kept_done", before.index + 1)
                        wait(pool, ph, "sum_done", before.index + 1)
                        pool.tensor_tensor(bn_sum[:, :], bn_sum[:, :],
                                           kept[:, bass.ds(before.index, 1), :].rearrange("p o d -> p (o d)"),
                                           ALU.add).then_inc(ph.m["sum_done"].sem, 1)
                    near = step.tile(1)
                    if ph.epi in ("norm2", "gcn_last") and near.exists:
                        slot_wait(pool, ph, "side_a", near)
                        pool.tensor_tensor(side_a[:, near.slot, :], side_a[:, near.slot, :], bias[:, :], ALU.add)\
                            .then_inc(ph.m["side_done"].sem, 1)
                    if ph.epi == "norm2":
                        if near.exists:
                            if not near.fixed or part_rows(near.index):
                                slot_wait(pool, ph, "x_loaded", near)
                            pool.tensor_tensor(side_b[:, near.slot, :], side_b[:, near.slot, :], beta_row[:, :],
                                               ALU.add).then_inc(ph.m["side_done"].sem, 1)
                        if step.exists:
                            if step.has(U):
                                wait(pool, ph, "normed", step.index - U + 1)
                            ln_pool(pool, ph, 0, step, False)
                        older = step.tile(-2)
                        if older.exists:
                            if older.has(U):
                                wait(pool, ph, "res_act", older.index - U + 1)
                            ln_pool(pool, ph, 1, older, True)
                    if ph.epi == "gcn_last" and before.exists:
                        if before.has(U):
                            wait(pool, ph, "res_act", before.index - U + 1)
                        ln_pool(pool, ph, 1, before, False)
                elif ph.kind == "norm":
                    if step.exists:
                        if step.has(U):
                            wait(pool, ph, "res_act", step.index - U + 1)
                        ln_pool(pool, ph, 1, step, False)
                elif ph.kind == "apply":
                    if step.exists:
                        wait(pool, ph, "mul_done", step.index + 1)
                        k_ = kept[:, bass.ds(step.index, 1), :].rearrange("p o d -> p (o d)")
                        pool.tensor_tensor(k_, k_, bn_sq[:, :], ALU.add).then_inc(ph.m["add_done"].sem, 1)
                    if ph.last and step.tile(-2).exists:
                        older = step.tile(-2)
                        if older.has(U):
                            wait(pool, ph, "res_act", older.index - U + 1)
                        ln_pool(pool, ph, 1, older, True)
            steps(pool, ph.n, body, 2, 4)

        def phase_tensor(pe, ph, is_crowded):
            if ph.kind == "norm":
                return
            if ph.kind == "apply":
                bn = ph.before
                wait(pe, bn, "sum_done", ph.n + 1)
                pe.matmul(y_ps[0][:, :], ones[:, :], bn_sum[:, :], start=True, stop=True)\
                    .then_inc(ph.m["totals_done"].sem, 1)
                wait(pe, bn, "sq_done", ph.n + 1)
                pe.matmul(y_ps[1][:, :], ones[:, :], bn_sq[:, :], start=True, stop=True)\
                    .then_inc(ph.m["totals_done"].sem, 1)
                return
            G = ph.groups
            if ph.turned:
                wait(pe, ph, "w_loaded", 16)
                for c in range(KC):
                    if c >= T:
                        wait(pe, ph, "w_lo_done", c - T + 1)
                    for o in range(KC):
                        last = pe.transpose(zt_ps[c % T][:, o * P:(o + 1) * P],
                                            ph.raw[:, o, c * P:(c + 1) * P], ident[:, :])
                    last.then_inc(ph.m["w_turned"].sem, 1)
            wait(pe, ph, "w_lo_done", ph.chunks)
            if ph.agg:
                spill_tensor(pe, ph, is_crowded)

            def turn(step):
                for g, (buf, chunks, ps) in enumerate(ph.parts):
                    if step.has(T):
                        wait(pe, ph, "lo_done", G * (step.index - T) + g + 1)
                    if buf is attr:
                        slot_wait(pe, ph, "attr", step)
                    elif ph.tile is not None:
                        slot_wait(pe, ph, "loaded", step)
                    else:
                        slot_wait(pe, ph, f"gathered{g}_", step)
                    if ph.agg == "pre":
                        slot_wait(pe, ph, "gathered0_", step)
                        wait(pe, ph, "selected", step.index + 1)
                    for c in range(chunks):
                        o = ps[step.pair][:, c * P:(c + 1) * P]
                        piece = buf[:, step.pair, c * P:(c + 1) * P]
                        if ph.agg == "pre":
                            pe.matmul(o, piece, ident[:, :], is_transpose=True, start=True, stop=False)
                            last = pe.matmul(o, gathered[:, step.pair, c * P:(c + 1) * P], select[:, step.pair, :],
                                             start=False, stop=True)
                        else:
                            last = pe.transpose(o, piece, ident[:, :])
                    last.then_inc(ph.m["turned"].sem, 1)

            free = {"mish": ("v_done", 1), "copy": ("res_act", 1), "bn": ("square_done", 1), "gcn": ("v_done", 1),
                    "gcn_last": ("x_done", 1), "norm2": ("v_done", 1), "sage": ("v_done", 2)}[ph.epi]

            def body(step):
                near = step.tile(1)
                if near.exists:
                    turn(near)
                if not step.exists:
                    return
                wait(pe, ph, "lo_done", G * (step.index + 1))
                if step.has(T):
                    wait(pe, ph, free[0], free[1] * (step.index - T + 1))
                y, i = y_ps[step.pair][:, :], step.pair
                for c in range(ph.chunks):
                    hi, lo = ph.hi[:, i, c * P:(c + 1) * P], ph.lo[:, i, c * P:(c + 1) * P]
                    pe.matmul(y, lo, ph.wh[:, c, :], start=c == 0, stop=False)
                    pe.matmul(y, hi, ph.wl[:, c, :], start=False, stop=False)
                    last = pe.matmul(y, hi, ph.wh[:, c, :], start=False,
                                     stop=c == ph.chunks - 1 and ph.agg != "post")
                if ph.agg in ("post", "sep"):
                    slot_wait(pe, ph, "gathered0_", step)
                    wait(pe, ph, "selected", step.index + 1)
                    last = pe.matmul(y if ph.agg == "post" else agg_ps[i][:, :], select[:, i, :],
                                     gathered[:, i, :], start=ph.agg == "sep", stop=True)
                last.then_inc(ph.m["mm_done"].sem, 1)
            steps(pe, ph.n, body, 1, 0)

        def phase_scalar(act, ph):
            if ph.kind == "dense":
                if ph.before.kind == "dense":
                    wait(act, ph.before, "mm_done", ph.before.n)
                if not ph.turned:
                    wait(act, ph, "w_loaded", 16 * (2 if ph.wide else 1))
                for c in range(ph.chunks):
                    if ph.turned:
                        wait(act, ph, "w_turned", c + 1)
                    src = zt_ps[c % T][:, :] if ph.turned else ph.raw[:, c, :]
                    nc.scalar.activation(ph.wh[:, c, :], src, ACT.Copy).then_inc(ph.m["w_hi_done"].sem, 1)

            if ph.kind == "apply":
                wait(act, ph, "bn_dve", 4)
                nc.scalar.activation(square[:, 1, :], bn_sum[:, :], ACT.Ln).then_inc(ph.m["bn_act"].sem, 1)
                wait(act, ph, "bn_act", 1)
                nc.scalar.activation(square[:, 1, :], square[:, 1, :], ACT.Exp, scale=-0.5)\
                    .then_inc(ph.m["bn_act"].sem, 1)

            def body(step):
                near, before, older = step.tile(1), step.tile(-1), step.tile(-2)
                s_ = step.slot
                if ph.kind == "dense" and near.exists:
                    for g, (buf, chunks, ps) in enumerate(ph.parts):
                        wait(act, ph, "turned", ph.groups * near.index + g + 1)
                        if near.has(T):
                            wait(act, ph, "mm_done", near.index - T + 1)
                        at = g * KC * P
                        nc.scalar.activation(ph.hi[:, near.pair, at:at + chunks * P],
                                             ps[near.pair][:, 0:chunks * P], ACT.Copy)\
                            .then_inc(ph.m["hi_done"].sem, 1)
                if ph.kind == "dense" and ph.epi == "mish" and before.exists:
                    m, e, t = ph.m["mish_act"], e_buf[:, before.slot, :], before.index
                    wait(act, ph, "clipped", t + 1)
                    if before.has(U):
                        wait(act, ph, "res_dve", t - U + 1)
                    nc.scalar.activation(e, c_buf[:, before.slot, :], ACT.Exp).then_inc(m.sem, 1)
                    act.wait_ge(m.sem, m.at(4 * t + 1))
                    nc.scalar.activation(e, e, ACT.Square, bias=1.0).then_inc(m.sem, 1)
                    act.wait_ge(m.sem, m.at(4 * t + 2))
                    nc.scalar.activation(e, e, ACT.Ln, bias=half[:, 0:1], scale=0.5).then_inc(m.sem, 1)
                    act.wait_ge(m.sem, m.at(4 * t + 3))
                    nc.scalar.activation(e, e, ACT.Exp, scale=-1.0).then_inc(m.sem, 1)
                if ph.kind == "dense" and step.exists:
                    if ph.epi == "copy":
                        wait(act, ph, "mm_done", step.index + 1)
                        if step.has(U):
                            slot_wait(act, ph, "stored", step, U)
                        nc.scalar.activation(res[:, s_, :], y_ps[step.pair][:, :], ACT.Copy)\
                            .then_inc(ph.m["res_act"].sem, 1)
                    if ph.epi == "bn":
                        wait(act, ph, "mm_done", step.index + 1)
                        hold(act, step)
                        d = dinv[:, bass.ds(step.index, 1)]
                        nc.scalar.activation(kept[:, bass.ds(step.index, 1), :].rearrange("p o d -> p (o d)"),
                                             y_ps[step.pair][:, :], ACT.Identity, scale=d)\
                            .then_inc(ph.m["kept_done"].sem, 1)
                        if step.has(T):
                            wait(act, ph, "sq_done", step.index - T + 2)
                        hold(act, step)
                        nc.scalar.activation(square[:, step.pair, :], y_ps[step.pair][:, :], ACT.Square, scale=d)\
                            .then_inc(ph.m["square_done"].sem, 1)
                    if ph.epi == "gcn":
                        wait(act, ph, "v_done", step.index + 1)
                        if step.has(U):
                            slot_wait(act, ph, "stored", step, U)
                        hold(act, step)
                        nc.scalar.activation(res[:, s_, :], v_buf[:, s_, :], ACT.Relu,
                                             scale=dinv[:, bass.ds(step.index, 1)])\
                            .then_inc(ph.m["res_act"].sem, 1)
                if ph.kind == "dense" and ph.epi == "norm2" and before.exists:
                    wait(act, ph, "ln_ready0", 3 * (before.index + 1))
                    sc, v = ln_sc[:, 0, before.slot, :], v_buf[:, before.slot, :]
                    nc.scalar.activation(v, v, ACT.Identity, scale=sc[:, 2:3], bias=sc[:, 3:4])\
                        .then_inc(ph.m["normed"].sem, 1)

                def normed_relu(of, source, target):
                    wait(act, ph, "ln_ready1", (4 if ln_scaled(ph, 1) else 3) * (of.index + 1))
                    if of.has(U):
                        slot_wait(act, ph, "stored", of, U)
                    hold(act, of)
                    sc = ln_sc[:, 1, of.slot, :]
                    nc.scalar.activation(target, source, ACT.Relu, scale=sc[:, 2:3], bias=sc[:, 3:4])\
                        .then_inc(ph.m["res_act"].sem, 1)

                oldest = step.tile(-3)
                if ph.kind == "dense" and ph.epi == "norm2" and oldest.exists:
                    normed_relu(oldest, x_out[:, oldest.slot, :], res[:, oldest.slot, :])
                if ph.kind == "dense" and ph.epi == "gcn_last" and older.exists:
                    normed_relu(older, x_out[:, older.slot, :], res[:, older.slot, :])
                if ph.kind == "norm" and before.exists:
                    normed_relu(before, side_a[:, before.slot, :], res[:, before.slot, :])
                if ph.kind == "apply":
                    if not ph.last and step.exists:
                        k_ = kept[:, bass.ds(step.index, 1), :].rearrange("p o d -> p (o d)")
                        wait(act, ph, "add_done", step.index + 1)
                        hold(act, step)
                        nc.scalar.activation(k_, k_, ACT.Relu, scale=dinv[:, bass.ds(step.index, 1)])\
                            .then_inc(ph.m["res_act"].sem, 1)
                    if ph.last and oldest.exists:
                        k_ = kept[:, bass.ds(oldest.index, 1), :].rearrange("p o d -> p (o d)")
                        normed_relu(oldest, k_, normed_out[:, oldest.slot, :])
            steps(act, ph.n, body, 1, 3)

        def phase_vector(dve, ph, is_crowded):
            def moments(k, of, source):
                st, mv, own = ln_st[:, k, of.slot, :], ln_mv[:, k, of.slot, :], ph.m[f"stats{k}"]
                if of.has(U):
                    wait(dve, ph, f"moments{k}", of.index - U + 1)
                hold(dve, of)
                dve.bn_stats(st, source).then_inc(own.sem, 1)
                dve.wait_ge(own.sem, own.at(of.index + 1))
                if of.has(U):
                    wait(dve, ph, f"ln_ready{k}", (4 if ln_scaled(ph, k) else 3) * (of.index - U + 1))
                hold(dve, of)
                dve.bn_aggr(mv, st).then_inc(ph.m[f"moments{k}"].sem, 1)

            if ph.kind == "dense":
                if ph.before.kind == "dense":
                    wait(dve, ph.before, "mm_done", ph.before.n)
                for c in range(ph.chunks):
                    wait(dve, ph, "w_hi_done", c + 1)
                    src = zt_ps[c % T][:, :] if ph.turned else ph.raw[:, c, :]
                    dve.tensor_tensor(ph.wl[:, c, :], src, ph.wh[:, c, :].bitcast(F32), ALU.subtract)\
                        .then_inc(ph.m["w_lo_done"].sem, 1)
                if ph.epi == "bn":
                    dve.memset(bn_sq[:, :], 0.0).then_inc(ph.m["sq_done"].sem, 1)
                if ph.epi in ("mish", "gcn", "sage", "norm2"):
                    wait(dve, ph, "rows_loaded", 48 if ph.epi == "norm2" else 16)
            if ph.kind == "apply":
                b_row, g_row, beta_r = gathered[:, 0, :], gathered[:, 1, :], square[:, 0, :]
                mean, t1 = tile_in[:, 0, :], tile_in[:, 1, :]
                own = ph.m["bn_dve"]
                wait(dve, ph, "totals_done", 1)
                dve.tensor_scalar(mean, y_ps[0][:, :], 1.0 / n_nodes, None, ALU.mult).then_inc(own.sem, 1)
                wait(dve, ph, "bn_dve", 1)
                dve.tensor_tensor(t1, mean, mean, ALU.mult).then_inc(own.sem, 1)
                wait(dve, ph, "totals_done", 2)
                wait(dve, ph, "bn_dve", 2)
                dve.scalar_tensor_tensor(out=bn_sum[:, :], in0=y_ps[1][:, :], scalar=1.0 / n_nodes, in1=t1,
                                         op0=ALU.mult, op1=ALU.subtract).then_inc(own.sem, 1)
                wait(dve, ph, "bn_dve", 3)
                dve.tensor_scalar(bn_sum[:, :], bn_sum[:, :], 0.0, EPS, ALU.max, ALU.add).then_inc(own.sem, 1)
                r, inv = square[:, 1, :], ph.m["bn_dve"].sem
                wait(dve, ph, "bn_act", 2)
                dve.tensor_tensor(t1, r, r, ALU.mult).then_inc(inv, 1)
                wait(dve, ph, "bn_dve", 5)
                dve.tensor_tensor(t1, t1, bn_sum[:, :], ALU.mult).then_inc(inv, 1)
                wait(dve, ph, "bn_dve", 6)
                dve.tensor_scalar(t1, t1, -0.5, 1.5, ALU.mult, ALU.add).then_inc(inv, 1)
                wait(dve, ph, "bn_dve", 7)
                dve.tensor_tensor(r, r, t1, ALU.mult).then_inc(inv, 1)
                wait(dve, ph, "rows_loaded", 48)
                wait(dve, ph, "bn_dve", 8)
                dve.tensor_tensor(bn_sum[:, :], r, g_row, ALU.mult).then_inc(inv, 1)
                dve.tensor_tensor(mean, mean, b_row, ALU.add).then_inc(inv, 1)
                wait(dve, ph, "bn_dve", 10)
                dve.tensor_tensor(t1, b_row, mean, ALU.subtract).then_inc(inv, 1)
                wait(dve, ph, "bn_dve", 11)
                dve.tensor_tensor(t1, t1, bn_sum[:, :], ALU.mult).then_inc(inv, 1)
                wait(dve, ph, "bn_dve", 12)
                dve.tensor_tensor(bn_sq[:, :], t1, beta_r, ALU.add).then_inc(inv, 1)

            if ph.kind == "dense" and ph.agg:
                spill_vector(dve, ph, is_crowded)

            def choose(step):
                if step.has(T):
                    wait(dve, ph, "turned" if ph.agg == "pre" else "mm_done", step.index - T + 1)
                dve.tensor_scalar(select[:, step.pair, :], iota_row[:, :], slot_node[:, bass.ds(step.index, 1)],
                                  None, ALU.is_equal).then_inc(ph.m["selected"].sem, 1)

            def body(step):
                near, before, older, s_ = step.tile(1), step.tile(-1), step.tile(-2), step.slot
                if ph.kind == "dense" and near.exists:
                    for g, (buf, chunks, ps) in enumerate(ph.parts):
                        wait(dve, ph, "hi_done", ph.groups * near.index + g + 1)
                        if near.has(T):
                            wait(dve, ph, "mm_done", near.index - T + 1)
                        at = g * KC * P
                        dve.tensor_tensor(ph.lo[:, near.pair, at:at + chunks * P], ps[near.pair][:, 0:chunks * P],
                                          ph.hi[:, near.pair, at:at + chunks * P].bitcast(F32), ALU.subtract)\
                            .then_inc(ph.m["lo_done"].sem, 1)
                if ph.kind == "dense" and ph.agg:
                    ahead = step.tile(2 if ph.agg == "pre" else 1)
                    if ahead.exists:
                        choose(ahead)
                if ph.kind == "dense" and ph.epi == "mish" and older.exists:
                    o_ = older.slot
                    wait(dve, ph, "mish_act", 4 * older.index + 4)
                    if older.has(U):
                        slot_wait(dve, ph, "stored", older, U)
                    dve.scalar_tensor_tensor(out=res[:, o_, :], in0=e_buf[:, o_, :], scalar=1.0,
                                             in1=v_buf[:, o_, :], op0=ALU.subtract, op1=ALU.mult,
                                             reverse0=True).then_inc(ph.m["res_dve"].sem, 1)
                if ph.kind == "dense" and ph.epi == "bn" and before.exists:
                    wait(dve, ph, "square_done", before.index + 1)
                    wait(dve, ph, "sq_done", before.index + 1)
                    dve.tensor_tensor(bn_sq[:, :], bn_sq[:, :], square[:, before.pair, :], ALU.add)\
                        .then_inc(ph.m["sq_done"].sem, 1)
                if ph.kind == "dense" and step.exists and ph.epi != "bn":
                    y = y_ps[step.pair][:, :]
                    wait_mm = ph.epi in ("mish", "gcn", "gcn_last", "norm2", "sage")
                    if wait_mm:
                        wait(dve, ph, "mm_done", step.index + 1)
                    if ph.epi == "mish":
                        if step.has(U):
                            wait(dve, ph, "res_dve", step.index - U + 1)
                        dve.tensor_tensor(v_buf[:, s_, :], y, bias[:, :], ALU.add)\
                            .then_inc(ph.m["v_done"].sem, 1)
                    if ph.epi == "gcn":
                        if step.has(U):
                            wait(dve, ph, "res_act", step.index - U + 1)
                        dve.scalar_tensor_tensor(out=v_buf[:, s_, :], in0=y,
                                                 scalar=dinv[:, bass.ds(step.index, 1)], in1=bias[:, :],
                                                 op0=ALU.mult, op1=ALU.add).then_inc(ph.m["v_done"].sem, 1)
                    if ph.epi == "gcn_last":
                        wait(dve, ph, "side_done", step.index + 1)
                        if step.has(U):
                            wait(dve, ph, "res_act", step.index - U + 1)
                            slot_wait(dve, ph, "x_stored", step, U)
                        dve.scalar_tensor_tensor(out=x_out[:, s_, :], in0=y,
                                                 scalar=dinv[:, bass.ds(step.index, 1)], in1=side_a[:, s_, :],
                                                 op0=ALU.mult, op1=ALU.add).then_inc(ph.m["x_done"].sem, 1)
                        wait(dve, ph, "x_done", step.index + 1)
                        moments(1, step, x_out[:, s_, :])
                    if ph.epi == "norm2":
                        wait(dve, ph, "side_done", 2 * step.index + 2)
                        if step.has(U):
                            wait(dve, ph, "x_done", step.index - U + 1)
                        dve.tensor_tensor(v_buf[:, s_, :], y, side_a[:, s_, :], ALU.add)\
                            .then_inc(ph.m["v_done"].sem, 1)
                        wait(dve, ph, "v_done", step.index + 1)
                        moments(0, step, v_buf[:, s_, :])
                    if ph.epi == "sage":
                        m = ph.m["v_done"]
                        if step.has(U):
                            wait(dve, ph, "res_dve", step.index - U + 1)
                        dve.scalar_tensor_tensor(out=v_buf[:, s_, :], in0=agg_ps[step.pair][:, :],
                                                 scalar=rdeg[:, bass.ds(step.index, 1)], in1=bias[:, :],
                                                 op0=ALU.mult, op1=ALU.add).then_inc(m.sem, 1)
                        dve.wait_ge(m.sem, m.at(2 * step.index + 1))
                        dve.tensor_tensor(v_buf[:, s_, :], v_buf[:, s_, :], y, ALU.add)\
                            .then_inc(m.sem, 1)
                        dve.wait_ge(m.sem, m.at(2 * step.index + 2))
                        slot_wait(dve, ph, "side_a", step)
                        if step.has(U):
                            slot_wait(dve, ph, "stored", step, U)
                        dve.scalar_tensor_tensor(out=res[:, s_, :], in0=v_buf[:, s_, :], scalar=0.0,
                                                 in1=side_a[:, s_, :], op0=ALU.max, op1=ALU.add)\
                            .then_inc(ph.m["res_dve"].sem, 1)
                if ph.kind == "dense" and older.exists:
                    b_ = older.slot
                    if ph.epi == "norm2":
                        wait(dve, ph, "normed", older.index + 1)
                        dve.tensor_tensor(v_buf[:, b_, :], v_buf[:, b_, :], gamma_row[:, :], ALU.mult)\
                            .then_inc(ph.m["scaled"].sem, 1)
                        wait(dve, ph, "scaled", older.index + 1)
                        if older.has(U):
                            wait(dve, ph, "res_act", older.index - U + 1)
                            slot_wait(dve, ph, "x_stored", older, U)
                        dve.tensor_tensor(x_out[:, b_, :], v_buf[:, b_, :], side_b[:, b_, :], ALU.add)\
                            .then_inc(ph.m["x_done"].sem, 1)
                        wait(dve, ph, "x_done", older.index + 1)
                        moments(1, older, x_out[:, b_, :])
                if ph.kind == "norm" and step.exists:
                    if not step.fixed or part_rows(step.index):
                        slot_wait(dve, ph, "x_loaded", step)
                    moments(1, step, side_a[:, s_, :])
                if ph.kind == "apply":
                    if step.exists:
                        if step.fixed and step.index == 0:
                            wait(dve, ph, "bn_dve", BN_STEPS)
                        k_ = kept[:, bass.ds(step.index, 1), :].rearrange("p o d -> p (o d)")
                        dve.tensor_tensor(k_, k_, bn_sum[:, :], ALU.mult).then_inc(ph.m["mul_done"].sem, 1)
                    if ph.last and before.exists:
                        k_ = kept[:, bass.ds(before.index, 1), :].rearrange("p o d -> p (o d)")
                        wait(dve, ph, "add_done", before.index + 1)
                        slot_wait(dve, ph, "side_a", before)
                        dve.scalar_tensor_tensor(out=k_, in0=k_, scalar=0.0, in1=x_slots[before.slot],
                                                 op0=ALU.max, op1=ALU.add).then_inc(ph.m["x_done"].sem, 1)
                        wait(dve, ph, "x_done", before.index + 1)
                        moments(1, before, k_)
            steps(dve, ph.n, body, 2, 4)

        held = {id(nc.gpsimd): sem("held_pool"), id(nc.scalar): sem("held_act"), id(nc.vector): sem("held_dve")}

        block = ctx.enter_context(nc.Block())

        @block.sync
        def _(sp):
            setup_sync(sp)
            for ph in phases:
                phase_sync(sp, ph)
                if ph.kind == "norm":
                    table_sync(sp)
            all_stored(sp, phases[-1])

        @block.gpsimd
        def _(pool):
            setup_pool(pool)
            dinv_pool(pool)
            scatter_pool(pool)
            is_crowded = None
            for ph in phases:
                if ph.kind != "norm" and is_crowded is None and ph.agg:
                    is_crowded = load_crowded(pool)
                phase_pool(pool, ph, is_crowded)

        @block.scalar
        def _(act):
            act.wait_ge(s_const, 14)
            nc.scalar.preload_act_table_set("natural_log_exp_and_others")
            for ph in phases:
                phase_scalar(act, ph)

        @block.vector
        def _(dve):
            setup_vector(dve)
            is_crowded = None
            for ph in phases:
                phase_vector(dve, ph, is_crowded)
                if ph.kind == "norm":
                    table_vector(dve)
                    is_crowded = load_crowded(dve)

        @block.tensor
        def _(pe):
            setup_tensor(pe)
            is_crowded = None
            for ph in phases:
                if ph.kind != "norm" and is_crowded is None and ph.agg:
                    is_crowded = load_crowded(pe)
                phase_tensor(pe, ph, is_crowded)


def kernel(**inputs):
    import numpy as _np
    import concourse.bacc as _bacc
    from concourse import mybir as _mybir
    from concourse.bass_utils import run_bass_kernel_spmd as _run

    nc = _bacc.Bacc("TRN2", target_bir_lowering=False, num_devices=1)
    arrays, handles = {}, {}
    for name, value in inputs.items():
        v = _np.ascontiguousarray(value)
        arrays[f"in_{name}"] = v
        handles[name] = nc.dram_tensor(f"in_{name}", v.shape, _mybir.dt.from_np(v.dtype), kind="ExternalInput").ap()
    out = nc.dram_tensor("out_x", inputs["x"].shape, _mybir.dt.float32, kind="ExternalOutput").ap()
    build(nc, handles, out)
    r = _run(nc, [arrays], core_ids=[0])
    return r.results[0]["out_x"]
```

```python
from contextlib import ExitStack

import concourse.bass as bass
from concourse import mybir

ALU = mybir.AluOpType
ACT = mybir.ActivationFunctionType
F32 = mybir.dt.float32
F32R = mybir.dt.float32r
BF16 = mybir.dt.bfloat16
I32 = mybir.dt.int32

P = 128
SLOTS = 96
U = 4
T = 2
EPS = 1e-5
FAR = 1 << 20
EXP_MAX = 20.0


class Mark:

    def __init__(self, sem, base):
        self.sem, self.base = sem, base

    def at(self, n):
        return self.base + n


class Step:

    def __init__(self, group, lane, n, fixed):
        self.group, self.lane, self.n, self.fixed = group, lane, n, fixed

    def tile(self, ahead):
        return Step(self.group + (self.lane + ahead) // U, (self.lane + ahead) % U, self.n, self.fixed)

    @property
    def index(self):
        return self.group * U + self.lane

    @property
    def slot(self):
        return self.lane

    @property
    def pair(self):
        return self.lane % T

    @property
    def exists(self):
        return not self.fixed or 0 <= self.index < self.n

    def has(self, before):
        return not self.fixed or self.index >= before


def steps(eng, n, body, ahead, behind, between=None, peel=2):
    first = peel * U
    last = (n - 2 * U) // U * U
    for t in range(-ahead, first):
        body(Step(t // U, t % U, n, True))
    with eng.Fori(first // U, last // U) as group:
        for lane in range(U):
            body(Step(group, lane, n, False))
    if between is not None:
        between()
    for t in range(last, n + behind):
        body(Step(t // U, t % U, n, True))


class Phase:

    def __init__(self, name, kind, n, before, out=None, tile=None, gathers=(), attr=False, agg=None, w=None,
                 wide=False, raw=None, turned=False, epi=None, bias=None, gamma=None, beta=None, side=(),
                 x_in=None, x_out=None, last=False):
        self.name, self.kind, self.n, self.before = name, kind, n, before
        self.m = {}
        self.early, self.raw_at, self.next = False, 0, None
        self.peel = 3 if epi == "norm2" else 2
        self.out, self.x_in, self.x_out = out, x_in, x_out
        self.tile, self.gathers, self.attr, self.side = tile, gathers, attr, side
        self.agg = agg
        self.split = agg is not None
        self.mixed = agg == "pre"
        self.parts_at = 3 if self.mixed else 1 if self.split else 0
        self.w, self.wide, self.raw, self.turned = w, wide, raw, turned
        self.epi, self.bias, self.gamma, self.beta, self.last = epi, bias, gamma, beta, last


def build(nc, a, out):
    x = a["x"]
    n_nodes, D = x.shape
    n_edges = a["src"].shape[0]
    DE = a["edge_attr_64"].shape[1]
    KC = D // P
    NT = -(-n_nodes // P)
    NT += -NT % U
    ET = -(-n_edges // P)
    ET += -ET % U
    NR, ER = NT * P, ET * P
    full_nt, rest_n = n_nodes // P, n_nodes % P
    EP = n_edges // ET
    assert EP * ET == n_edges and EP <= P

    def scratch(name, shape, dt=F32):
        return nc.dram_tensor(name, shape, dt, kind="Internal").ap()

    h0 = scratch("h0", [NR, D])
    ga = scratch("ga", [NR, D])
    gb = scratch("gb", [NR, D])
    msg = scratch("msg", [ER, D])
    e1 = scratch("e1", [ER, D])
    e2 = scratch("e2", [ER, D])
    u0 = scratch("u0", [NR, D])
    x1 = scratch("x1", [NR, D])
    x2 = scratch("x2", [NR, D])
    x3 = scratch("x3", [NR, D])
    spill = scratch("spill", [NR, D])
    slots_dram = scratch("slot_table", [NR, 4], I32)

    with ExitStack() as ctx:
        def sb(name, shape, dt=F32):
            return ctx.enter_context(nc.sbuf_tensor(name, shape, dt))

        def psum(name, shape, dt=F32):
            return ctx.enter_context(nc.psum_tensor(name, shape, dt))

        sems, stood = {}, {}

        def sem(name):
            if name not in sems:
                sems[name] = ctx.enter_context(nc.semaphore(name))
                stood[name] = 0
            return sems[name]

        w_hi = sb("w_hi", [P, KC, D], F32R)
        w_lo = sb("w_lo", [P, KC, D], F32R)
        rest = ExitStack()
        normed_out = rest.enter_context(nc.sbuf_tensor("normed_out", [P, U, D], F32))
        rest.close()
        zt_hi = sb("zt_hi", [P, T, KC * P], F32R)
        zt_lo = sb("zt_lo", [P, T, KC * P], F32R)
        share = ExitStack()
        w_raw_bn = share.enter_context(nc.sbuf_tensor("w_raw_bn", [P, KC, D], F32))
        share.close()
        tile_in = sb("tile_in", [P, T, D])
        gathered = sb("gathered", [P, T, D])
        equal = ExitStack()
        same = equal.enter_context(nc.sbuf_tensor("same", [P, T, P], F32))
        equal.close()
        select = sb("select", [P, T, P], F32R)
        ident = sb("ident", [P, P])
        ones = sb("ones", [P, P])
        iota_row = sb("iota_row", [P, P])
        src_col = sb("src_col", [P, ET], I32)
        dst_col = sb("dst_col", [P, ET], I32)
        dst_f = sb("dst_f", [P, ET])
        edge_id = sb("edge_id", [P, ET], I32)
        slot_src = sb("slot_src", [P, NT], I32)
        slot_edge = sb("slot_edge", [P, NT], I32)
        slot_node = sb("slot_node", [P, NT])
        spill_row = sb("spill_row", [P, NT], I32)
        dinv = sb("dinv", [P, NT])
        rdeg = sb("rdeg", [P, NT])
        minus_half = sb("minus_half", [P, 1])
        idx = sb("idx", [P, 2, T], I32)
        idx_spill = sb("idx_spill", [P, 2], I32)
        crowded = sb("crowded", [P, 1], I32)
        ln_st = sb("ln_st", [P, 2, U, 6])
        ln_mv = sb("ln_mv", [P, 2, U, 2])
        ln_sc = sb("ln_sc", [P, 2, U, 4])
        own = ExitStack()
        bn_sum = own.enter_context(nc.sbuf_tensor("bn_sum", [P, D], F32))
        bn_sq = own.enter_context(nc.sbuf_tensor("bn_sq", [P, D], F32))
        square = own.enter_context(nc.sbuf_tensor("square", [P, D], F32))
        gb_hi = own.enter_context(nc.sbuf_tensor("gb_hi", [P, 1, D], F32R))
        gb_lo = own.enter_context(nc.sbuf_tensor("gb_lo", [P, 1, D], F32R))
        kept = own.enter_context(nc.sbuf_tensor("kept", [P, NT, D], F32))
        own.close()

        w_raw = sb("w_raw", [P, 2 * KC + 1, D])
        w1_hi = sb("w1_hi", [P, 2 * KC + 1, D], F32R)
        w1_lo = sb("w1_lo", [P, 2 * KC + 1, D], F32R)
        e_hi = sb("e_hi", [P, T, (2 * KC + 1) * P], F32R)
        e_lo = sb("e_lo", [P, T, (2 * KC + 1) * P], F32R)
        attr = sb("attr", [P, T, P])
        v_buf = sb("v_buf", [P, U, D])
        e_buf = sb("e_buf", [P, U, D])
        res = sb("res", [P, U, D])
        x_out = sb("x_out", [P, U, D])
        side_a = sb("side_a", [P, U, D])
        side_b = sb("side_b", [P, U, D])
        bias = sb("bias", [P, D])
        gamma_row = sb("gamma_row", [P, D])
        beta_row = sb("beta_row", [P, D])
        half = sb("half", [P, 1])
        one_row = sb("one_row", [1, P], F32R)
        bias_hi = sb("bias_hi", [1, D], F32R)
        bias_lo = sb("bias_lo", [1, D], F32R)

        x_slots = [tile_in[:, 0, :], tile_in[:, 1, :], gathered[:, 0, :], gathered[:, 1, :]]
        def g_parts(ph, step):
            if ph.epi == "bn":
                return gb_hi[:, 0, :], gb_lo[:, 0, :], 1
            return e_hi[:, step.pair, 0:D], e_lo[:, step.pair, 0:D], T

        zt_ps = [psum(f"zt_ps{i}", [P, D]) for i in range(T)]
        y_ps = [psum(f"y_ps{i}", [P, D]) for i in range(T)]
        agg_ps = [psum(f"agg_ps{i}", [P, D]) for i in range(T)]
        at_ps = [psum(f"at_ps{i}", [P, D]) for i in range(T)]

        phases = []

        def phase(name, kind, n, **kw):
            ph = Phase(name, kind, n, phases[-1] if phases else None, **kw)
            phases.append(ph)
            return ph

        def count(ph, name, total):
            s_ = sem(name)
            ph.m[name] = Mark(s_, stood[name])
            stood[name] += total

        def node_rows(t_):
            return t_[0:NR, :]

        L0, L1, L2, L3 = "L0_gnn_", "L1_gnn_", "L2_gnn_", "L3_gnn_"
        w1 = a[L0 + "W1"]
        one = [("tile", KC, 0)]
        phase("norm_in", "norm", NT, out=h0)
        phase("edge_1", "dense", ET, tile=None, gathers=[(h0, src_col), (h0, dst_col)], attr=True, agg=None,
              w=w1, wide=True, raw=w_raw, epi="mish", bias=a[L0 + "b1"], out=e1)
        phase("edge_2", "dense", ET, tile=e1, gathers=[], attr=False, agg=None,
              w=a[L0 + "W2"], wide=False, raw=w_raw, epi="mish", bias=a[L0 + "b2"], out=e2)
        phase("edge_3", "dense", ET, tile=e2, gathers=[], attr=False, agg=None,
              w=a[L0 + "W3"][D:2 * D, :], wide=False, raw=w_raw, epi="copy", bias=None, out=msg)
        phase("node_1", "dense", NT, tile=h0, gathers=[(msg, slot_edge)], attr=False, agg="post",
              w=a[L0 + "W3"][0:D, :], wide=False, raw=w_raw, epi="mish", bias=a[L0 + "b3"], out=u0)
        phase("node_2", "dense", NT, tile=u0, gathers=[], attr=False, agg=None,
              w=a[L0 + "W4"], wide=False, raw=w_raw, epi="norm2", bias=a[L0 + "b4"], side=[h0, None],
              gamma=a[L0 + "gamma"], beta=a[L0 + "beta"], out=ga, x_out=x1)
        g_now, g_next = ga, gb
        n_bn = a[L1 + "W"].shape[0]
        for l in range(n_bn):
            phase(f"bn_{l}", "dense", NT, tile=ga, gathers=[(ga, slot_src)], attr=False, agg="pre",
                  w=a[L1 + "W"][l], wide=False, raw=w_raw_bn, turned=True, epi="bn", bias=None, out=None)
            phase(f"bn_apply_{l}", "apply", NT, bias=a[L1 + "b"][l], gamma=a[L1 + "gamma"][l],
                  beta=a[L1 + "beta"][l], last=l == n_bn - 1, out=ga, x_in=x1, x_out=x2)
        for l in (1, 2):
            phase(f"gcn_{l}", "dense", NT, tile=g_now, gathers=[(g_now, slot_src)], attr=False, agg="pre",
                  w=a[L2 + f"W{l}"], wide=False, raw=w_raw, epi="gcn", bias=a[L2 + f"b{l}"], out=g_next)
            g_now, g_next = g_next, g_now
        phase("gcn_3", "dense", NT, tile=g_now, gathers=[(g_now, slot_src)], attr=False, agg="pre",
              w=a[L2 + "W3"], wide=False, raw=w_raw, epi="gcn_last", bias=a[L2 + "b3"], side=[x2],
              out=h0, x_out=x3)
        phase("sage_edge", "dense", ET, tile=None, gathers=[(h0, src_col)], attr=False, agg=None,
              w=a[L3 + "W"][D:2 * D, :], wide=False, raw=w_raw, epi="copy", bias=None, out=msg)
        phase("sage_node", "dense", NT, tile=h0, gathers=[(msg, slot_edge)], attr=False, agg="sep",
              w=a[L3 + "W"][0:D, :], wide=False, raw=w_raw, epi="sage", bias=a[L3 + "b"], side=[x3], out=out)

        BN_STEPS = 12

        def ring(what):
            return T if what.startswith(("loaded", "gathered", "attr")) else U

        side = 0
        for ph in phases:
            if ph.kind == "dense" and not ph.turned:
                prev = ph.before
                ph.early = prev.kind == "norm" or (prev.kind == "dense" and not prev.turned)
                side = 1 if ph.wide or (ph.early and side == 0) else 0
                ph.wh, ph.wl = (w1_hi, w1_lo) if side else (w_hi, w_lo)
                ph.raw_at = KC if side and not ph.wide else 0
            ph.next = phases[phases.index(ph) + 1] if ph is not phases[-1] else None

        for ph in phases:
            n = ph.n
            ph.spills = sum(p_.kind == "dense" and p_.agg is not None for p_ in phases[:phases.index(ph)])
            ph.groups = 1
            if ph.kind == "dense":
                if ph.tile is not None:
                    ph.parts = [(tile_in, KC, zt_ps)]
                else:
                    ph.parts = [(gathered, KC, zt_ps)]
                if ph.attr:
                    ph.parts = [(gathered, KC, zt_ps), (tile_in, KC, agg_ps), (attr, 1, at_ps)]
                ph.groups = len(ph.parts)
                ph.hi, ph.lo = (e_hi, e_lo) if ph.wide else (zt_hi, zt_lo)
                if ph.turned:
                    ph.wh, ph.wl = w_hi, w_lo
                ph.chunks = sum(c for _, c, _ in ph.parts)
                count(ph, "w_loaded", 16 * (1 if not ph.wide else 2))
                count(ph, "rows_loaded", 16 * sum(r is not None for r in (ph.bias, ph.gamma,
                                                                        ph.beta)))
                count(ph, "w_turned", KC if ph.turned else 0)
                if ph.turned:
                    count(ph, "lanes_zeroed", 1)
                count(ph, "w_hi_done", ph.chunks)
                count(ph, "w_lo_done", ph.chunks)
                if ph.agg:
                    count(ph, "selected", n)
                if ph.split:
                    count(ph, "g_hi_done", n)
                    count(ph, "g_lo_done", n)
                if ph.mixed:
                    count(ph, "agg_done", n)
                    count(ph, "mixed_done", n)
                count(ph, "turned", n * ph.groups)
                count(ph, "hi_done", n * ph.groups)
                count(ph, "lo_done", n * ph.groups)
                count(ph, "mm_done", n)
                for i in range(len(ph.gathers)):
                    count(ph, f"idx_done{i}", n)
                    for s_ in range(T):
                        count(ph, f"gathered{i}_{s_}", 16 * (n // T))
                if ph.attr:
                    for s_ in range(T):
                        count(ph, f"attr{s_}", 16 * (n // T))
                e = ph.epi
                if e == "mish":
                    count(ph, "v_done", n)
                    count(ph, "clipped", n)
                    count(ph, "mish_act", 4 * n)
                    count(ph, "res_dve", n)
                elif e == "copy":
                    count(ph, "res_act", n)
                elif e == "bn":
                    count(ph, "kept_done", n)
                    count(ph, "square_done", n)
                    count(ph, "sum_done", n + 1)
                    count(ph, "sq_done", n + 1)
                elif e == "gcn":
                    count(ph, "v_done", n)
                    count(ph, "res_act", n)
                elif e == "gcn_last":
                    count(ph, "side_done", n)
                    count(ph, "x_done", n)
                    count(ph, "res_act", n)
                elif e == "norm2":
                    count(ph, "side_done", n)
                    count(ph, "bias_hi_done", 2)
                    count(ph, "bias_lo_done", 1)
                    count(ph, "v_done", n)
                    count(ph, "normed", n)
                    count(ph, "scaled", n)
                    count(ph, "x_done", n)
                    count(ph, "res_act", n)
                elif e == "sage":
                    count(ph, "v_done", 2 * n)
                    count(ph, "res_dve", n)
                if e in ("gcn_last", "norm2"):
                    for k in ((0, 1) if e == "norm2" else (1,)):
                        count(ph, f"stats{k}", n)
                        count(ph, f"gauged{k}", n)
                        count(ph, f"moments{k}", n)
                        count(ph, f"ln_ready{k}", (3 if k == 1 and e == "norm2" else 2) * n)
            if ph.kind == "norm":
                count(ph, "stats1", n)
                count(ph, "gauged1", n)
                count(ph, "moments1", n)
                count(ph, "ln_ready1", 2 * n)
                count(ph, "res_act", n)
            if ph.kind == "apply":
                count(ph, "rows_loaded", 48)
                count(ph, "totals_done", 2)
                count(ph, "bn_dve", BN_STEPS)
                count(ph, "bn_act", 2)
                count(ph, "mul_done", n)
                count(ph, "add_done", n - n // U)
                count(ph, "add_dve", n // U)
                count(ph, "res_act", n)
                if ph.last:
                    count(ph, "x_done", n)
                    count(ph, "stats1", n)
                    count(ph, "gauged1", n)
                    count(ph, "moments1", n)
                    count(ph, "ln_ready1", 3 * n)
            def loads(what, on):
                for s_ in range(ring(what)):
                    if on:
                        count(ph, f"{what}{s_}", 16 * (n // ring(what)))
            ph.loads_x = ph.kind == "norm" or (ph.kind == "dense" and ph.epi == "norm2")
            loads("loaded", ph.kind == "dense" and ph.tile is not None)
            loads("side_a", (ph.kind == "dense" and len(ph.side) > 0) or (ph.kind == "apply" and ph.last))
            if ph.loads_x:
                for s_ in range(U):
                    count(ph, f"x_loaded{s_}",
                          sum(16 for t in range(s_, n, U) if t < full_nt or (t == full_nt and rest_n)))
            loads("x_stored", ph.x_out is not None and (ph.kind == "dense" or ph.last))
            if ph.kind == "dense" and ph.epi == "sage":
                for s_ in range(U):
                    count(ph, f"stored{s_}",
                          sum(16 for t in range(s_, n, U) if t < full_nt or (t == full_nt and rest_n)))
            else:
                loads("stored", ph.out is not None)

        def hold(eng, step):
            if not step.fixed:
                eng.sem_inc(held[id(eng)], 1)

        def slot_wait(eng, ph, name, step, ahead_of=0):
            r = ring(name)
            m = ph.m[f"{name}{step.lane % r}"]
            eng.wait_ge(m.sem, m.at(16 * (step.group * (U // r) + step.lane // r + 1 - ahead_of // r)))
            if eng is nc.gpsimd:
                hold(eng, step)

        def all_stored(eng, ph):
            for name in ("stored", "x_stored"):
                for s_ in range(U):
                    if f"{name}{s_}" in ph.m:
                        m = ph.m[f"{name}{s_}"]
                        total = m.base + 16 * (ph.n // U)
                        if ph.kind == "dense" and ph.epi == "sage":
                            total = m.base + sum(16 for t in range(s_, ph.n, U)
                                                 if t < full_nt or (t == full_nt and rest_n))
                        eng.wait_ge(m.sem, total)

        def wait(eng, ph, name, n):
            m = ph.m[name]
            eng.wait_ge(m.sem, m.at(n))

        def rows(t_, step):
            return t_[bass.ds(step.index * P, P), :]

        def bcast(row):
            return row.rearrange("(o d) -> o d", o=1).to_broadcast([P, row.shape[0]])

        n_grp = 5
        assert ET % (n_grp * T) == 0 and n_grp * NT <= 512 and NT == 2 * ET
        of_tile = sb("of_tile", [P, ET, NT], BF16)
        earlier = sb("earlier", [P, ET, NT], BF16)
        of_node = sb("of_node", [P, ET, P], BF16)
        before_me = sb("before_me", [P, P], BF16)
        ones_bf = sb("ones_bf", [P, P], BF16)
        ranked = sb("ranked", [P, T, n_grp, NT])
        lane = sb("lane", [P, 1], I32)
        lane_f = sb("lane_f", [P, 1])
        row_i = sb("row_i", [P, P], I32)
        tile_i = sb("tile_i", [P, ET], I32)
        tile_f = sb("tile_f", [P, ET])
        node_i = sb("node_i", [P, ET], I32)
        node_f = sb("node_f", [P, ET])
        rank = sb("rank", [P, ET])
        over = sb("over", [P, ET])
        position = sb("position", [P, ET], I32)
        payload = sb("payload", [P, ET, 4], I32)
        pay_now = sb("pay_now", [P, U, 4], I32)
        at_now = sb("at_now", [P, U], I32)
        degree = sb("degree", [P, NT])
        exponent = sb("exponent", [P, NT])
        deg1 = sb("deg1", [P, NT])
        empty = sb("empty", [P, NT, 4], I32)
        slots = sb("slots", [P, NT, 4], I32)
        node_id = sb("node_id", [P, NT], I32)
        node_id_f = sb("node_id_f", [P, NT])
        real_f = sb("real_f", [P, NT])
        crowded_f = sb("crowded_f", [P, 1])
        many = sb("many", [P, NT])
        slot_f = sb("slot_f", [P, 2, NT])
        spill_f = sb("spill_f", [P, 2, NT])
        last_sum = sb("last_sum", [P, NT], BF16)
        counted = sb("counted", [P, NT])
        s_memset, s_const, s_cols, s_consts = sem("s_memset"), sem("s_const"), sem("s_cols"), sem("s_consts")
        s_prep, s_ranks, s_rank, s_pos = sem("s_prep"), sem("s_ranks"), sem("s_rank"), sem("s_pos")
        s_count, s_pay, s_put = sem("s_count"), sem("s_pay"), [sem(f"s_put{i}") for i in range(U)]
        s_empty, s_slots, s_table, s_dinv, s_inv = (sem("s_empty"), sem("s_slots"), sem("s_table"), sem("s_dinv"),
                                                    sem("s_inv"))

        def grouped(eng, group):
            for g in range(T):
                group(g, g, True)
            with eng.Fori(1, ET // n_grp // T) as q:
                for s_ in range(T):
                    group(q * T + s_, s_, False)

        def setup_sync(sp):
            sp.wait_ge(s_memset, 2)
            for col, name in ((src_col, "src"), (dst_col, "dst")):
                sp.dma_start(col[0:EP, :], a[name].rearrange("(p k) -> p k", k=ET)).then_inc(s_cols, 16)
            sp.wait_ge(s_memset, 5)
            sp.wait_ge(s_const, 14)
            sp.dma_start(slots_dram.rearrange("(a p) c -> p a c", p=P), empty[:, :, :]).then_inc(s_empty, 16)

        def table_sync(sp):
            for s_ in range(U):
                sp.wait_ge(s_put[s_], 16 * (ET // U))
            sp.dma_start(slots[:, :, :], slots_dram.rearrange("(a p) c -> p a c", p=P)).then_inc(s_slots, 16)

        def setup_pool(pool):
            pool.memset(src_col[:, :], FAR).then_inc(s_memset, 1)
            pool.memset(dst_col[:, :], FAR).then_inc(s_memset, 1)
            pool.memset(empty[:, :, 0:2], FAR).then_inc(s_memset, 1)
            pool.memset(empty[:, :, 2:3], 2 * P).then_inc(s_memset, 1)
            pool.memset(empty[:, :, 3:4], 0).then_inc(s_memset, 1)
            pool.iota(lane[:, :], pattern=[[0, 1]], base=0, channel_multiplier=1).then_inc(s_const, 1)
            pool.iota(row_i[:, :], pattern=[[1, P]], base=0, channel_multiplier=0).then_inc(s_const, 1)
            pool.iota(edge_id[:, :], pattern=[[P, ET]], base=0, channel_multiplier=1).then_inc(s_const, 1)
            pool.iota(node_id[:, :], pattern=[[P, NT]], base=0, channel_multiplier=1).then_inc(s_const, 1)
            pool.memset(minus_half[:, :], -0.5).then_inc(s_const, 1)
            pool.memset(ones_bf[:, :], 1.0).then_inc(s_const, 1)
            pool.memset(ones[:, :], 1.0).then_inc(s_const, 1)
            pool.memset(gathered[:, :, :], 0.0).then_inc(s_const, 1)
            pool.memset(tile_in[:, :, :], 0.0).then_inc(s_const, 1)
            pool.memset(attr[:, :, :], 0.0).then_inc(s_const, 1)
            pool.memset(w_raw[:, 2 * KC, :], 0.0).then_inc(s_const, 1)
            pool.memset(side_b[:, :, :], 0.0).then_inc(s_const, 1)
            pool.memset(side_a[:, :, :], 0.0).then_inc(s_const, 1)
            pool.memset(half[:, :], 0.5).then_inc(s_const, 1)

        def scatter_pool(pool):
            pool.wait_ge(s_empty, 16)
            pool.wait_ge(s_pos, 9)

            def body(step):
                k = step.index
                if step.has(U):
                    pool.wait_ge(s_put[step.slot], 16 * step.group)
                    hold(pool, step)
                pool.tensor_copy(pay_now[:, step.slot, :], payload[:, bass.ds(k, 1), :]
                                 .rearrange("p o c -> p (o c)")).then_inc(s_pay, 1)
                pool.tensor_copy(at_now[:, step.slot:step.slot + 1], position[:, bass.ds(k, 1)]).then_inc(s_pay, 1)
                pool.wait_ge(s_pay, 2 * k + 2)
                hold(pool, step)
                pool.indirect_dma_start(slots_dram[:, :],
                                        bass.IndirectOffsetOnAxis(ap=at_now[:, step.slot:step.slot + 1], axis=0),
                                        pay_now[:, step.slot, :], None, bounds_check=NR - 1,
                                        oob_is_err=False).then_inc(s_put[step.slot], 16)
            steps(pool, ET, body, 0, 0)

        def dinv_pool(pool):
            pool.wait_ge(s_dinv, 1)
            pool.memset(exponent[:, :], -0.5).then_inc(s_inv, 1)
            pool.wait_ge(s_inv, 1)
            pool.tensor_tensor(deg1[:, :], deg1[:, :], exponent[:, :], ALU.pow).then_inc(s_inv, 1)

        def setup_vector(dve):
            dve.wait_ge(s_const, 14)
            dve.tensor_copy(lane_f[:, :], lane[:, :]).then_inc(s_consts, 1)
            dve.tensor_copy(iota_row[:, :], row_i[:, :]).then_inc(s_consts, 1)
            dve.tensor_copy(node_id_f[:, :], node_id[:, :]).then_inc(s_consts, 1)
            dve.memset(earlier[:, 0, :], 0.0).then_inc(s_consts, 1)
            dve.wait_ge(s_consts, 4)
            dve.tensor_scalar(ident[:, :], iota_row[:, :], lane_f[:, 0:1], None, ALU.is_equal).then_inc(s_consts, 1)
            dve.tensor_scalar(before_me[:, :], iota_row[:, :], lane_f[:, 0:1], None, ALU.is_gt).then_inc(s_consts, 1)
            dve.tensor_scalar(real_f[:, :], node_id_f[:, :], float(n_nodes), None, ALU.is_lt).then_inc(s_consts, 1)
            dve.memset(degree[:, :], 0.0).then_inc(s_consts, 1)
            dve.wait_ge(s_cols, 32)
            dve.tensor_scalar(tile_i[:, :], dst_col[:, :], 7, None, ALU.logical_shift_right).then_inc(s_pos, 1)
            dve.tensor_scalar(node_i[:, :], dst_col[:, :], P - 1, None, ALU.bitwise_and).then_inc(s_pos, 1)
            dve.wait_ge(s_pos, 2)
            dve.tensor_copy(tile_f[:, :], tile_i[:, :]).then_inc(s_pos, 1)
            dve.tensor_copy(node_f[:, :], node_i[:, :]).then_inc(s_pos, 1)
            dve.wait_ge(s_pos, 4)

        def prepare(dve, step):
            k = step.group * (U // 2) + step.lane // 2
            if step.lane % 2 == 0:
                dve.tensor_scalar(of_tile[:, bass.ds(k, 1), :].rearrange("p o a -> p (o a)"), iota_row[:, 0:NT],
                                  tile_f[:, bass.ds(k, 1)], None, ALU.is_equal).then_inc(s_prep, 1)
                return
            dve.tensor_scalar(of_node[:, bass.ds(k, 1), :].rearrange("p o a -> p (o a)"), iota_row[:, :],
                              node_f[:, bass.ds(k, 1)], None, ALU.is_equal).then_inc(s_prep, 1)
            if not step.fixed or k > 0:
                dve.wait_ge(s_prep, 3 * k - 1)
                dve.tensor_tensor(earlier[:, bass.ds(k, 1), :], earlier[:, bass.ds(k - 1, 1), :],
                                  of_tile[:, bass.ds(k - 1, 1), :], ALU.add).then_inc(s_prep, 1)

        def ranks_vector(dve):
            dve.wait_ge(s_prep, 3 * ET - 1)
            dve.tensor_tensor(last_sum[:, :], earlier[:, ET - 1, :], of_tile[:, ET - 1, :],
                              ALU.add).then_inc(s_prep, 1)

            dve.wait_ge(s_consts, 8)

            def group(g, s_, first):
                dve.wait_ge(s_ranks, g + 1)
                if not first:
                    dve.wait_ge(s_rank, 3 * g - 3 * T + 3)
                dve.tensor_tensor(ranked[:, s_, :, :].rearrange("p k a -> p (k a)"), y_ps[s_][:, 0:n_grp * NT],
                                  of_tile[:, bass.ds(g * n_grp, n_grp), :].rearrange("p k a -> p (k a)"),
                                  ALU.mult).then_inc(s_rank, 1)
                dve.tensor_tensor(degree[:, :], degree[:, :], agg_ps[s_][:, 0:NT], ALU.add).then_inc(s_rank, 1)
                dve.wait_ge(s_rank, 3 * g + 2)
                dve.tensor_reduce(rank[:, bass.ds(g * n_grp, n_grp)], ranked[:, s_, :, :],
                                  mybir.AxisListType.X, ALU.add).then_inc(s_rank, 1)
            grouped(dve, group)
            dve.wait_ge(s_rank, 3 * ET // n_grp)
            dve.tensor_scalar(over[:, :], rank[:, :], float(SLOTS), float(FAR), ALU.is_ge, ALU.mult).then_inc(s_pos, 1)
            dve.scalar_tensor_tensor(out=rank[:, :], in0=tile_f[:, :], scalar=float(P), in1=rank[:, :],
                                     op0=ALU.mult, op1=ALU.add).then_inc(s_pos, 1)
            dve.wait_ge(s_pos, 6)
            dve.tensor_tensor(position[:, :], rank[:, :], over[:, :], ALU.add).then_inc(s_pos, 1)
            dve.tensor_copy(payload[:, :, 0], src_col[:, :]).then_inc(s_pos, 1)
            dve.tensor_copy(payload[:, :, 1], edge_id[:, :])
            dve.tensor_copy(payload[:, :, 2], node_i[:, :])
            dve.tensor_copy(payload[:, :, 3], node_i[:, :]).then_inc(s_pos, 1)
            dve.tensor_scalar(deg1[:, :], degree[:, :], 1.0, None, ALU.add).then_inc(s_dinv, 1)
            dve.tensor_scalar(rdeg[:, :], degree[:, :], 1.0, None, ALU.max).then_inc(s_dinv, 1)
            dve.wait_ge(s_dinv, 2)
            dve.reciprocal(rdeg[:, :], rdeg[:, :]).then_inc(s_dinv, 1)
            dve.wait_ge(s_count, 1)
            dve.tensor_scalar(many[:, :], zt_ps[0][:, 0:NT], float(SLOTS), None, ALU.is_gt).then_inc(s_dinv, 1)

        def table_vector(dve):
            dve.wait_ge(s_inv, 2)
            dve.tensor_tensor(dinv[:, :], deg1[:, :], real_f[:, :], ALU.mult).then_inc(s_dinv, 1)
            dve.wait_ge(s_slots, 16)
            dve.wait_ge(s_dinv, 5)
            dve.tensor_copy(slot_f[:, 0, :], slots[:, :, 0]).then_inc(s_table, 1)
            dve.tensor_copy(slot_f[:, 1, :], slots[:, :, 1]).then_inc(s_table, 1)
            dve.tensor_copy(slot_node[:, :], slots[:, :, 2]).then_inc(s_table, 1)
            dve.tensor_scalar(counted[:, :], node_id_f[:, :], -float(FAR), None, ALU.add).then_inc(s_table, 1)
            dve.wait_ge(s_table, 4)
            for i in range(2):
                dve.tensor_scalar(spill_f[:, i, :], slot_f[:, i, :], -1.0, float(FAR), ALU.mult, ALU.add)\
                    .then_inc(s_table, 1)
            dve.tensor_tensor(counted[:, :], counted[:, :], many[:, :], ALU.mult).then_inc(s_table, 1)
            dve.wait_ge(s_table, 7)
            dve.tensor_scalar(spill_row[:, :], counted[:, :], float(FAR), None, ALU.add).then_inc(s_table, 1)
            for i in range(2):
                dve.tensor_tensor(spill_f[:, i, :], spill_f[:, i, :], many[:, :], ALU.mult).then_inc(s_table, 1)
            dve.wait_ge(s_table, 10)
            dve.tensor_tensor(slot_src[:, :], slot_f[:, 0, :], spill_f[:, 0, :], ALU.add).then_inc(s_table, 1)
            dve.tensor_tensor(slot_edge[:, :], slot_f[:, 1, :], spill_f[:, 1, :], ALU.add).then_inc(s_table, 1)
            dve.tensor_scalar(counted[:, :], slot_node[:, :], lane_f[:, 0:1], -1.0, ALU.subtract,
                              ALU.mult).then_inc(s_table, 1)
            dve.wait_ge(s_table, 13)
            dve.tensor_tensor(counted[:, :], counted[:, :], many[:, :], ALU.mult).then_inc(s_table, 1)
            dve.wait_ge(s_table, 14)
            dve.tensor_tensor(slot_node[:, :], slot_node[:, :], counted[:, :], ALU.add).then_inc(s_table, 1)
            dve.tensor_reduce(crowded_f[:, :], many[:, :], mybir.AxisListType.X, ALU.max).then_inc(s_table, 1)
            dve.tensor_copy(dst_f[:, :], dst_col[:, :]).then_inc(s_table, 1)
            dve.wait_ge(s_table, 17)
            dve.tensor_copy(crowded[:, :], crowded_f[:, :]).then_inc(s_table, 1)

        def setup_tensor(pe):
            pe.wait_ge(s_consts, 6)
            pe.wait_ge(s_prep, 3 * ET)

            def group(g, s_, first):
                if not first:
                    pe.wait_ge(s_rank, 3 * g - 3 * T + 3)
                for i in range(n_grp):
                    o = y_ps[s_][:, i * NT:(i + 1) * NT]
                    tiles = of_tile[:, bass.ds(g * n_grp + i, 1), :].rearrange("p o a -> p (o a)")
                    sums = earlier[:, bass.ds(g * n_grp + i, 1), :].rearrange("p o a -> p (o a)")
                    pe.matmul(o, before_me[:, :], tiles, start=True, stop=False)
                    pe.matmul(o, ones_bf[:, :], sums, start=False, stop=True)
                for i in range(n_grp):
                    tiles = of_tile[:, bass.ds(g * n_grp + i, 1), :].rearrange("p o a -> p (o a)")
                    nodes = of_node[:, bass.ds(g * n_grp + i, 1), :].rearrange("p o a -> p (o a)")
                    last = pe.matmul(agg_ps[s_][:, 0:NT], nodes, tiles, start=(i == 0), stop=(i == n_grp - 1))
                last.then_inc(s_ranks, 1)
            grouped(pe, group)
            pe.matmul(zt_ps[0][:, 0:NT], ones_bf[:, :], last_sum[:, :], start=True, stop=True).then_inc(s_count, 1)
            pe.wait_ge(s_rank, 3 * (ET // n_grp))
            pe.wait_ge(s_dinv, 4)

        s_zeroed, s_sp_rows, s_sp_put, s_sp_add = sem("spill_zeroed"), sem("spill_rows"), sem("spill_put"), \
            sem("spill_slots")
        s_sp_pool, s_sp_dve, s_sp_pe, s_sp_idx = sem("spill_pool"), sem("spill_dve"), sem("spill_pe"), \
            sem("spill_idx")

        def load_crowded(eng):
            reg = eng.alloc_register("crowded")
            eng.wait_ge(s_table, 18)
            eng.reg_load(reg, crowded[0:1, 0:1])
            return reg

        def spill_pool(pool, ph, is_crowded):
            table, column = ph.gathers[0][0], (src_col if ph.agg == "pre" else edge_id)
            sp = ph.spills
            with pool.If_ne(is_crowded, 0):
                pool.memset(gathered[:, :, :], 0.0).then_inc(s_sp_pool, 1)
                done = sp * (1 + 2 * ET) + 1
                pool.wait_ge(s_sp_pool, done)
                with pool.Fori(0, NT) as t:
                    pool.dma_start(spill[bass.ds(t * P, P), :], gathered[:, 0, :]).then_inc(s_zeroed, 16)
                pool.wait_ge(s_zeroed, 16 * NT * (sp + 1))
                with pool.Fori(0, ET) as k:
                    pool.tensor_copy(idx_spill[:, 0:1], column[:, bass.ds(k, 1)]).then_inc(s_sp_pool, 1)
                    pool.tensor_copy(idx_spill[:, 1:2], dst_col[:, bass.ds(k, 1)]).then_inc(s_sp_pool, 1)
                    pool.wait_ge(s_sp_pool, 2 * k + (done + 2))
                    pool.sem_inc(held[id(pool)], 1)
                    pool.indirect_dma_start(gathered[:, 0, :], None, table[:, :],
                                            bass.IndirectOffsetOnAxis(ap=idx_spill[:, 0:1], axis=0),
                                            bounds_check=table.shape[0] - 1, oob_is_err=False)\
                        .then_inc(s_sp_rows, 16)
                    pool.indirect_dma_start(gathered[:, 1, :], None, spill[:, :],
                                            bass.IndirectOffsetOnAxis(ap=idx_spill[:, 1:2], axis=0),
                                            bounds_check=NR - 1, oob_is_err=False).then_inc(s_sp_rows, 16)
                    pool.wait_ge(s_sp_dve, 3 * ET * sp + 3 * k + 3)
                    pool.sem_inc(held[id(pool)], 1)
                    pool.indirect_dma_start(spill[:, :], bass.IndirectOffsetOnAxis(ap=idx_spill[:, 1:2], axis=0),
                                            gathered[:, 1, :], None, bounds_check=NR - 1,
                                            oob_is_err=False).then_inc(s_sp_put, 16)
                    pool.wait_ge(s_sp_put, 16 * ET * sp + 16 * k + 16)
                    pool.sem_inc(held[id(pool)], 1)

        def spill_vector(dve, ph, is_crowded):
            sp = ph.spills
            with dve.If_ne(is_crowded, 0):
                with dve.Fori(0, ET) as k:
                    target, done = dst_f[:, bass.ds(k, 1)], 3 * ET * sp
                    dve.wait_ge(s_sp_rows, 32 * ET * sp + 32 * k + 32)
                    dve.tensor_scalar(same[:, 1, :], ones[:, :], target, None, ALU.mult).then_inc(s_sp_dve, 1)
                    dve.wait_ge(s_sp_pe, 2 * ET * sp + 2 * k + 1)
                    dve.tensor_scalar(same[:, 0, :], at_ps[0][:, 0:P], target, None, ALU.is_equal)\
                        .then_inc(s_sp_dve, 1)
                    dve.wait_ge(s_sp_pe, 2 * ET * sp + 2 * k + 2)
                    dve.tensor_tensor(gathered[:, 1, :], gathered[:, 1, :], at_ps[1][:, :], ALU.add)\
                        .then_inc(s_sp_dve, 1)

        def spill_tensor(pe, ph, is_crowded):
            sp = ph.spills
            with pe.If_ne(is_crowded, 0):
                with pe.Fori(0, ET) as k:
                    pe.wait_ge(s_sp_dve, 3 * ET * sp + 3 * k + 1)
                    pe.matmul(at_ps[0][:, 0:P], same[:, 1, :], ident[:, :], start=True, stop=True)\
                        .then_inc(s_sp_pe, 1)
                    pe.wait_ge(s_sp_dve, 3 * ET * sp + 3 * k + 2)
                    pe.matmul(at_ps[1][:, :], same[:, 0, :], gathered[:, 0, :], start=True, stop=True)\
                        .then_inc(s_sp_pe, 1)

        def spill_slots(pool, ph, step, is_crowded):
            at = ph.spills * NT + step.index + 1
            with pool.If_ne(is_crowded, 0):
                pool.tensor_copy(idx_spill[:, 0:1], spill_row[:, bass.ds(step.index, 1)]).then_inc(s_sp_idx, 1)
                pool.wait_ge(s_sp_idx, at)
                hold(pool, step)
                pool.indirect_dma_start(gathered[:, step.pair, :], None, spill[:, :],
                                        bass.IndirectOffsetOnAxis(ap=idx_spill[:, 0:1], axis=0),
                                        bounds_check=NR - 1, oob_is_err=False).then_inc(s_sp_add, 16)
                pool.wait_ge(s_sp_add, 16 * at)
                hold(pool, step)

        def part_rows(t):
            return P if t < full_nt else (rest_n if t == full_nt else 0)

        def added(eng, ph, step):
            if step.lane == U - 1:
                wait(eng, ph, "add_dve", step.group + 1)
            else:
                wait(eng, ph, "add_done", step.group * (U - 1) + step.lane + 1)

        def lag(ph, what):
            kind = ph.epi if ph.kind == "dense" else ph.kind
            return {("mish", "res"): 2, ("norm2", "x_out"): 3, ("norm2", "res"): 5, ("gcn_last", "res"): 3, ("gcn", "res"): 1,
                    ("norm", "res"): 1, ("apply", "x_out"): 1, ("apply", "res"): 4 if ph.last else 0}\
                .get((kind, what), 0)

        def weights_sync(sp, ph):
            if ph.wide:
                sp.wait_ge(s_const, 14)
                sp.dma_start(w_raw[:, 0:2 * KC, :], ph.w[0:2 * D, :].rearrange("(c p) d -> p c d", p=P))\
                    .then_inc(ph.m["w_loaded"].sem, 16)
                sp.dma_start(w_raw[0:DE, 2 * KC, :], ph.w[2 * D:2 * D + DE, :]).then_inc(ph.m["w_loaded"].sem, 16)
            else:
                sp.dma_start(ph.raw[:, ph.raw_at:ph.raw_at + KC, :], ph.w.rearrange("(c p) d -> p c d", p=P))\
                    .then_inc(ph.m["w_loaded"].sem, 16)

        def phase_sync(sp, ph):
            prev = ph.before
            if ph.kind == "dense" and not ph.early:
                if prev.kind == "apply" and not prev.last:
                    wait(sp, prev, "bn_dve", BN_STEPS)
                else:
                    all_stored(sp, prev)
                weights_sync(sp, ph)
            if prev is not None:
                all_stored(sp, prev)
                if prev.kind == "dense" and prev.epi == "bn":
                    wait(sp, prev, "mm_done", prev.n)
                    wait(sp, prev, "sum_done", prev.n + 1)
                    wait(sp, prev, "sq_done", prev.n + 1)
            if ph.kind != "norm":
                if ph.kind == "apply":
                    places = (gathered[:, 0, :], gathered[:, 1, :], square[:, :])
                else:
                    places = (bias[:, :], gamma_row[:, :], beta_row[:, :])
                for row, place in zip((ph.bias, ph.gamma, ph.beta), places):
                    if row is not None:
                        sp.dma_start(place, bcast(row)).then_inc(ph.m["rows_loaded"].sem, 16)
            if ph.kind == "dense" and ph.raw is w_raw_bn:
                wait(sp, ph, "w_turned", KC)

            if ph.next is not None and ph.next.early:
                if ph.kind == "dense":
                    wait(sp, ph, "w_hi_done", ph.chunks)
                    wait(sp, ph, "w_lo_done", ph.chunks)
                weights_sync(sp, ph.next)

            def inc(name, step):
                return ph.m[f"{name}{step.lane % ring(name)}"].sem

            def load_x(step, buf):
                r = part_rows(step.index) if step.fixed else P
                if r == P:
                    sp.dma_start(buf[:, step.slot, :], rows(x, step)).then_inc(inc("x_loaded", step), 16)
                elif r:
                    sp.dma_start(buf[0:r, step.slot, :], x[full_nt * P:n_nodes, :])\
                        .then_inc(inc("x_loaded", step), 16)

            def body(step):
                far = step.tile(2)
                if ph.kind == "dense" and ph.tile is not None and far.exists:
                    if far.has(T):
                        wait(sp, ph, "turned", ph.groups * (far.index - T + 1))
                    sp.dma_start(tile_in[:, far.pair, :], rows(ph.tile, far)).then_inc(inc("loaded", far), 16)
                if ph.kind == "dense" and ph.attr and far.exists:
                    if far.has(T):
                        wait(sp, ph, "turned", ph.groups * (far.index - T + 1))
                    sp.dma_start(attr[0:EP, far.pair, 0:DE],
                                 a["edge_attr_64"].rearrange("(p k) d -> p k d", k=ET)[:, bass.ds(far.index, 1), :]
                                 .rearrange("p o d -> p (o d)")).then_inc(inc("attr", far), 16)
                if ph.kind == "norm" and far.exists:
                    if far.has(U):
                        wait(sp, ph, "res_act", far.index - U + 1)
                    load_x(far, side_a)
                if ph.kind == "dense" and ph.side and far.exists:
                    name = {"norm2": "v_done", "gcn_last": "x_done", "sage": "res_dve"}[ph.epi]
                    if far.has(U):
                        wait(sp, ph, name, far.index - U + 1)
                    sp.dma_start(side_a[:, far.slot, :], rows(ph.side[0], far)).then_inc(inc("side_a", far), 16)
                if ph.kind == "dense" and ph.epi == "norm2" and step.exists:
                    if step.has(U):
                        wait(sp, ph, "x_done", step.index - U + 1)
                    load_x(step, side_b)
                if ph.kind == "apply" and ph.last and far.exists:
                    if far.has(U):
                        wait(sp, ph, "x_done", far.index - U + 1)
                    elif far.fixed and far.index == 0:
                        wait(sp, ph, "bn_dve", BN_STEPS)
                    sp.dma_start(x_slots[far.slot], rows(ph.x_in, far)).then_inc(inc("side_a", far), 16)
                x_late, late = step.tile(-lag(ph, "x_out") - 2), step.tile(-lag(ph, "res") - 2)
                if ph.x_out is not None and (ph.kind == "dense" or ph.last) and x_late.exists:
                    wait(sp, ph, "x_done", x_late.index + 1)
                    buf = x_out[:, x_late.slot, :] if ph.kind == "dense" else \
                        kept[:, bass.ds(x_late.index, 1), :].rearrange("p o d -> p (o d)")
                    sp.dma_start(rows(ph.x_out, x_late), buf).then_inc(inc("x_stored", x_late), 16)
                if ph.out is not None:
                    if late.exists:
                        which = "res_dve" if ph.kind == "dense" and ph.epi in ("mish", "sage") else "res_act"
                        r = part_rows(late.index) if late.fixed and ph.out is out else P
                        if r:
                            wait(sp, ph, which, late.index + 1)
                        if ph.kind == "apply":
                            buf = (normed_out[:, late.slot, :] if ph.last else
                                   kept[:, bass.ds(late.index, 1), :].rearrange("p o d -> p (o d)"))
                        else:
                            buf = res[:, late.slot, :]
                        if r == P:
                            sp.dma_start(rows(ph.out, late), buf).then_inc(inc("stored", late), 16)
                        elif r:
                            sp.dma_start(out[full_nt * P:n_nodes, :], buf[0:r, :]).then_inc(inc("stored", late), 16)
            steps(sp, ph.n, body, 2, 8, peel=ph.peel)

        def gather(pool, ph, i, step, is_crowded):
            table, column = ph.gathers[i]
            dest = (gathered, tile_in)[i]
            m = ph.m[f"idx_done{i}"]
            if ph.agg:
                spill_slots(pool, ph, step, is_crowded)
            pool.tensor_copy(idx[:, i, step.pair:step.pair + 1], column[:, bass.ds(step.index, 1)]).then_inc(m.sem, 1)
            pool.wait_ge(m.sem, m.at(step.index + 1))
            hold(pool, step)
            lanes = SLOTS if ph.agg else P
            pool.indirect_dma_start(dest[0:lanes, step.pair, :], None, table[:, :],
                                    bass.IndirectOffsetOnAxis(ap=idx[0:lanes, i, step.pair:step.pair + 1], axis=0),
                                    bounds_check=table.shape[0] - 1, oob_is_err=False)\
                .then_inc(ph.m[f"gathered{i}_{step.pair}"].sem, 16)

        def ln_pool(pool, ph, k, step, scaled):
            m, s_, mv = ph.m[f"ln_ready{k}"], ln_sc[:, k, step.slot, :], ln_mv[:, k, step.slot, :]
            per = 3 if scaled else 2
            done = step.index * per
            wait(pool, ph, f"moments{k}", step.index + 1)
            hold(pool, step)
            pool.tensor_tensor(s_[:, 1:2] if scaled else s_[:, 2:3], mv[:, 1:2], minus_half[:, 0:1], ALU.pow)\
                .then_inc(m.sem, 1)
            if scaled:
                pool.wait_ge(m.sem, m.at(done + 1))
                pool.tensor_tensor(s_[:, 2:3], s_[:, 1:2], dinv[:, bass.ds(step.index, 1)], ALU.mult)\
                    .then_inc(m.sem, 1)
            pool.wait_ge(m.sem, m.at(done + per - 1))
            hold(pool, step)
            pool.tensor_scalar(s_[:, 3:4], mv[:, 0:1], s_[:, 2:3], -1.0, ALU.mult, ALU.mult).then_inc(m.sem, 1)

        def ln_scaled(ph, k):
            return ph.kind == "apply" or (ph.kind == "dense" and ph.epi == "norm2" and k == 1)

        def phase_pool(pool, ph, is_crowded):
            if ph.kind == "dense":
                if ph.epi == "bn":
                    if ph.before.kind == "apply":
                        wait(pool, ph.before, "mul_done", ph.n)
                    pool.memset(bn_sum[:, :], 0.0).then_inc(ph.m["sum_done"].sem, 1)
                if ph.gathers:
                    all_stored(pool, ph.before)
                if ph.turned:
                    wait(pool, ph, "w_turned", KC)
                    pool.memset(gathered[:, :, :], 0.0).then_inc(ph.m["lanes_zeroed"].sem, 1)
                    wait(pool, ph, "lanes_zeroed", 1)
                if ph.agg:
                    spill_pool(pool, ph, is_crowded)
                if ph.epi in ("norm2", "gcn_last"):
                    wait(pool, ph, "rows_loaded", 48 if ph.epi == "norm2" else 16)
            if ph.kind == "apply":
                wait(pool, ph, "bn_dve", BN_STEPS)

            def body(step):
                if ph.kind == "dense":
                    ahead, before = step.tile(ph.parts_at + 2), step.tile(-1)
                    if ahead.exists:
                        for i in range(len(ph.gathers)):
                            if ahead.has(T):
                                if ph.split:
                                    wait(pool, ph, "g_lo_done", ahead.index - T + 1)
                                else:
                                    wait(pool, ph, "turned", ph.groups * (ahead.index - T + 1))
                                hold(pool, ahead)
                            gather(pool, ph, i, ahead, is_crowded)
                    if ph.epi == "bn" and before.exists:
                        wait(pool, ph, "kept_done", before.index + 1)
                        wait(pool, ph, "sum_done", before.index + 1)
                        pool.tensor_tensor(bn_sum[:, :], bn_sum[:, :],
                                           kept[:, bass.ds(before.index, 1), :].rearrange("p o d -> p (o d)"),
                                           ALU.add).then_inc(ph.m["sum_done"].sem, 1)
                    near, older, fourth = step.tile(1), step.tile(-2), step.tile(-4)
                    if ph.epi == "gcn_last" and near.exists:
                        slot_wait(pool, ph, "side_a", near)
                        pool.tensor_tensor(side_a[:, near.slot, :], side_a[:, near.slot, :], bias[:, :], ALU.add)\
                            .then_inc(ph.m["side_done"].sem, 1)
                    if ph.epi == "norm2":
                        if older.exists:
                            if not older.fixed or part_rows(older.index):
                                slot_wait(pool, ph, "x_loaded", older)
                            pool.tensor_tensor(side_b[:, older.slot, :], side_b[:, older.slot, :],
                                               beta_row[:, :], ALU.add).then_inc(ph.m["side_done"].sem, 1)
                        if before.exists:
                            if before.has(U):
                                wait(pool, ph, "normed", before.index - U + 1)
                            ln_pool(pool, ph, 0, before, False)
                        if fourth.exists:
                            if fourth.has(U):
                                wait(pool, ph, "res_act", fourth.index - U + 1)
                            ln_pool(pool, ph, 1, fourth, True)
                    if ph.epi == "gcn_last" and older.exists:
                        if older.has(U):
                            wait(pool, ph, "res_act", older.index - U + 1)
                        ln_pool(pool, ph, 1, older, False)
                elif ph.kind == "norm":
                    if step.exists:
                        if step.has(U):
                            wait(pool, ph, "res_act", step.index - U + 1)
                        ln_pool(pool, ph, 1, step, False)
                elif ph.kind == "apply":
                    if step.exists and step.lane < U - 1:
                        wait(pool, ph, "mul_done", step.index + 1)
                        k_ = kept[:, bass.ds(step.index, 1), :].rearrange("p o d -> p (o d)")
                        pool.tensor_tensor(k_, k_, bn_sq[:, :], ALU.add).then_inc(ph.m["add_done"].sem, 1)
                    third = step.tile(-3)
                    if ph.last and third.exists:
                        if third.has(U):
                            wait(pool, ph, "res_act", third.index - U + 1)
                        ln_pool(pool, ph, 1, third, True)
            steps(pool, ph.n, body, 5, 5, peel=ph.peel)

        def phase_tensor(pe, ph, is_crowded):
            if ph.kind == "norm":
                return
            if ph.kind == "apply":
                bn = ph.before
                wait(pe, bn, "sum_done", ph.n + 1)
                pe.matmul(y_ps[0][:, :], ones[:, :], bn_sum[:, :], start=True, stop=True)\
                    .then_inc(ph.m["totals_done"].sem, 1)
                wait(pe, bn, "sq_done", ph.n + 1)
                pe.matmul(y_ps[1][:, :], ones[:, :], bn_sq[:, :], start=True, stop=True)\
                    .then_inc(ph.m["totals_done"].sem, 1)
                return
            G = ph.groups
            if ph.turned:
                wait(pe, ph, "w_loaded", 16)
                for c in range(KC):
                    if c >= T:
                        wait(pe, ph, "w_lo_done", c - T + 1)
                    for o in range(KC):
                        last = pe.transpose(zt_ps[c % T][:, o * P:(o + 1) * P],
                                            ph.raw[:, o, c * P:(c + 1) * P], ident[:, :])
                    last.then_inc(ph.m["w_turned"].sem, 1)
            wait(pe, ph, "w_lo_done", ph.chunks)
            if ph.agg:
                spill_tensor(pe, ph, is_crowded)

            def turn(step):
                for g, (buf, chunks, ps) in enumerate(ph.parts):
                    if step.has(T):
                        wait(pe, ph, "lo_done", G * (step.index - T) + g + 1)
                    if buf is attr:
                        slot_wait(pe, ph, "attr", step)
                    elif ph.mixed:
                        wait(pe, ph, "mixed_done", step.index + 1)
                    elif ph.tile is not None:
                        slot_wait(pe, ph, "loaded", step)
                    else:
                        slot_wait(pe, ph, f"gathered{g}_", step)
                    for c in range(chunks):
                        last = pe.transpose(ps[step.pair][:, c * P:(c + 1) * P],
                                            buf[:, step.pair, c * P:(c + 1) * P], ident[:, :])
                    last.then_inc(ph.m["turned"].sem, 1)

            def neighbours(step, target, start):
                wait(pe, ph, "g_lo_done", step.index + 1)
                wait(pe, ph, "selected", step.index + 1)
                pick = select[:, step.pair, :]
                g_hi, g_lo, _ = g_parts(ph, step)
                pe.matmul(target, pick, g_lo, start=start, stop=False)
                return pe.matmul(target, pick, g_hi, start=False, stop=True)

            free = {"mish": ("v_done", 1), "copy": ("res_act", 1), "bn": ("square_done", 1), "gcn": ("v_done", 1),
                    "gcn_last": ("x_done", 1), "norm2": ("v_done", 1), "sage": ("v_done", 2)}[ph.epi]

            def body(step):
                near = step.tile(1)
                if near.exists:
                    turn(near)
                far = step.tile(2)
                if ph.mixed and far.exists:
                    if far.has(T):
                        wait(pe, ph, "mixed_done", far.index - T + 1)
                    neighbours(far, agg_ps[far.pair][:, :], True).then_inc(ph.m["agg_done"].sem, 1)
                if not step.exists:
                    return
                wait(pe, ph, "lo_done", G * (step.index + 1))
                if step.has(T):
                    wait(pe, ph, free[0], free[1] * (step.index - T + 1))
                y, i = y_ps[step.pair][:, :], step.pair
                if ph.epi == "norm2":
                    wait(pe, ph, "bias_hi_done", 2)
                    wait(pe, ph, "bias_lo_done", 1)
                    pe.matmul(y, one_row[:, :], bias_lo[:, :], start=True, stop=False)
                    pe.matmul(y, one_row[:, :], bias_hi[:, :], start=False, stop=False)
                for c in range(ph.chunks):
                    hi, lo = ph.hi[:, i, c * P:(c + 1) * P], ph.lo[:, i, c * P:(c + 1) * P]
                    pe.matmul(y, lo, ph.wh[:, c, :], start=c == 0 and ph.epi != "norm2", stop=False)
                    pe.matmul(y, hi, ph.wl[:, c, :], start=False, stop=False)
                    last = pe.matmul(y, hi, ph.wh[:, c, :], start=False,
                                     stop=c == ph.chunks - 1 and ph.agg != "post")
                if ph.agg in ("post", "sep"):
                    last = neighbours(step, y if ph.agg == "post" else agg_ps[i][:, :], ph.agg == "sep")
                last.then_inc(ph.m["mm_done"].sem, 1)
            steps(pe, ph.n, body, 2, 0, peel=ph.peel)

        def splits_early(ph):
            return ph.kind == "dense" and ph.next is not None and ph.next.early

        def old_weights(eng, ph):
            old = ph.before.before if ph.early else ph.before
            if old is not None and old.kind == "dense":
                wait(eng, old, "mm_done", old.n)

        def weights_scalar(act, ph):
            old_weights(act, ph)
            if not ph.turned:
                wait(act, ph, "w_loaded", 16 * (2 if ph.wide else 1))
            for c in range(ph.chunks):
                if ph.turned:
                    wait(act, ph, "w_turned", c + 1)
                src = zt_ps[c % T][:, :] if ph.turned else ph.raw[:, ph.raw_at + c, :]
                nc.scalar.activation(ph.wh[:, c, :], src, ACT.Copy).then_inc(ph.m["w_hi_done"].sem, 1)

        def phase_scalar(act, ph):
            if ph.kind == "dense" and not ph.early:
                weights_scalar(act, ph)
            if ph.kind == "dense" and ph.epi == "norm2":
                wait(act, ph, "rows_loaded", 48)
                nc.scalar.activation(bias_hi[:, :], bias[0:1, :], ACT.Copy).then_inc(ph.m["bias_hi_done"].sem, 1)
                nc.scalar.activation(one_row[:, :], ones[0:1, :], ACT.Copy).then_inc(ph.m["bias_hi_done"].sem, 1)
            if ph.kind == "norm":
                weights_scalar(act, ph.next)
            if ph.kind == "apply":
                wait(act, ph, "bn_dve", 4)
                nc.scalar.activation(normed_out[:, 0, :], bn_sum[:, :], ACT.Ln).then_inc(ph.m["bn_act"].sem, 1)
                wait(act, ph, "bn_act", 1)
                nc.scalar.activation(normed_out[:, 0, :], normed_out[:, 0, :], ACT.Exp, scale=-0.5)\
                    .then_inc(ph.m["bn_act"].sem, 1)

            def body(step):
                near, before, older = step.tile(1), step.tile(-1), step.tile(-2)
                s_ = step.slot
                if ph.kind == "dense" and near.exists:
                    for g, (buf, chunks, ps) in enumerate(ph.parts):
                        wait(act, ph, "turned", ph.groups * near.index + g + 1)
                        if near.has(T):
                            wait(act, ph, "mm_done", near.index - T + 1)
                        at = g * KC * P
                        nc.scalar.activation(ph.hi[:, near.pair, at:at + chunks * P],
                                             ps[near.pair][:, 0:chunks * P], ACT.Copy)\
                            .then_inc(ph.m["hi_done"].sem, 1)
                ahead = step.tile(ph.parts_at)
                if ph.split and ahead.exists:
                    g_hi, _, ring_g = g_parts(ph, ahead)
                    slot_wait(act, ph, "gathered0_", ahead)
                    if ahead.has(ring_g):
                        wait(act, ph, "agg_done" if ph.mixed else "mm_done", ahead.index - ring_g + 1)
                    nc.scalar.activation(g_hi, gathered[:, ahead.pair, :], ACT.Copy)\
                        .then_inc(ph.m["g_hi_done"].sem, 1)
                if ph.kind == "dense" and ph.epi == "mish" and before.exists:
                    m, e, t = ph.m["mish_act"], e_buf[:, before.slot, :], before.index
                    wait(act, ph, "clipped", t + 1)
                    nc.scalar.activation(e, e, ACT.Exp).then_inc(m.sem, 1)
                    act.wait_ge(m.sem, m.at(4 * t + 1))
                    nc.scalar.activation(e, e, ACT.Square, bias=1.0).then_inc(m.sem, 1)
                    act.wait_ge(m.sem, m.at(4 * t + 2))
                    nc.scalar.activation(e, e, ACT.Ln, bias=half[:, 0:1], scale=0.5).then_inc(m.sem, 1)
                    act.wait_ge(m.sem, m.at(4 * t + 3))
                    nc.scalar.activation(e, e, ACT.Exp, scale=-1.0).then_inc(m.sem, 1)
                if ph.kind == "dense" and step.exists:
                    if ph.epi == "copy":
                        wait(act, ph, "mm_done", step.index + 1)
                        if step.has(U):
                            slot_wait(act, ph, "stored", step, U)
                        nc.scalar.activation(res[:, s_, :], y_ps[step.pair][:, :], ACT.Copy)\
                            .then_inc(ph.m["res_act"].sem, 1)
                if ph.kind == "dense" and ph.epi == "bn" and before.exists:
                    d = dinv[:, bass.ds(before.index, 1)]
                    wait(act, ph, "mm_done", before.index + 1)
                    hold(act, before)
                    nc.scalar.activation(kept[:, bass.ds(before.index, 1), :].rearrange("p o d -> p (o d)"),
                                         y_ps[before.pair][:, :], ACT.Identity, scale=d)\
                        .then_inc(ph.m["kept_done"].sem, 1)
                    if before.has(1):
                        wait(act, ph, "sq_done", before.index + 1)
                    hold(act, before)
                    nc.scalar.activation(square[:, :], y_ps[before.pair][:, :], ACT.Square, scale=d)\
                        .then_inc(ph.m["square_done"].sem, 1)
                if ph.kind == "dense" and ph.epi == "gcn" and before.exists:
                    wait(act, ph, "v_done", before.index + 1)
                    if before.has(U):
                        slot_wait(act, ph, "stored", before, U)
                    hold(act, before)
                    nc.scalar.activation(res[:, before.slot, :], v_buf[:, before.slot, :], ACT.Relu,
                                         scale=dinv[:, bass.ds(before.index, 1)]).then_inc(ph.m["res_act"].sem, 1)
                if ph.kind == "dense" and ph.epi == "norm2" and older.exists:
                    wait(act, ph, "ln_ready0", 2 * (older.index + 1))
                    sc, v = ln_sc[:, 0, older.slot, :], v_buf[:, older.slot, :]
                    nc.scalar.activation(v, v, ACT.Identity, scale=sc[:, 2:3], bias=sc[:, 3:4])\
                        .then_inc(ph.m["normed"].sem, 1)

                def normed_relu(of, source, target):
                    wait(act, ph, "ln_ready1", (3 if ln_scaled(ph, 1) else 2) * (of.index + 1))
                    if of.has(U):
                        slot_wait(act, ph, "stored", of, U)
                    hold(act, of)
                    sc = ln_sc[:, 1, of.slot, :]
                    nc.scalar.activation(target, source, ACT.Relu, scale=sc[:, 2:3], bias=sc[:, 3:4])\
                        .then_inc(ph.m["res_act"].sem, 1)

                ended = step.tile(-lag(ph, "res"))
                if ph.kind == "dense" and ph.epi in ("norm2", "gcn_last") and ended.exists:
                    normed_relu(ended, x_out[:, ended.slot, :], res[:, ended.slot, :])
                if ph.kind == "norm" and ended.exists:
                    normed_relu(ended, side_a[:, ended.slot, :], res[:, ended.slot, :])
                if ph.kind == "apply":
                    if not ph.last and step.exists:
                        k_ = kept[:, bass.ds(step.index, 1), :].rearrange("p o d -> p (o d)")
                        added(act, ph, step)
                        hold(act, step)
                        nc.scalar.activation(k_, k_, ACT.Relu, scale=dinv[:, bass.ds(step.index, 1)])\
                            .then_inc(ph.m["res_act"].sem, 1)
                    if ph.last and ended.exists:
                        k_ = kept[:, bass.ds(ended.index, 1), :].rearrange("p o d -> p (o d)")
                        normed_relu(ended, k_, normed_out[:, ended.slot, :])
            steps(act, ph.n, body, 3, 6, (lambda: weights_scalar(act, ph.next)) if splits_early(ph) else None,
                  ph.peel)

        def weights_vector(dve, ph):
            old_weights(dve, ph)
            for c in range(ph.chunks):
                wait(dve, ph, "w_hi_done", c + 1)
                src = zt_ps[c % T][:, :] if ph.turned else ph.raw[:, ph.raw_at + c, :]
                dve.tensor_tensor(ph.wl[:, c, :], src, ph.wh[:, c, :].bitcast(F32), ALU.subtract)\
                    .then_inc(ph.m["w_lo_done"].sem, 1)

        def phase_vector(dve, ph, is_crowded):
            def stats(k, of, source):
                if of.has(U):
                    wait(dve, ph, f"gauged{k}", of.index - U + 1)
                hold(dve, of)
                dve.bn_stats(ln_st[:, k, of.slot, :], source).then_inc(ph.m[f"stats{k}"].sem, 1)

            def gauge(k, of):
                wait(dve, ph, f"stats{k}", of.index + 1)
                if of.has(U):
                    wait(dve, ph, f"ln_ready{k}", (3 if ln_scaled(ph, k) else 2) * (of.index - U + 1))
                hold(dve, of)
                dve.bn_aggr(ln_mv[:, k, of.slot, :], ln_st[:, k, of.slot, :]).then_inc(ph.m[f"gauged{k}"].sem, 1)

            def add_eps(k, of):
                var = ln_mv[:, k, of.slot, 1:2]
                wait(dve, ph, f"gauged{k}", of.index + 1)
                hold(dve, of)
                dve.tensor_scalar(var, var, EPS, None, ALU.add).then_inc(ph.m[f"moments{k}"].sem, 1)

            if ph.kind == "dense" and not ph.early:
                weights_vector(dve, ph)
            if ph.kind == "dense" and ph.epi == "norm2":
                wait(dve, ph, "bias_hi_done", 1)
                dve.tensor_tensor(bias_lo[:, :], bias[0:1, :], bias_hi[:, :].bitcast(F32), ALU.subtract)\
                    .then_inc(ph.m["bias_lo_done"].sem, 1)
            if ph.kind == "dense" and ph.epi == "bn":
                dve.memset(bn_sq[:, :], 0.0).then_inc(ph.m["sq_done"].sem, 1)
            if ph.kind == "norm":
                weights_vector(dve, ph.next)
            if ph.kind == "apply":
                b_row, g_row, beta_r = gathered[:, 0, :], gathered[:, 1, :], square[:, :]
                mean, t1 = tile_in[:, 0, :], tile_in[:, 1, :]
                own = ph.m["bn_dve"]
                wait(dve, ph, "totals_done", 1)
                dve.tensor_scalar(mean, y_ps[0][:, :], 1.0 / n_nodes, None, ALU.mult).then_inc(own.sem, 1)
                wait(dve, ph, "bn_dve", 1)
                dve.tensor_tensor(t1, mean, mean, ALU.mult).then_inc(own.sem, 1)
                wait(dve, ph, "totals_done", 2)
                wait(dve, ph, "bn_dve", 2)
                dve.scalar_tensor_tensor(out=bn_sum[:, :], in0=y_ps[1][:, :], scalar=1.0 / n_nodes, in1=t1,
                                         op0=ALU.mult, op1=ALU.subtract).then_inc(own.sem, 1)
                wait(dve, ph, "bn_dve", 3)
                dve.tensor_scalar(bn_sum[:, :], bn_sum[:, :], 0.0, EPS, ALU.max, ALU.add).then_inc(own.sem, 1)
                r, inv = normed_out[:, 0, :], ph.m["bn_dve"].sem
                wait(dve, ph, "rows_loaded", 48)
                dve.tensor_tensor(mean, mean, b_row, ALU.add).then_inc(inv, 1)
                wait(dve, ph, "bn_dve", 5)
                dve.tensor_tensor(mean, b_row, mean, ALU.subtract).then_inc(inv, 1)
                wait(dve, ph, "bn_act", 2)
                dve.tensor_tensor(t1, r, r, ALU.mult).then_inc(inv, 1)
                wait(dve, ph, "bn_dve", 7)
                dve.scalar_tensor_tensor(out=t1, in0=t1, scalar=-0.5, in1=bn_sum[:, :], op0=ALU.mult,
                                         op1=ALU.mult).then_inc(inv, 1)
                wait(dve, ph, "bn_dve", 8)
                dve.scalar_tensor_tensor(out=r, in0=t1, scalar=1.5, in1=r, op0=ALU.add,
                                         op1=ALU.mult).then_inc(inv, 1)
                wait(dve, ph, "bn_dve", 9)
                dve.tensor_tensor(bn_sum[:, :], r, g_row, ALU.mult).then_inc(inv, 1)
                wait(dve, ph, "bn_dve", 10)
                dve.tensor_tensor(mean, mean, bn_sum[:, :], ALU.mult).then_inc(inv, 1)
                wait(dve, ph, "bn_dve", 11)
                dve.tensor_tensor(bn_sq[:, :], mean, beta_r, ALU.add).then_inc(inv, 1)

            if ph.kind == "dense" and ph.agg:
                spill_vector(dve, ph, is_crowded)

            def choose(step):
                if step.has(T):
                    wait(dve, ph, "agg_done" if ph.mixed else "mm_done", step.index - T + 1)
                dve.tensor_scalar(select[:, step.pair, :], iota_row[:, :], slot_node[:, bass.ds(step.index, 1)],
                                  None, ALU.is_equal).then_inc(ph.m["selected"].sem, 1)

            def body(step):
                near, before, older, s_ = step.tile(1), step.tile(-1), step.tile(-2), step.slot
                if ph.kind == "dense" and near.exists:
                    for g, (buf, chunks, ps) in enumerate(ph.parts):
                        wait(dve, ph, "hi_done", ph.groups * near.index + g + 1)
                        if near.has(T):
                            wait(dve, ph, "mm_done", near.index - T + 1)
                        at = g * KC * P
                        dve.tensor_tensor(ph.lo[:, near.pair, at:at + chunks * P], ps[near.pair][:, 0:chunks * P],
                                          ph.hi[:, near.pair, at:at + chunks * P].bitcast(F32), ALU.subtract)\
                            .then_inc(ph.m["lo_done"].sem, 1)
                third, fourth = step.tile(-3), step.tile(-4)
                if ph.kind == "dense" and ph.epi == "norm2" and third.exists:
                    v = v_buf[:, third.slot, :]
                    wait(dve, ph, "normed", third.index + 1)
                    dve.tensor_tensor(v, v, gamma_row[:, :], ALU.mult).then_inc(ph.m["scaled"].sem, 1)
                far, ahead = step.tile(2), step.tile(ph.parts_at)
                if ph.mixed and far.exists:
                    own = tile_in[:, far.pair, :]
                    slot_wait(dve, ph, "loaded", far)
                    wait(dve, ph, "agg_done", far.index + 1)
                    dve.tensor_tensor(own, own, agg_ps[far.pair][:, :], ALU.add)\
                        .then_inc(ph.m["mixed_done"].sem, 1)
                if ph.split and ahead.exists:
                    g_hi, g_lo, ring_g = g_parts(ph, ahead)
                    wait(dve, ph, "g_hi_done", ahead.index + 1)
                    if ahead.has(ring_g):
                        wait(dve, ph, "agg_done" if ph.mixed else "mm_done", ahead.index - ring_g + 1)
                    dve.tensor_tensor(g_lo, gathered[:, ahead.pair, :], g_hi.bitcast(F32), ALU.subtract)\
                        .then_inc(ph.m["g_lo_done"].sem, 1)
                if ph.kind == "dense" and ph.agg:
                    ahead = step.tile(ph.parts_at if ph.split else 2)
                    if ahead.exists:
                        choose(ahead)
                if ph.kind == "dense" and ph.epi == "mish" and older.exists:
                    o_ = older.slot
                    wait(dve, ph, "mish_act", 4 * older.index + 4)
                    if older.has(U):
                        slot_wait(dve, ph, "stored", older, U)
                    dve.scalar_tensor_tensor(out=res[:, o_, :], in0=e_buf[:, o_, :], scalar=1.0,
                                             in1=v_buf[:, o_, :], op0=ALU.subtract, op1=ALU.mult,
                                             reverse0=True).then_inc(ph.m["res_dve"].sem, 1)
                if ph.kind == "dense" and ph.epi == "bn" and before.exists:
                    wait(dve, ph, "square_done", before.index + 1)
                    wait(dve, ph, "sq_done", before.index + 1)
                    dve.tensor_tensor(bn_sq[:, :], bn_sq[:, :], square[:, :], ALU.add)\
                        .then_inc(ph.m["sq_done"].sem, 1)
                if ph.kind == "dense" and step.exists and ph.epi != "bn":
                    y = y_ps[step.pair][:, :]
                    if step.fixed and step.index == 0 and ph.epi in ("mish", "gcn", "sage", "norm2"):
                        wait(dve, ph, "rows_loaded", 48 if ph.epi == "norm2" else 16)
                    if ph.epi != "copy":
                        wait(dve, ph, "mm_done", step.index + 1)
                    if ph.epi == "mish":
                        if step.has(U):
                            wait(dve, ph, "res_dve", step.index - U + 1)
                        dve.tensor_tensor(v_buf[:, s_, :], y, bias[:, :], ALU.add)\
                            .then_inc(ph.m["v_done"].sem, 1)
                        wait(dve, ph, "v_done", step.index + 1)
                        dve.tensor_scalar(e_buf[:, s_, :], v_buf[:, s_, :], EXP_MAX, -80.0, ALU.min, ALU.max)\
                            .then_inc(ph.m["clipped"].sem, 1)
                    if ph.epi == "gcn":
                        if step.has(U):
                            wait(dve, ph, "res_act", step.index - U + 1)
                        dve.scalar_tensor_tensor(out=v_buf[:, s_, :], in0=y,
                                                 scalar=dinv[:, bass.ds(step.index, 1)], in1=bias[:, :],
                                                 op0=ALU.mult, op1=ALU.add).then_inc(ph.m["v_done"].sem, 1)
                    if ph.epi == "gcn_last":
                        wait(dve, ph, "side_done", step.index + 1)
                        if step.has(U):
                            wait(dve, ph, "res_act", step.index - U + 1)
                            slot_wait(dve, ph, "x_stored", step, U)
                        dve.scalar_tensor_tensor(out=x_out[:, s_, :], in0=y,
                                                 scalar=dinv[:, bass.ds(step.index, 1)], in1=side_a[:, s_, :],
                                                 op0=ALU.mult, op1=ALU.add).then_inc(ph.m["x_done"].sem, 1)
                    if ph.epi == "norm2":
                        slot_wait(dve, ph, "side_a", step)
                        if step.has(U):
                            wait(dve, ph, "x_done", step.index - U + 1)
                        dve.tensor_tensor(v_buf[:, s_, :], y, side_a[:, s_, :], ALU.add)\
                            .then_inc(ph.m["v_done"].sem, 1)
                    if ph.epi == "sage":
                        m = ph.m["v_done"]
                        if step.has(U):
                            wait(dve, ph, "res_dve", step.index - U + 1)
                        dve.scalar_tensor_tensor(out=v_buf[:, s_, :], in0=agg_ps[step.pair][:, :],
                                                 scalar=rdeg[:, bass.ds(step.index, 1)], in1=bias[:, :],
                                                 op0=ALU.mult, op1=ALU.add).then_inc(m.sem, 1)
                        dve.wait_ge(m.sem, m.at(2 * step.index + 1))
                        dve.tensor_tensor(v_buf[:, s_, :], v_buf[:, s_, :], y, ALU.add)\
                            .then_inc(m.sem, 1)
                        dve.wait_ge(m.sem, m.at(2 * step.index + 2))
                        slot_wait(dve, ph, "side_a", step)
                        if step.has(U):
                            slot_wait(dve, ph, "stored", step, U)
                        dve.scalar_tensor_tensor(out=res[:, s_, :], in0=v_buf[:, s_, :], scalar=0.0,
                                                 in1=side_a[:, s_, :], op0=ALU.max, op1=ALU.add)\
                            .then_inc(ph.m["res_dve"].sem, 1)
                if ph.kind == "dense" and ph.epi == "gcn_last":
                    if before.exists:
                        gauge(1, before)
                    if step.exists:
                        wait(dve, ph, "x_done", step.index + 1)
                        stats(1, step, x_out[:, s_, :])
                    if before.exists:
                        add_eps(1, before)
                if ph.kind == "dense" and ph.epi == "norm2":
                    if third.exists:
                        wait(dve, ph, "scaled", third.index + 1)
                        wait(dve, ph, "side_done", third.index + 1)
                        if third.has(U):
                            wait(dve, ph, "res_act", third.index - U + 1)
                            slot_wait(dve, ph, "x_stored", third, U)
                        dve.tensor_tensor(x_out[:, third.slot, :], v_buf[:, third.slot, :],
                                          side_b[:, third.slot, :], ALU.add).then_inc(ph.m["x_done"].sem, 1)
                    if before.exists:
                        gauge(0, before)
                    if fourth.exists:
                        gauge(1, fourth)
                    if step.exists:
                        wait(dve, ph, "v_done", step.index + 1)
                        stats(0, step, v_buf[:, s_, :])
                    if before.exists:
                        add_eps(0, before)
                    if fourth.exists:
                        add_eps(1, fourth)
                    if third.exists:
                        wait(dve, ph, "x_done", third.index + 1)
                        stats(1, third, x_out[:, third.slot, :])
                if ph.kind == "norm" and step.exists:
                    if not step.fixed or part_rows(step.index):
                        slot_wait(dve, ph, "x_loaded", step)
                    stats(1, step, side_a[:, s_, :])
                    prepare(dve, step)
                    gauge(1, step)
                    add_eps(1, step)
                if ph.kind == "apply":
                    if ph.last and before.exists:
                        x_new = kept[:, bass.ds(before.index, 1), :].rearrange("p o d -> p (o d)")
                        added(dve, ph, before)
                        slot_wait(dve, ph, "side_a", before)
                        dve.scalar_tensor_tensor(out=x_new, in0=x_new, scalar=0.0, in1=x_slots[before.slot],
                                                 op0=ALU.max, op1=ALU.add).then_inc(ph.m["x_done"].sem, 1)
                    if ph.last and older.exists:
                        gauge(1, older)
                    if near.exists:
                        if near.fixed and near.index == 0:
                            wait(dve, ph, "bn_dve", BN_STEPS)
                        k_ = kept[:, bass.ds(near.index, 1), :].rearrange("p o d -> p (o d)")
                        dve.tensor_tensor(k_, k_, bn_sum[:, :], ALU.mult).then_inc(ph.m["mul_done"].sem, 1)
                        if near.lane == U - 1:
                            wait(dve, ph, "mul_done", near.index + 1)
                            dve.tensor_tensor(k_, k_, bn_sq[:, :], ALU.add).then_inc(ph.m["add_dve"].sem, 1)
                    if ph.last and older.exists:
                        add_eps(1, older)
                    if ph.last and before.exists:
                        wait(dve, ph, "x_done", before.index + 1)
                        stats(1, before, x_new)
            steps(dve, ph.n, body, 3, 5, (lambda: weights_vector(dve, ph.next)) if splits_early(ph) else None,
                  ph.peel)

        held = {id(nc.gpsimd): sem("held_pool"), id(nc.scalar): sem("held_act"), id(nc.vector): sem("held_dve")}

        block = ctx.enter_context(nc.Block())

        @block.sync
        def _(sp):
            setup_sync(sp)
            for ph in phases:
                phase_sync(sp, ph)
                if ph.name == "edge_3":
                    table_sync(sp)
            all_stored(sp, phases[-1])

        @block.gpsimd
        def _(pool):
            setup_pool(pool)
            is_crowded = None
            for ph in phases:
                if ph.name == "edge_3":
                    dinv_pool(pool)
                    scatter_pool(pool)
                if ph.kind != "norm" and is_crowded is None and ph.agg:
                    is_crowded = load_crowded(pool)
                phase_pool(pool, ph, is_crowded)

        @block.scalar
        def _(act):
            act.wait_ge(s_const, 14)
            nc.scalar.preload_act_table_set("natural_log_exp_and_others")
            for ph in phases:
                phase_scalar(act, ph)

        @block.vector
        def _(dve):
            setup_vector(dve)
            is_crowded = None
            for ph in phases:
                phase_vector(dve, ph, is_crowded)
                if ph.kind == "norm":
                    ranks_vector(dve)
                if ph.name == "edge_3":
                    table_vector(dve)
                    is_crowded = load_crowded(dve)

        @block.tensor
        def _(pe):
            setup_tensor(pe)
            is_crowded = None
            for ph in phases:
                if ph.kind != "norm" and is_crowded is None and ph.agg:
                    is_crowded = load_crowded(pe)
                phase_tensor(pe, ph, is_crowded)


def kernel(**inputs):
    import numpy as _np
    import concourse.bacc as _bacc
    from concourse import mybir as _mybir
    from concourse.bass_utils import run_bass_kernel_spmd as _run

    nc = _bacc.Bacc("TRN2", target_bir_lowering=False, num_devices=1)
    arrays, handles = {}, {}
    for name, value in inputs.items():
        v = _np.ascontiguousarray(value)
        arrays[f"in_{name}"] = v
        handles[name] = nc.dram_tensor(f"in_{name}", v.shape, _mybir.dt.from_np(v.dtype), kind="ExternalInput").ap()
    out = nc.dram_tensor("out_x", inputs["x"].shape, _mybir.dt.float32, kind="ExternalOutput").ap()
    build(nc, handles, out)
    r = _run(nc, [arrays], core_ids=[0])
    return r.results[0]["out_x"]
```
